# Optimizing a Trainium2 kernel written in Bass

```python
import numpy as np
import jax
import jax.numpy as jnp

def _softmax(x, axis=-1):
    return jax.nn.softmax(x, axis=axis)

def _gelu(x):
    return jax.nn.gelu(x, approximate=True)

def _silu(x):
    return jax.nn.silu(x)

def _sigmoid(x):
    return jax.nn.sigmoid(x)

def _layernorm(x, axis=-1, eps=1e-05):
    m = jnp.mean(x, axis=axis, keepdims=True)
    v = jnp.var(x, axis=axis, keepdims=True)
    return (x - m) / jnp.sqrt(v + eps)

def _scatter_add(tgt, idx, src, axis=0):
    return tgt.at[idx].add(src)

def _segment_sum(src, seg, n):
    return jax.ops.segment_sum(src, seg, n)
kernel_name = 'mk_sandwich_d2_jaxref_r4_233af0'

def setup_inputs(seed: int=0):
    np.random.seed(seed)
    _w = jnp.asarray

    def _L0_attn_setup():
        import jax, jax.numpy as jnp
        import numpy as np
        from jax import lax
        D = 256
        ORDER = 2
        FILT = 64
        EMB = 3
        INNER = D * (ORDER + 1)
        DF = D * (ORDER - 1)
        L_MAX = 512

        def _pos_emb(L):
            t = jnp.linspace(0.0, 1.0, L)[:, None]
            tr = jnp.linspace(0.0, L - 1.0, L)[:, None]
            w = 2.0 * np.pi * tr / L
            f = jnp.array([0.0001], jnp.float32)[None, :]
            z = jnp.concatenate([t, jnp.cos(f * w), -jnp.sin(f * w)], axis=-1)
            return (z, t)

        def _decay(t):
            max_d = np.log(0.01) / 0.3
            min_d = np.log(0.01) / 1.5
            deltas = jnp.linspace(min_d, max_d, DF)[None, :]
            return jnp.exp(-t * jnp.abs(deltas))
        key = jax.random.key(seed)
        ks = jax.random.split(key, 16)
        s = 0.02
        return {'u': jax.random.normal(ks[0], (4, L_MAX, D), jnp.float32), 'in_w': jax.random.normal(ks[1], (D, INNER), jnp.float32) * s, 'in_b': jnp.zeros((INNER,), jnp.float32), 'short_w': jax.random.normal(ks[2], (INNER, 3), jnp.float32) * 0.3, 'short_b': jnp.zeros((INNER,), jnp.float32), 'mlp_w1': jax.random.normal(ks[3], (EMB, FILT), jnp.float32) * 0.3, 'mlp_b1': jnp.zeros((FILT,), jnp.float32), 'mlp_w2': jax.random.normal(ks[4], (FILT, FILT), jnp.float32) * 0.1, 'mlp_b2': jnp.zeros((FILT,), jnp.float32), 'mlp_w3': jax.random.normal(ks[5], (FILT, FILT), jnp.float32) * 0.1, 'mlp_b3': jnp.zeros((FILT,), jnp.float32), 'mlp_wo': jax.random.normal(ks[6], (FILT, DF), jnp.float32) * 0.1, 'freq': jnp.ones((1, FILT), jnp.float32), 'filt_bias': jax.random.normal(ks[7], (DF,), jnp.float32), 'out_w': jax.random.normal(ks[8], (D, D), jnp.float32) * s, 'out_b': jnp.zeros((D,), jnp.float32)}
    _L0_attn_in = _L0_attn_setup()

    def _L0_ffn_setup():
        import jax, jax.numpy as jnp
        import numpy as np
        DIM = 256

        def _reference_tuple_inner(x, W_r, W_k, W_v, mu_r, mu_k):
            B, T, C = x.shape
            x_prev = jnp.concatenate([jnp.zeros((B, 1, C), x.dtype), x[:, :-1, :]], axis=1)
            xr = mu_r * x + (1.0 - mu_r) * x_prev
            xk = mu_k * x + (1.0 - mu_k) * x_prev
            r = jax.nn.sigmoid(jnp.einsum('btc,dc->btd', xr, W_r))
            k = jnp.einsum('btc,dc->btd', xk, W_k)
            k_act = jnp.square(jax.nn.relu(k))
            out = r * jnp.einsum('btc,dc->btd', k_act, W_v)
            new_state = x[:, -1, :]
            return (out, new_state)
        key = jax.random.key(seed)
        ks = jax.random.split(key, 6)
        B, T, C = (8, 512, DIM)
        x = jax.random.normal(ks[0], (B, T, C), dtype=jnp.float32)
        s = 1.0 / np.sqrt(C)
        W_r = jax.random.uniform(ks[1], (C, C), jnp.float32, -s, s)
        W_k = jax.random.uniform(ks[2], (C, C), jnp.float32, -s, s)
        W_v = jax.random.uniform(ks[3], (C, C), jnp.float32, -s, s)
        mu_r = jax.random.uniform(ks[4], (C,), jnp.float32)
        mu_k = jax.random.uniform(ks[5], (C,), jnp.float32)
        return {'x': x, 'W_r': W_r, 'W_k': W_k, 'W_v': W_v, 'mu_r': mu_r, 'mu_k': mu_k}
    _L0_ffn_in = _L0_ffn_setup()

    def _L1_attn_setup():
        import jax, jax.numpy as jnp
        import numpy as np
        DIM = 256
        HEADS = 16
        HD = DIM // HEADS
        B, S = (4, 1024)
        LEVELS = 3
        HID = 4 * DIM
        CHUNK = 128
        EPS = 1e-05

        def layernorm(x, g, b):
            m = jnp.mean(x, axis=-1, keepdims=True)
            v = jnp.var(x, axis=-1, keepdims=True)
            return (x - m) * jax.lax.rsqrt(v + EPS) * g + b

        def _linear_attn_with_memory(h, wq, wk, wv, wo):
            b, s, d = h.shape

            def heads(w):
                return (h @ w).reshape(b, s, HEADS, HD).transpose(0, 2, 1, 3)
            q, k, v = (heads(wq), heads(wk), heads(wv))
            nc = s // CHUNK

            def to_chunks(a):
                return a.reshape(b, HEADS, nc, CHUNK, HD).transpose(2, 0, 1, 3, 4)
            mask = jnp.tril(jnp.ones((CHUNK, CHUNK), h.dtype))

            def step(M, qkv):
                qc, kc, vc = qkv
                inter = jnp.einsum('bhvk,bhck->bhcv', M, qc)
                scores = jnp.einsum('bhcd,bhed->bhce', qc, kc) * mask
                intra = jnp.einsum('bhce,bhev->bhcv', scores, vc)
                M_new = M + jnp.einsum('bhcv,bhck->bhvk', vc, kc)
                return (M_new, inter + intra)
            M0 = jnp.zeros((b, HEADS, HD, HD), h.dtype)
            _, ys = jax.lax.scan(step, M0, (to_chunks(q), to_chunks(k), to_chunks(v)))
            y = ys.transpose(1, 2, 0, 3, 4).reshape(b, HEADS, s, HD)
            y = y.transpose(0, 2, 1, 3).reshape(b, s, d)
            return y @ wo
        key = jax.random.key(seed)
        ks = jax.random.split(key, 10)
        std = 0.02
        return {'x': jax.random.normal(ks[0], (B, S, DIM), jnp.float32), 'ln1_g': jnp.ones((DIM,), jnp.float32), 'ln1_b': jnp.zeros((DIM,), jnp.float32), 'wq': jax.random.normal(ks[1], (DIM, DIM), jnp.float32) * std, 'wk': jax.random.normal(ks[2], (DIM, DIM), jnp.float32) * std, 'wv': jax.random.normal(ks[3], (DIM, DIM), jnp.float32) * std, 'wo': jax.random.normal(ks[4], (DIM, DIM), jnp.float32) * std, 'ln2_g': jnp.ones((DIM,), jnp.float32), 'ln2_b': jnp.zeros((DIM,), jnp.float32), 'cms_w1': jax.random.normal(ks[5], (LEVELS, DIM, HID), jnp.float32) * std, 'cms_b1': jnp.zeros((LEVELS, HID), jnp.float32), 'cms_w2': jax.random.normal(ks[6], (LEVELS, HID, DIM), jnp.float32) * std, 'cms_b2': jnp.zeros((LEVELS, DIM), jnp.float32)}
    _L1_attn_in = _L1_attn_setup()

    def _L1_ffn_setup():
        import jax, jax.numpy as jnp
        import numpy as np
        B, S, H, F, E = (8, 512, 256, 1024, 8)
        INIT_LAMBDA = 0.2
        key = jax.random.key(seed)
        ks = jax.random.split(key, 12)
        std = 0.02
        return {'hidden_states': jax.random.normal(ks[0], (B, S, H), jnp.float32), 'gate_w1': jax.random.normal(ks[1], (H, H), jnp.float32) * 0.01, 'gate_b1': jnp.zeros((H,), jnp.float32), 'gate_w2': jax.random.normal(ks[2], (E, H), jnp.float32) * 0.01, 'gate_b2': jnp.full((E,), INIT_LAMBDA, jnp.float32), 'W1': jax.random.normal(ks[3], (F, H), jnp.float32) * std, 'b1': jax.random.normal(ks[4], (F,), jnp.float32) * std, 'W2': jax.random.normal(ks[5], (H, F), jnp.float32) * std, 'b2': jax.random.normal(ks[6], (H,), jnp.float32) * std, 'TW1': jax.random.normal(ks[7], (E, F, H), jnp.float32) * std, 'Tb1': jax.random.normal(ks[8], (E, F), jnp.float32) * std, 'TW2': jax.random.normal(ks[9], (E, H, F), jnp.float32) * std, 'Tb2': jax.random.normal(ks[10], (E, H), jnp.float32) * std}
    _L1_ffn_in = _L1_ffn_setup()
    _d = {'L0_attn_u': _L0_attn_in['u'], 'L0_attn_in_w': _L0_attn_in['in_w'], 'L0_attn_in_b': _L0_attn_in['in_b'], 'L0_attn_short_w': _L0_attn_in['short_w'], 'L0_attn_short_b': _L0_attn_in['short_b'], 'L0_attn_mlp_w1': _L0_attn_in['mlp_w1'], 'L0_attn_mlp_b1': _L0_attn_in['mlp_b1'], 'L0_attn_mlp_w2': _L0_attn_in['mlp_w2'], 'L0_attn_mlp_b2': _L0_attn_in['mlp_b2'], 'L0_attn_mlp_w3': _L0_attn_in['mlp_w3'], 'L0_attn_mlp_b3': _L0_attn_in['mlp_b3'], 'L0_attn_mlp_wo': _L0_attn_in['mlp_wo'], 'L0_attn_freq': _L0_attn_in['freq'], 'L0_attn_filt_bias': _L0_attn_in['filt_bias'], 'L0_attn_out_w': _L0_attn_in['out_w'], 'L0_attn_out_b': _L0_attn_in['out_b'], 'L0_ffn_W_r': _L0_ffn_in['W_r'], 'L0_ffn_W_k': _L0_ffn_in['W_k'], 'L0_ffn_W_v': _L0_ffn_in['W_v'], 'L0_ffn_mu_r': _L0_ffn_in['mu_r'], 'L0_ffn_mu_k': _L0_ffn_in['mu_k'], 'L1_attn_ln1_g': _L1_attn_in['ln1_g'], 'L1_attn_ln1_b': _L1_attn_in['ln1_b'], 'L1_attn_wq': _L1_attn_in['wq'], 'L1_attn_wk': _L1_attn_in['wk'], 'L1_attn_wv': _L1_attn_in['wv'], 'L1_attn_wo': _L1_attn_in['wo'], 'L1_attn_ln2_g': _L1_attn_in['ln2_g'], 'L1_attn_ln2_b': _L1_attn_in['ln2_b'], 'L1_attn_cms_w1': _L1_attn_in['cms_w1'], 'L1_attn_cms_b1': _L1_attn_in['cms_b1'], 'L1_attn_cms_w2': _L1_attn_in['cms_w2'], 'L1_attn_cms_b2': _L1_attn_in['cms_b2'], 'L1_ffn_gate_w1': _L1_ffn_in['gate_w1'], 'L1_ffn_gate_b1': _L1_ffn_in['gate_b1'], 'L1_ffn_gate_w2': _L1_ffn_in['gate_w2'], 'L1_ffn_gate_b2': _L1_ffn_in['gate_b2'], 'L1_ffn_W1': _L1_ffn_in['W1'], 'L1_ffn_b1': _L1_ffn_in['b1'], 'L1_ffn_W2': _L1_ffn_in['W2'], 'L1_ffn_b2': _L1_ffn_in['b2'], 'L1_ffn_TW1': _L1_ffn_in['TW1'], 'L1_ffn_Tb1': _L1_ffn_in['Tb1'], 'L1_ffn_TW2': _L1_ffn_in['TW2'], 'L1_ffn_Tb2': _L1_ffn_in['Tb2']}
    _x0 = _d['L0_attn_u']
    _d['L0_attn_u'] = jax.random.normal(jax.random.fold_in(jax.random.key(seed), 1), (8, 1024, 256), dtype=_x0.dtype)
    del _x0
    return _d

def reference(L0_attn_u, L0_attn_in_w, L0_attn_in_b, L0_attn_short_w, L0_attn_short_b, L0_attn_mlp_w1, L0_attn_mlp_b1, L0_attn_mlp_w2, L0_attn_mlp_b2, L0_attn_mlp_w3, L0_attn_mlp_b3, L0_attn_mlp_wo, L0_attn_freq, L0_attn_filt_bias, L0_attn_out_w, L0_attn_out_b, L0_ffn_W_r, L0_ffn_W_k, L0_ffn_W_v, L0_ffn_mu_r, L0_ffn_mu_k, L1_attn_ln1_g, L1_attn_ln1_b, L1_attn_wq, L1_attn_wk, L1_attn_wv, L1_attn_wo, L1_attn_ln2_g, L1_attn_ln2_b, L1_attn_cms_w1, L1_attn_cms_b1, L1_attn_cms_w2, L1_attn_cms_b2, L1_ffn_gate_w1, L1_ffn_gate_b1, L1_ffn_gate_w2, L1_ffn_gate_b2, L1_ffn_W1, L1_ffn_b1, L1_ffn_W2, L1_ffn_b2, L1_ffn_TW1, L1_ffn_Tb1, L1_ffn_TW2, L1_ffn_Tb2):

    def _L0_attn_ref(u, in_w, in_b, short_w, short_b, mlp_w1, mlp_b1, mlp_w2, mlp_b2, mlp_w3, mlp_b3, mlp_wo, freq, filt_bias, out_w, out_b):
        import jax, jax.numpy as jnp
        import numpy as np
        from jax import lax
        D = 256
        ORDER = 2
        FILT = 64
        EMB = 3
        INNER = D * (ORDER + 1)
        DF = D * (ORDER - 1)
        L_MAX = 512

        def _pos_emb(L):
            t = jnp.linspace(0.0, 1.0, L)[:, None]
            tr = jnp.linspace(0.0, L - 1.0, L)[:, None]
            w = 2.0 * np.pi * tr / L
            f = jnp.array([0.0001], jnp.float32)[None, :]
            z = jnp.concatenate([t, jnp.cos(f * w), -jnp.sin(f * w)], axis=-1)
            return (z, t)

        def _decay(t):
            max_d = np.log(0.01) / 0.3
            min_d = np.log(0.01) / 1.5
            deltas = jnp.linspace(min_d, max_d, DF)[None, :]
            return jnp.exp(-t * jnp.abs(deltas))
        B, L, _ = u.shape
        up = jnp.einsum('bld,de->ble', u, in_w) + in_b
        up = up.transpose(0, 2, 1)
        uc = lax.conv_general_dilated(up, short_w[:, None, :], (1,), [(2, 2)], feature_group_count=INNER, dimension_numbers=('NCH', 'OIH', 'NCH'))
        uc = uc[..., :L] + short_b[None, :, None]
        x0, x1, v = (uc[:, :D], uc[:, D:2 * D], uc[:, 2 * D:])
        z, t = _pos_emb(L)
        h = jnp.sin(freq * (z @ mlp_w1 + mlp_b1))
        h = jnp.sin(freq * (h @ mlp_w2 + mlp_b2))
        h = jnp.sin(freq * (h @ mlp_w3 + mlp_b3))
        h = h @ mlp_wo
        k = (h * _decay(t)).T
        vx = v * x1
        n = 2 * L
        y = jnp.fft.irfft(jnp.fft.rfft(vx, n=n) * jnp.fft.rfft(k, n=n), n=n)[..., :L]
        v = y + vx * filt_bias[None, :, None]
        yv = (v * x0).transpose(0, 2, 1)
        return jnp.einsum('bld,de->ble', yv, out_w) + out_b

    def _L0_ffn_ref(x, W_r, W_k, W_v, mu_r, mu_k):
        import jax, jax.numpy as jnp
        import numpy as np
        DIM = 256

        def _reference_tuple_inner(x, W_r, W_k, W_v, mu_r, mu_k):
            B, T, C = x.shape
            x_prev = jnp.concatenate([jnp.zeros((B, 1, C), x.dtype), x[:, :-1, :]], axis=1)
            xr = mu_r * x + (1.0 - mu_r) * x_prev
            xk = mu_k * x + (1.0 - mu_k) * x_prev
            r = jax.nn.sigmoid(jnp.einsum('btc,dc->btd', xr, W_r))
            k = jnp.einsum('btc,dc->btd', xk, W_k)
            k_act = jnp.square(jax.nn.relu(k))
            out = r * jnp.einsum('btc,dc->btd', k_act, W_v)
            new_state = x[:, -1, :]
            return (out, new_state)
        return _reference_tuple_inner(x, W_r, W_k, W_v, mu_r, mu_k)[0]

    def _L1_attn_ref(x, ln1_g, ln1_b, wq, wk, wv, wo, ln2_g, ln2_b, cms_w1, cms_b1, cms_w2, cms_b2):
        import jax, jax.numpy as jnp
        import numpy as np
        DIM = 256
        HEADS = 16
        HD = DIM // HEADS
        B, S = (4, 1024)
        LEVELS = 3
        HID = 4 * DIM
        CHUNK = 128
        EPS = 1e-05

        def layernorm(x, g, b):
            m = jnp.mean(x, axis=-1, keepdims=True)
            v = jnp.var(x, axis=-1, keepdims=True)
            return (x - m) * jax.lax.rsqrt(v + EPS) * g + b

        def _linear_attn_with_memory(h, wq, wk, wv, wo):
            b, s, d = h.shape

            def heads(w):
                return (h @ w).reshape(b, s, HEADS, HD).transpose(0, 2, 1, 3)
            q, k, v = (heads(wq), heads(wk), heads(wv))
            nc = s // CHUNK

            def to_chunks(a):
                return a.reshape(b, HEADS, nc, CHUNK, HD).transpose(2, 0, 1, 3, 4)
            mask = jnp.tril(jnp.ones((CHUNK, CHUNK), h.dtype))

            def step(M, qkv):
                qc, kc, vc = qkv
                inter = jnp.einsum('bhvk,bhck->bhcv', M, qc)
                scores = jnp.einsum('bhcd,bhed->bhce', qc, kc) * mask
                intra = jnp.einsum('bhce,bhev->bhcv', scores, vc)
                M_new = M + jnp.einsum('bhcv,bhck->bhvk', vc, kc)
                return (M_new, inter + intra)
            M0 = jnp.zeros((b, HEADS, HD, HD), h.dtype)
            _, ys = jax.lax.scan(step, M0, (to_chunks(q), to_chunks(k), to_chunks(v)))
            y = ys.transpose(1, 2, 0, 3, 4).reshape(b, HEADS, s, HD)
            y = y.transpose(0, 2, 1, 3).reshape(b, s, d)
            return y @ wo
        x = x + _linear_attn_with_memory(layernorm(x, ln1_g, ln1_b), wq, wk, wv, wo)
        h = layernorm(x, ln2_g, ln2_b)
        for l in range(LEVELS):
            h = jax.nn.gelu(h @ cms_w1[l] + cms_b1[l]) @ cms_w2[l] + cms_b2[l]
        return x + h

    def _L1_ffn_ref(hidden_states, gate_w1, gate_b1, gate_w2, gate_b2, W1, b1, W2, b2, TW1, Tb1, TW2, Tb2):
        import jax, jax.numpy as jnp
        import numpy as np
        B, S, H, F, E = (8, 512, 256, 1024, 8)
        INIT_LAMBDA = 0.2
        x = hidden_states
        h = jax.nn.relu(jnp.einsum('bsh,oh->bso', x, gate_w1) + gate_b1)
        g = jnp.einsum('bso,eo->bse', h, gate_w2) + gate_b2
        g = g.mean(axis=1)
        mW1 = W1 + jnp.einsum('be,efh->bfh', g, TW1)
        mb1 = b1 + g @ Tb1
        mW2 = W2 + jnp.einsum('be,ehf->bhf', g, TW2)
        mb2 = b2 + g @ Tb2
        u = jax.nn.gelu(jnp.einsum('bsh,bfh->bsf', x, mW1) + mb1[:, None, :])
        out = jnp.einsum('bsf,bhf->bsh', u, mW2) + mb2[:, None, :]
        return out
    x = L0_attn_u
    x = x + _layernorm(_L0_attn_ref(_layernorm(x, axis=-1), L0_attn_in_w, L0_attn_in_b, L0_attn_short_w, L0_attn_short_b, L0_attn_mlp_w1, L0_attn_mlp_b1, L0_attn_mlp_w2, L0_attn_mlp_b2, L0_attn_mlp_w3, L0_attn_mlp_b3, L0_attn_mlp_wo, L0_attn_freq, L0_attn_filt_bias, L0_attn_out_w, L0_attn_out_b), axis=-1)
    x = x + _layernorm(_L0_ffn_ref(_layernorm(x, axis=-1), L0_ffn_W_r, L0_ffn_W_k, L0_ffn_W_v, L0_ffn_mu_r, L0_ffn_mu_k), axis=-1)
    x = x + _layernorm(_L1_attn_ref(_layernorm(x, axis=-1), L1_attn_ln1_g, L1_attn_ln1_b, L1_attn_wq, L1_attn_wk, L1_attn_wv, L1_attn_wo, L1_attn_ln2_g, L1_attn_ln2_b, L1_attn_cms_w1, L1_attn_cms_b1, L1_attn_cms_w2, L1_attn_cms_b2), axis=-1)
    x = x + _layernorm(_L1_ffn_ref(_layernorm(x, axis=-1), L1_ffn_gate_w1, L1_ffn_gate_b1, L1_ffn_gate_w2, L1_ffn_gate_b2, L1_ffn_W1, L1_ffn_b1, L1_ffn_W2, L1_ffn_b2, L1_ffn_TW1, L1_ffn_Tb1, L1_ffn_TW2, L1_ffn_Tb2), axis=-1)
    return x

_drawn_inputs = setup_inputs


def setup_inputs(seed=0):
    import zlib

    import numpy as np

    out = dict(_drawn_inputs(seed))
    spreads = {'L0_attn_in_b': (0.0, 0.1),
     'L0_attn_short_b': (0.0, 0.1),
     'L0_attn_mlp_b1': (0.0, 0.1),
     'L0_attn_mlp_b2': (0.0, 0.1),
     'L0_attn_mlp_b3': (0.0, 0.1),
     'L0_attn_freq': (1.0, 0.2),
     'L0_attn_out_b': (0.0, 0.1),
     'L1_attn_ln1_g': (1.0, 0.2),
     'L1_attn_ln1_b': (0.0, 0.1),
     'L1_attn_ln2_g': (1.0, 0.6),
     'L1_attn_ln2_b': (0.0, 0.8),
     'L1_attn_cms_b1': (0.0, 0.8),
     'L1_attn_cms_b2': (0.0, 2.0),
     'L1_ffn_gate_b1': (0.0, 0.46),
     'L1_ffn_gate_b2': (0.20000000298023224, 0.2)}
    factors = {'L0_attn_filt_bias': 2.776,
     'L1_attn_cms_w1': 8.0,
     'L1_attn_cms_w2': 8.0,
     'L1_ffn_gate_w1': 4.499,
     'L1_ffn_b1': 2.732,
     'L1_ffn_Tb1': 4.152}
    for name, (base, spread) in spreads.items():
        noise = np.random.default_rng([zlib.crc32(name.encode()), seed]).standard_normal(out[name].shape)
        drawn = base * np.exp(spread * noise) if base else spread * noise
        out[name] = jnp.asarray(drawn.astype(out[name].dtype))
    for name, factor in factors.items():
        out[name] = (out[name] * factor).astype(out[name].dtype)
    return out
```

```python
from contextlib import ExitStack

import numpy as np

import concourse.bass as bass
from concourse import mybir

P = 128
EPS = 1e-5
F32 = mybir.dt.float32
F32R = mybir.dt.float32r
ALU = mybir.AluOpType
ACT = mybir.ActivationFunctionType

BATCH, SEQ, D = 8, 1024, 256
TOKENS = BATCH * SEQ
DH = D // P
BLK = 512
NBLK = TOKENS // BLK
TT = BLK // P


def wait(eng, sem, value):
    if isinstance(value, int) and value <= 0:
        return
    eng.wait_ge(sem, value)


def rounds(eng, n, body):
    body(0, 0, True, False)
    body(0, 1, False, False)
    if n > 4:
        with eng.Fori(1, n // 2 - 1) as p:
            body(p, 0, False, False)
            body(p, 1, False, False)
    body(n // 2 - 1, 0, False, False)
    body(n // 2 - 1, 1, False, True)


def after(p, par):
    return (p, 1) if par == 0 else (p + 1, 0)


def before(p, par):
    return (p, 0) if par == 1 else (p - 1, 1)


def three_pass(pe, out, w, x, start, stop):
    (w_hi, w_lo), (x_hi, x_lo) = w, x
    pe.matmul(out, w_lo, x_hi, start=start, stop=False)
    pe.matmul(out, w_hi, x_lo, start=False, stop=False)
    return pe.matmul(out, w_hi, x_hi, start=False, stop=stop)


class Phase:

    def __init__(self, nc, ctx, name):
        self.nc, self.ctx, self.name, self.sems = nc, ctx, name, []
        ctx.callback(self.close)

    def close(self):
        if self.sems:
            self.nc.clear_and_free_semaphores(self.sems)
            self.nc.all_engine_barrier()

    def sb(self, name, shape, dt=F32):
        return self.ctx.enter_context(self.nc.sbuf_tensor(f"{self.name}_{name}", shape, dt))

    def ps(self, name, shape, dt=F32):
        return self.ctx.enter_context(self.nc.psum_tensor(f"{self.name}_{name}", shape, dt))

    def sem(self, name):
        self.sems.append(self.nc.alloc_semaphore(name=f"{self.name}_{name}"))
        return self.sems[-1]

    def pair(self, name, shape):
        return self.sb(name + "_hi", shape, F32R), self.sb(name + "_lo", shape, F32R)


def load_weights(nc, name, plain, split, chunk=2048):
    with ExitStack() as ctx:
        ph = Phase(nc, ctx, name)
        n_bufs = 3
        raw = [ph.sb(f"raw{b}", [P, chunk]) for b in range(n_bufs)] if split else []
        loaded_plain = ph.sem("loaded_plain")
        loaded = [ph.sem(f"loaded{b}") for b in range(n_bufs)]
        hi_done = ph.sem("hi_done")
        lo_done = ph.sem("lo_done")
        pieces = []
        for (hi, lo), src in split:
            rows, n = src.shape
            for c in range(0, n, chunk):
                m = min(chunk, n - c)
                pieces.append((rows, m, hi[:, c:c + m], lo[:, c:c + m], src[:, c:c + m]))
        block = ctx.enter_context(nc.Block())

        @block.sync
        def _(sp):
            for n, (rows, m, _, _, src) in enumerate(pieces):
                wait(sp, lo_done, n - n_bufs + 1)
                sp.dma_start(raw[n % n_bufs][0:rows, 0:m], src).then_inc(loaded[n % n_bufs], 16)

        @block.gpsimd
        def _(pool):
            for dst, src in plain:
                pool.dma_start(dst, src).then_inc(loaded_plain, 16)
            if plain:
                pool.wait_ge(loaded_plain, 16 * len(plain))

        @block.scalar
        def _(act):
            for n, (rows, m, hi, _, _) in enumerate(pieces):
                act.wait_ge(loaded[n % n_bufs], 16 * (n // n_bufs + 1))
                act.activation(hi, raw[n % n_bufs][0:rows, 0:m], ACT.Identity).then_inc(hi_done, 1)

        @block.vector
        def _(dve):
            for n, (rows, m, hi, lo, _) in enumerate(pieces):
                dve.wait_ge(hi_done, n + 1)
                dve.tensor_tensor(lo, raw[n % n_bufs][0:rows, 0:m], hi.bitcast(F32),
                                  ALU.subtract).then_inc(lo_done, 1)


class Front:

    def __init__(self, ph, x_dram, ident, in_place=False):
        self.ph, self.x_dram, self.ident = ph, x_dram, ident
        self.x = [ph.sb(f"f_x{b}", [P, TT, D]) for b in range(2)]
        self.xn = self.x if in_place else [ph.sb(f"f_xn{b}", [P, TT, D]) for b in range(2)]
        self.st = [ph.sb(f"f_st{b}", [P, TT, 6]) for b in range(2)]
        self.mv = [ph.sb(f"f_mv{b}", [P, TT, 2]) for b in range(2)]
        self.rs = [ph.sb(f"f_rs{b}", [P, TT]) for b in range(2)]
        self.ve = [ph.sb(f"f_ve{b}", [P, TT]) for b in range(2)]
        self.tick = ph.sb("f_tick", [P, 1])
        self.loaded = [ph.sem(f"x_loaded{b}") for b in range(2)]
        self.st_done = ph.sem("f_stats")
        self.mv_done = ph.sem("f_mv")
        self.ve_done = ph.sem("f_ve")
        self.rs_done = ph.sem("f_rstd")
        self.xn_done = ph.sem("f_xn")
        self.turned = ph.sem("f_turned")

    def load(self, sp, p, par):
        i = 2 * p + par
        src = self.x_dram[bass.ds(i * BLK, BLK), :].rearrange("(t p) d -> p t d", p=P)
        sp.dma_start(self.x[par][:, :, :], src).then_inc(self.loaded[par], 16)

    def stats(self, dve, p, par):
        i = 2 * p + par
        dve.wait_ge(self.loaded[par], 16 * (p + 1))
        for t in range(TT):
            last = dve.bn_stats(self.st[par][:, t, :], self.x[par][:, t, :])
        last.then_inc(self.st_done, 1)
        dve.wait_ge(self.st_done, i + 1)
        wait(dve, self.rs_done, i - 1)
        dve.memset(self.tick[:, :], 0.0)
        for t in range(TT):
            last = dve.bn_aggr(self.mv[par][:, t, :], self.st[par][:, t, :])
        last.then_inc(self.mv_done, 1)

    def rstd(self, pool, consts, p, par):
        i = 2 * p + par
        pool.wait_ge(self.mv_done, i + 1)
        wait(pool, self.xn_done, i - 1)
        pool.tensor_tensor(self.ve[par][:, :], self.mv[par][:, :, 1], consts["eps"], ALU.add).then_inc(self.ve_done, 1)
        pool.wait_ge(self.ve_done, i + 1)
        pool.tensor_tensor(self.rs[par][:, :], self.ve[par][:, :], consts["mhalf"], ALU.pow).then_inc(self.rs_done, 1)

    def norm(self, dve, p, par):
        i = 2 * p + par
        dve.wait_ge(self.rs_done, i + 1)
        wait(dve, self.turned, i - 1)
        for t in range(TT):
            last = dve.tensor_scalar(self.xn[par][:, t, :], self.x[par][:, t, :], self.mv[par][:, t, 0:1],
                                     self.rs[par][:, t:t + 1], ALU.subtract, ALU.mult)
        last.then_inc(self.xn_done, 1)

    def turn(self, pe, banks, p, par):
        pe.wait_ge(self.xn_done, 2 * p + par + 1)
        for h in range(DH):
            for t in range(TT):
                last = pe.transpose(banks[h][:, t * P:(t + 1) * P], self.xn[par][:, t, h * P:(h + 1) * P],
                                    self.ident[:, :])
        last.then_inc(self.turned, 1)


class Back:

    def __init__(self, ph, front, y_dram):
        self.ph, self.front, self.y_dram = ph, front, y_dram
        self.z = [ph.sb(f"z{b}", [P, TT, D]) for b in range(2)]
        self.st = [ph.sb(f"b_st{b}", [P, TT, 6]) for b in range(2)]
        self.mv = [ph.sb(f"b_mv{b}", [P, TT, 2]) for b in range(2)]
        self.rs = [ph.sb(f"b_rs{b}", [P, TT]) for b in range(2)]
        self.ve = [ph.sb(f"b_ve{b}", [P, TT]) for b in range(2)]
        self.tick = ph.sb("b_tick", [P, 1])
        self.st_done = ph.sem("b_stats")
        self.mv_done = ph.sem("b_mv")
        self.ve_done = ph.sem("b_ve")
        self.rs_done = ph.sem("b_rstd")
        self.zn_done = ph.sem("b_zn")
        self.added = ph.sem("b_added")
        self.stored = [ph.sem(f"b_stored{b}") for b in range(2)]

    def z_free(self, eng, p, par):
        wait(eng, self.stored[par], 16 * p)

    def stats(self, dve, z_sem, z_count, p, par):
        i = 2 * p + par
        dve.wait_ge(z_sem, z_count)
        for t in range(TT):
            last = dve.bn_stats(self.st[par][:, t, :], self.z[par][:, t, :])
        last.then_inc(self.st_done, 1)
        dve.wait_ge(self.st_done, i + 1)
        wait(dve, self.rs_done, i - 1)
        dve.memset(self.tick[:, :], 0.0)
        for t in range(TT):
            last = dve.bn_aggr(self.mv[par][:, t, :], self.st[par][:, t, :])
        last.then_inc(self.mv_done, 1)

    def rstd(self, pool, consts, p, par):
        i = 2 * p + par
        pool.wait_ge(self.mv_done, i + 1)
        wait(pool, self.zn_done, i - 1)
        pool.tensor_tensor(self.ve[par][:, :], self.mv[par][:, :, 1], consts["eps"], ALU.add).then_inc(self.ve_done, 1)
        pool.wait_ge(self.ve_done, i + 1)
        pool.tensor_tensor(self.rs[par][:, :], self.ve[par][:, :], consts["mhalf"], ALU.pow).then_inc(self.rs_done, 1)

    def norm(self, dve, p, par):
        i = 2 * p + par
        dve.wait_ge(self.rs_done, i + 1)
        z = self.z[par]
        for t in range(TT):
            last = dve.tensor_scalar(z[:, t, :], z[:, t, :], self.mv[par][:, t, 0:1],
                                     self.rs[par][:, t:t + 1], ALU.subtract, ALU.mult)
        last.then_inc(self.zn_done, 1)

    def add(self, pool, p, par):
        pool.wait_ge(self.zn_done, 2 * p + par + 1)
        z = self.z[par]
        pool.tensor_tensor(z[:, :, :], z[:, :, :], self.front.x[par][:, :, :], ALU.add).then_inc(self.added, 1)

    def store(self, eng, p, par):
        i = 2 * p + par
        eng.wait_ge(self.added, i + 1)
        dst = self.y_dram[bass.ds(i * BLK, BLK), :].rearrange("(t p) d -> p t d", p=P)
        eng.dma_start(dst, self.z[par][:, :, :]).then_inc(self.stored[par], 16)

    def all_stored(self, eng):
        for s in self.stored:
            eng.wait_ge(s, 16 * NBLK // 2)


def channel_mix(nc, x_dram, y_dram, consts, W_r, W_k, W_v, mu_r, mu_k):
    with ExitStack() as ctx:
        ph = Phase(nc, ctx, "cm")
        wr = ph.pair("wr", [P, DH, D])
        wk = ph.pair("wk", [P, DH, D])
        wv = ph.pair("wv", [P, DH, D])
        mu = ph.sb("mu", [P, 2, DH])
        flat = lambda w: tuple(t[:, :, :].rearrange("p a b -> p (a b)") for t in w)
        dram = lambda w: w
        load_weights(nc, "cml",
                     [(mu[:, 0, :], mu_r), (mu[:, 1, :], mu_k)],
                     [(flat(wr), dram(W_r)), (flat(wk), dram(W_k)), (flat(wv), dram(W_v))])
        front = Front(ph, x_dram, consts["ident"])
        back = Back(ph, front, y_dram)
        xT = [ph.sb(f"xT{b}", [P, DH, BLK + 1]) for b in range(2)]
        dx = ph.sb("dx", [P, DH, BLK])
        mixed = {m: [ph.sb(f"mix_{m}{b}", [P, DH, BLK]) for b in range(2)] for m in "rk"}
        mixp = {m: [ph.pair(f"mixp_{m}{b}", [P, DH, BLK]) for b in range(2)] for m in "rk"}
        kr = ph.sb("kr", [P, DH, BLK])
        ka = ph.sb("ka", [P, DH, BLK])
        kap = ph.pair("kap", [P, DH, BLK])
        r = ph.sb("r", [P, TT, D])
        pT = [ph.ps(f"pT{h}", [P, BLK]) for h in range(DH)]
        pK = [ph.ps(f"pK{h}", [P, BLK]) for h in range(DH)]
        pR = [ph.ps(f"pR{h}", [P, 2, D]) for h in range(2)]
        pV = [ph.ps(f"pV{h}", [P, 2, D]) for h in range(2)]
        zeroed = ph.sem("zeroed")
        xT_done = ph.sem("xT")
        dx_done = ph.sem("dx")
        mix_done = ph.sem("mix")
        hi_done = ph.sem("mix_hi")
        lo_done = ph.sem("mix_lo")
        k_done = ph.sem("k")
        kr_done = ph.sem("kr")
        ka_done = ph.sem("ka")
        kahi_done = ph.sem("kahi")
        kalo_done = ph.sem("kalo")
        r_done = ph.sem("r_mm")
        rs_done = ph.sem("r_sig")
        v_done = ph.sem("v_mm")
        z_done = ph.sem("z")
        block = ctx.enter_context(nc.Block())

        @block.sync
        def _(sp):
            front.load(sp, 0, 0)
            front.load(sp, 0, 1)

            def body(p, par, first, last):
                back.store(sp, p, par)
                if not (isinstance(p, int) and p == NBLK // 2 - 1):
                    front.load(sp, p + 1, par)

            rounds(sp, NBLK, body)
            back.all_stored(sp)

        @block.gpsimd
        def _(pool):
            pool.memset(xT[0][:, :, 0:1], 0.0).then_inc(zeroed, 1)
            front.rstd(pool, consts, 0, 0)

            def body(p, par, first, last):
                i = 2 * p + par
                if not first:
                    back.add(pool, *before(p, par))
                pool.wait_ge(xT_done, i + 1)
                wait(pool, mix_done, 2 * i)
                if first:
                    pool.wait_ge(zeroed, 1)
                pool.tensor_tensor(dx[:, :, :], xT[par][:, :, 1:BLK + 1], xT[par][:, :, 0:BLK],
                                   ALU.subtract).then_inc(dx_done, 1)
                pool.wait_ge(kr_done, i + 1)
                wait(pool, kalo_done, i)
                pool.tensor_tensor(ka[:, :, :], kr[:, :, :], kr[:, :, :], ALU.mult).then_inc(ka_done, 1)
                if not last:
                    front.rstd(pool, consts, *after(p, par))
                back.rstd(pool, consts, p, par)

            rounds(pool, NBLK, body)
            back.add(pool, NBLK // 2 - 1, 1)

        @block.scalar
        def _(act):
            def take(p, par):
                i = 2 * p + par
                act.wait_ge(front.turned, i + 1)
                wait(act, mix_done, 2 * (i - 1))
                for h in range(DH):
                    last = act.activation(xT[par][:, h, 1:BLK + 1], pT[h][:, :], ACT.Identity)
                if par:
                    last = act.activation(xT[1][:, :, 0:1], xT[0][:, :, BLK:BLK + 1], ACT.Identity)
                last.then_inc(xT_done, 1)

            take(0, 0)

            def body(p, par, first, last):
                i = 2 * p + par
                for n, m in enumerate("kr"):
                    act.wait_ge(mix_done, 2 * i + n + 1)
                    wait(act, r_done if m == "r" else k_done, i - 1)
                    act.activation(mixp[m][par][0][:, :, :], mixed[m][par][:, :, :],
                                   ACT.Identity).then_inc(hi_done, 1)
                act.wait_ge(k_done, i + 1)
                wait(act, ka_done, i)
                for h in range(DH):
                    last_ = act.activation(kr[:, h, :], pK[h][:, :], ACT.Relu)
                last_.then_inc(kr_done, 1)
                act.wait_ge(r_done, i + 1)
                wait(act, z_done, i)
                for h in range(2):
                    last_ = act.activation(r[:, 2 * h:2 * h + 2, :], pR[h][:, :, :], ACT.Sigmoid)
                last_.then_inc(rs_done, 1)
                act.wait_ge(ka_done, i + 1)
                wait(act, v_done, i)
                act.activation(kap[0][:, :, :], ka[:, :, :], ACT.Identity).then_inc(kahi_done, 1)
                if not last:
                    take(*after(p, par))

            rounds(act, NBLK, body)

        @block.vector
        def _(dve):
            front.stats(dve, 0, 0)
            front.norm(dve, 0, 0)

            def body(p, par, first, last):
                i = 2 * p + par
                if not first:
                    back.norm(dve, *before(p, par))
                dve.wait_ge(dx_done, i + 1)
                for n, m in enumerate("kr"):
                    wait(dve, lo_done, 2 * (i - 2) + n + 1)
                    wait(dve, hi_done, 2 * (i - 2) + n + 1)
                    for h in range(DH):
                        s = mu[:, 0 if m == "r" else 1, h:h + 1]
                        last_ = dve.scalar_tensor_tensor(mixed[m][par][:, h, :], dx[:, h, :], s,
                                                         xT[par][:, h, 0:BLK], ALU.mult, ALU.add)
                    last_.then_inc(mix_done, 1)
                for n, m in enumerate("kr"):
                    dve.wait_ge(hi_done, 2 * i + n + 1)
                    hi, lo = mixp[m][par]
                    dve.wait_ge(mix_done, 2 * i + n + 1)
                    wait(dve, r_done if m == "r" else k_done, i - 1)
                    dve.tensor_tensor(lo[:, :, :], mixed[m][par][:, :, :], hi[:, :, :].bitcast(F32),
                                      ALU.subtract).then_inc(lo_done, 1)
                if not last:
                    front.stats(dve, *after(p, par))
                dve.wait_ge(kahi_done, i + 1)
                wait(dve, v_done, i)
                dve.tensor_tensor(kap[1][:, :, :], ka[:, :, :], kap[0][:, :, :].bitcast(F32),
                                  ALU.subtract).then_inc(kalo_done, 1)
                if not last:
                    front.norm(dve, *after(p, par))
                dve.wait_ge(v_done, i + 1)
                dve.wait_ge(rs_done, i + 1)
                back.z_free(dve, p, par)
                for h in range(2):
                    last_ = dve.tensor_tensor(back.z[par][:, 2 * h:2 * h + 2, :], pV[h][:, :, :],
                                              r[:, 2 * h:2 * h + 2, :], ALU.mult)
                last_.then_inc(z_done, 1)
                back.stats(dve, z_done, i + 1, p, par)

            rounds(dve, NBLK, body)
            back.norm(dve, NBLK // 2 - 1, 1)

        @block.tensor
        def _(pe):
            front.turn(pe, pT, 0, 0)

            def body(p, par, first, last):
                i = 2 * p + par
                pe.wait_ge(lo_done, 2 * i + 1)
                wait(pe, kr_done, i)
                kh, kl = mixp["k"][par]
                for m in range(DH):
                    for k in range(DH):
                        mm = three_pass(pe, pK[m][:, :], (wk[0][:, k, m * P:(m + 1) * P], wk[1][:, k, m * P:(m + 1) * P]),
                                        (kh[:, k, :], kl[:, k, :]), k == 0, k == DH - 1)
                mm.then_inc(k_done, 1)
                pe.wait_ge(lo_done, 2 * i + 2)
                wait(pe, rs_done, i)
                rh, rl = mixp["r"][par]
                for t in range(TT):
                    for k in range(DH):
                        ts = slice(t * P, (t + 1) * P)
                        mm = three_pass(pe, pR[t // 2][:, t % 2, :], (rh[:, k, ts], rl[:, k, ts]),
                                        (wr[0][:, k, :], wr[1][:, k, :]), k == 0, k == DH - 1)
                mm.then_inc(r_done, 1)
                if not last:
                    pe.wait_ge(xT_done, i + 1)
                    front.turn(pe, pT, *after(p, par))
                pe.wait_ge(kalo_done, i + 1)
                wait(pe, z_done, i)
                for t in range(TT):
                    for k in range(DH):
                        ts = slice(t * P, (t + 1) * P)
                        mm = three_pass(pe, pV[t // 2][:, t % 2, :], (kap[0][:, k, ts], kap[1][:, k, ts]),
                                        (wv[0][:, k, :], wv[1][:, k, :]), k == 0, k == DH - 1)
                mm.then_inc(v_done, 1)

            rounds(pe, NBLK, body)


def make_consts(nc, ctx, ident_d):
    ph = Phase(nc, ctx, "c")
    ident = ph.sb("ident", [P, P])
    mhalf = ph.sb("mhalf", [P, TT])
    eps = ph.sb("eps", [P, TT])
    one = ph.sb("one", [P, TT])
    loaded = ph.sem("loaded")
    made = ph.sem("made")
    with nc.Block() as block:
        @block.sync
        def _(sp):
            sp.dma_start(ident[:, :], ident_d).then_inc(loaded, 16)
            sp.wait_ge(loaded, 16)

        @block.gpsimd
        def _(pool):
            pool.memset(mhalf[:, :], -0.5).then_inc(made, 1)
            pool.memset(eps[:, :], EPS).then_inc(made, 1)
            pool.memset(one[:, :], 1.0).then_inc(made, 1)
            pool.wait_ge(made, 3)
    return {"ident": ident, "mhalf": mhalf[:, :], "eps": eps[:, :], "one": one[:, :]}


HEADS = 16
HD = D // HEADS
CHUNK = 128
PAIRS = P // (2 * HD)


def linear_attention(nc, x_dram, y_dram, consts, wq, wk, wv, wo, ln_g, ln_b, odd_d, causal_d, same_d):
    with ExitStack() as ctx:
        ph = Phase(nc, ctx, "la")
        w = {n: ph.pair(f"w{n}", [P, DH, D]) for n in ("q", "k", "o")}
        wkv = ph.pair("wkv", [P, DH, 2 * D])
        gb = ph.sb("gb", [P, 2, DH])
        odd = ph.sb("odd", [P, 2])
        causal = ph.sb("causal", [P, P])
        same = ph.sb("same", [P, DH, P])
        flat = lambda t: tuple(x[:, :, :].rearrange("p a b -> p (a b)") for x in t)
        kvd = []
        for h in range(DH):
            for n, src in enumerate((wk, wv)):
                kvd.append((tuple(t[:, h, n * D:(n + 1) * D] for t in wkv), src[:, h * D:(h + 1) * D]))
        load_weights(nc, "lal",
                     [(gb[:, 0, :], ln_g), (gb[:, 1, :], ln_b), (odd[:, :], odd_d), (causal[:, :], causal_d),
                      (same[:, 0, :], same_d), (same[:, 1, :], same_d)],
                     [(flat(w["q"]), wq), (flat(w["k"]), wk), (flat(w["o"]), wo)] + kvd)
        front = Front(ph, x_dram, consts["ident"])
        tmp = ph.sb("tmp", [P, 5, TT])
        res = [ph.sb(f"res{b}", [P, TT]) for b in range(2)]
        hf = ph.sb("hf", [P, DH, BLK])
        hp = ph.pair("hp", [P, DH, BLK])
        qT = ph.sb("qT", [P, DH, BLK])
        kE = [ph.sb(f"kE{o}", [P, DH, BLK]) for o in range(2)]
        kv = ph.sb("kv", [P, TT, 2 * D])
        sT = [ph.sb(f"sT{b}", [P, PAIRS, 4, P]) for b in range(2)]
        state = [ph.sb(f"state{b}", [P, DH, P]) for b in range(2)]
        ys = ph.sb("ys", [P, TT, D])
        yp = ph.pair("yp", [P, DH, BLK])
        z = [ph.sb(f"z{b}", [P, TT, D]) for b in range(2)]
        pA = [ph.ps(f"pA{h}", [P, BLK]) for h in range(DH)]
        pS = [ph.ps(f"pS{j}", [P, 4, P]) for j in range(PAIRS)]
        pY = ph.ps("pY", [P, 2 * D])
        pM = ph.ps("pM", [P, DH * P * 2])
        small = ph.sem("small")
        hf_done = ph.sem("hf")
        hhi_done = ph.sem("hhi")
        hlo_done = ph.sem("hlo")
        q_mm, k_mm, kv_mm = ph.sem("q_mm"), ph.sem("k_mm"), ph.sem("kv_mm")
        q_ev, k_ev, kv_ev = ph.sem("q_ev"), ph.sem("k_ev"), ph.sem("kv_ev")
        s_mm = ph.sem("s_mm")
        s_ev = ph.sem("s_ev")
        m_mm = ph.sem("m_mm")
        m_ev = ph.sem("m_ev")
        y_mm = ph.sem("y_mm")
        y_ev = ph.sem("y_ev")
        yT_mm = ph.sem("yT_mm")
        yhi_done = ph.sem("yhi")
        ylo_done = ph.sem("ylo")
        o_mm = ph.sem("o_mm")
        z_done = ph.sem("z")
        stored = [ph.sem(f"stored{b}") for b in range(2)]
        block = ctx.enter_context(nc.Block())

        @block.sync
        def _(sp):
            front.load(sp, 0, 0)
            front.load(sp, 0, 1)

            def body(p, par, first, last):
                i = 2 * p + par
                if not (isinstance(p, int) and p == NBLK // 2 - 1):
                    sp.wait_ge(front.xn_done, i + 1)
                    front.load(sp, p + 1, par)
                sp.wait_ge(z_done, i + 1)
                dst = y_dram[bass.ds(i * BLK, BLK), :].rearrange("(t p) d -> p t d", p=P)
                sp.dma_start(dst, z[par][:, :, :]).then_inc(stored[par], 16)

            rounds(sp, NBLK, body)
            for s in stored:
                sp.wait_ge(s, 16 * NBLK // 2)

        @block.gpsimd
        def _(pool):
            def rstd(p, par):
                i = 2 * p + par
                var = front.mv[par][:, :, 1]
                a, r1, r2, t1, t2 = (tmp[:, n, :] for n in range(5))
                count = [0]

                def step(ins):
                    count[0] += 1
                    ins.then_inc(small, 1)
                    pool.wait_ge(small, 7 * i + count[0])

                pool.wait_ge(front.mv_done, i + 1)
                wait(pool, front.xn_done, i - 1)
                wait(pool, z_done, i - 1)
                step(pool.tensor_tensor(a, var, consts["eps"], ALU.add))
                step(pool.tensor_tensor(r1, a, consts["mhalf"], ALU.pow))
                step(pool.tensor_tensor(t1, r1, r1, ALU.mult))
                step(pool.tensor_tensor(t2, t1, var, ALU.mult))
                step(pool.tensor_tensor(a, t2, consts["eps"], ALU.add))
                step(pool.tensor_tensor(r2, a, consts["mhalf"], ALU.pow))
                step(pool.tensor_tensor(res[par][:, :], a, r2, ALU.mult))
                pool.tensor_tensor(front.rs[par][:, :], r1, r2, ALU.mult).then_inc(front.rs_done, 1)

            rstd(0, 0)

            def body(p, par, first, last):
                if not last:
                    rstd(*after(p, par))

            rounds(pool, NBLK, body)

        @block.scalar
        def _(act):
            def body(p, par, first, last):
                i = 2 * p + par
                act.wait_ge(front.turned, i + 1)
                wait(act, hlo_done, i)
                for h in range(DH):
                    last_ = act.activation(hf[:, h, :], pA[h][:, :], ACT.Identity, bias=gb[:, 1, h:h + 1],
                                           scale=gb[:, 0, h:h + 1])
                last_.then_inc(hf_done, 1)
                act.wait_ge(hf_done, i + 1)
                wait(act, kv_mm, TT * i)
                act.activation(hp[0][:, :, :], hf[:, :, :], ACT.Identity).then_inc(hhi_done, 1)
                act.wait_ge(q_mm, i + 1)
                wait(act, y_mm, TT * i)
                for h in range(DH):
                    last_ = act.activation(qT[:, h, :], pA[h][:, :], ACT.Identity)
                last_.then_inc(q_ev, 1)
                act.wait_ge(k_mm, i + 1)
                wait(act, s_mm, TT * i)
                for o in range(2):
                    for h in range(DH):
                        last_ = act.activation(kE[o][:, h, :], pA[h][:, :], ACT.Identity, scale=odd[:, o:o + 1])
                last_.then_inc(k_ev, 1)
                for t in range(TT):
                    act.wait_ge(y_mm, TT * i + t + 1)
                    if t == 0:
                        wait(act, yT_mm, i)
                    act.activation(ys[:, t, :], pY[:, 0:D], ACT.Identity).then_inc(y_ev, 1)
                act.wait_ge(yT_mm, i + 1)
                wait(act, o_mm, i)
                for h in range(DH):
                    last_ = act.activation(yp[0][:, h, :], pA[h][:, :], ACT.Identity)
                last_.then_inc(yhi_done, 1)

            rounds(act, NBLK, body)

        @block.vector
        def _(dve):
            front.stats(dve, 0, 0)
            front.norm(dve, 0, 0)

            def body(p, par, first, last):
                i = 2 * p + par
                if not last:
                    front.stats(dve, *after(p, par))
                dve.wait_ge(hf_done, i + 1)
                dve.wait_ge(hhi_done, i + 1)
                wait(dve, kv_mm, TT * i)
                dve.tensor_tensor(hp[1][:, :, :], hf[:, :, :], hp[0][:, :, :].bitcast(F32),
                                  ALU.subtract).then_inc(hlo_done, 1)
                for t in range(TT):
                    dve.wait_ge(kv_mm, TT * i + t + 1)
                    if t == 0:
                        wait(dve, y_mm, TT * i)
                    dve.tensor_copy(kv[:, t, :], pS[t][:, :, :].rearrange("p a b -> p (a b)")).then_inc(kv_ev, 1)
                if not last:
                    front.norm(dve, *after(p, par))
                for t in range(TT):
                    c = TT * i + t
                    wait(dve, y_mm, c - 1)
                    for j in range(PAIRS):
                        dve.wait_ge(s_mm, c + 1)
                        mask = causal[:, :].unsqueeze(1).broadcast_to([P, 4, P])
                        dve.tensor_tensor(sT[t % 2][:, j, :, :], pS[j][:, :, :], mask, ALU.mult).then_inc(s_ev, 1)
                    if not (par == 1 and t == TT - 1):
                        dve.wait_ge(m_mm, 7 * p + TT * par + t + 1)
                        dve.tensor_tensor(state[t % 2][:, :, :],
                                          pM[:, 0:DH * P].rearrange("p (a b) -> p a b", a=DH),
                                          same[:, :, :], ALU.mult).then_inc(m_ev, 1)
                dve.wait_ge(yhi_done, i + 1)
                wait(dve, o_mm, i)
                for h in range(DH):
                    last_ = dve.tensor_tensor(yp[1][:, h, :], pA[h][:, :], yp[0][:, h, :].bitcast(F32), ALU.subtract)
                last_.then_inc(ylo_done, 1)
                dve.wait_ge(o_mm, i + 1)
                wait(dve, stored[par], 16 * p)
                for t in range(TT):
                    po = pS[t // 2][:, 2 * (t % 2):2 * (t % 2) + 2, :].rearrange("p a b -> p (a b)")
                    last_ = dve.scalar_tensor_tensor(z[par][:, t, :], front.xn[par][:, t, :], res[par][:, t:t + 1],
                                                     po, ALU.mult, ALU.add)
                last_.then_inc(z_done, 1)

            rounds(dve, NBLK, body)

        @block.tensor
        def _(pe):
            def body(p, par, first, last):
                i = 2 * p + par
                wait(pe, ylo_done, i)
                front.turn(pe, pA, p, par)
                pe.wait_ge(hf_done, i + 1)
                pe.wait_ge(hlo_done, i + 1)
                hh, hl = hp
                for name, done, free in (("q", q_mm, None), ("k", k_mm, q_ev)):
                    if free is not None:
                        pe.wait_ge(free, i + 1)
                    for m in range(DH):
                        for k in range(DH):
                            wh, wl = (x[:, k, m * P:(m + 1) * P] for x in w[name])
                            mm = three_pass(pe, pA[m][:, :], (wh, wl), (hh[:, k, :], hl[:, k, :]),
                                            k == 0, k == DH - 1)
                    mm.then_inc(done, 1)
                wait(pe, z_done, i)
                for t in range(TT):
                    ts = slice(t * P, (t + 1) * P)
                    for k in range(DH):
                        mm = three_pass(pe, pS[t][:, :, :].rearrange("p a b -> p (a b)"),
                                        (hh[:, k, ts], hl[:, k, ts]),
                                        (wkv[0][:, k, :], wkv[1][:, k, :]), k == 0, k == DH - 1)
                    mm.then_inc(kv_mm, 1)
                pe.wait_ge(k_ev, i + 1)
                pe.wait_ge(kv_ev, TT * (i + 1))
                for t in range(TT):
                    c = TT * i + t
                    ts = slice(t * P, (t + 1) * P)
                    if t:
                        pe.wait_ge(s_ev, PAIRS * c)
                    for h in range(DH):
                        for o in range(2):
                            for j in range(PAIRS):
                                js = slice(2 * HD * j, 2 * HD * (j + 1))
                                mm = pe.matmul(pS[j][:, 2 * h + o, :], kE[o][js, h, ts], qT[js, h, ts],
                                               start=True, stop=True)
                    mm.then_inc(s_mm, 1)
                    if not (par == 1 and t == TT - 1):
                        n = 7 * p + TT * par + t
                        wait(pe, m_ev, n)
                        for h in range(DH):
                            hs = slice(h * P, (h + 1) * P)
                            mm = pe.matmul(pM[:, hs], kv[:, t, hs], kv[:, t, D + h * P:D + (h + 1) * P],
                                           start=(par == 0 and t == 0 and h == 0), stop=True,
                                           skip_group_check=True)
                        mm.then_inc(m_mm, 1)
                    wait(pe, y_ev, c)
                    begun = False
                    if not (par == 0 and t == 0):
                        pe.wait_ge(m_ev, 7 * p + TT * par + t)
                        for h in range(DH):
                            pe.matmul(pY[:, h * P:(h + 1) * P], qT[:, h, ts], state[(t - 1) % 2][:, h, :],
                                      start=not begun, stop=False, skip_group_check=True)
                            begun = True
                    for h in range(DH):
                        for j in range(PAIRS):
                            pe.wait_ge(s_ev, PAIRS * c + j + 1)
                            for o in range(2):
                                head = 8 * h + 2 * j + o
                                vs = slice(head * HD, (head + 1) * HD)
                                mm = pe.matmul(pY[:, vs], sT[t % 2][:, j, 2 * h + o, :],
                                               kv[:, t, D + head * HD:D + (head + 1) * HD],
                                               start=not begun, stop=True, skip_group_check=True)
                                begun = True
                    mm.then_inc(y_mm, 1)
                pe.wait_ge(y_ev, TT * (i + 1))
                for h in range(DH):
                    for t in range(TT):
                        mm = pe.transpose(pA[h][:, t * P:(t + 1) * P], ys[:, t, h * P:(h + 1) * P],
                                          consts["ident"][:, :])
                mm.then_inc(yT_mm, 1)
                pe.wait_ge(ylo_done, i + 1)
                for t in range(TT):
                    po = pS[t // 2][:, 2 * (t % 2):2 * (t % 2) + 2, :].rearrange("p a b -> p (a b)")
                    ts = slice(t * P, (t + 1) * P)
                    for k in range(DH):
                        mm = three_pass(pe, po, (yp[0][:, k, ts], yp[1][:, k, ts]),
                                        (w["o"][0][:, k, :], w["o"][1][:, k, :]), k == 0, k == DH - 1)
                mm.then_inc(o_mm, 1)

            rounds(pe, NBLK, body)


HID = 1024
FT = HID // P
RING = 4


class Hidden:

    def __init__(self, ph):
        self.g = [ph.sb(f"g{n}", [P, BLK]) for n in range(RING)]
        self.gp = [ph.pair(f"gp{n}", [P, BLK]) for n in range(RING)]
        self.pg = [ph.ps(f"pg{n}", [P, BLK]) for n in range(RING)]
        self.mm = ph.sem("hid_mm")
        self.g_done = ph.sem("hid_gelu")
        self.hi_done = ph.sem("hid_hi")
        self.lo_done = ph.sem("hid_lo")
        self.used = ph.sem("hid_used")

    def up(self, pe, n, f, w, h, waits):
        s = f % RING
        for sem, value in waits:
            wait(pe, sem, value)
        wait(pe, self.g_done, n - RING + 1)
        for k in range(DH):
            mm = three_pass(pe, self.pg[s][:, :], tuple(x[:, k, f * P:(f + 1) * P] for x in w),
                            tuple(x[:, k, :] for x in h), k == 0, k == DH - 1)
        mm.then_inc(self.mm, 1)

    def gelu(self, act, n, f, bias):
        s = f % RING
        act.wait_ge(self.mm, n + 1)
        wait(act, self.lo_done, n - RING + 1)
        act.activation(self.g[s][:, :], self.pg[s][:, :], ACT.Gelu_apprx_tanh, bias=bias).then_inc(self.g_done, 1)

    def high(self, act, n, f):
        s = f % RING
        act.wait_ge(self.g_done, n + 1)
        wait(act, self.used, n - RING + 1)
        act.activation(self.gp[s][0][:, :], self.g[s][:, :], ACT.Identity).then_inc(self.hi_done, 1)

    def low(self, dve, n, f):
        s = f % RING
        dve.wait_ge(self.hi_done, n + 1)
        wait(dve, self.used, n - RING + 1)
        dve.tensor_tensor(self.gp[s][1][:, :], self.g[s][:, :], self.gp[s][0][:, :].bitcast(F32),
                          ALU.subtract).then_inc(self.lo_done, 1)

    def down(self, pe, n, f, w, banks):
        s = f % RING
        pe.wait_ge(self.lo_done, n + 1)
        for m in range(DH):
            mm = three_pass(pe, banks[m][:, :], tuple(x[:, f, m * P:(m + 1) * P] for x in w),
                            tuple(x[:, :] for x in self.gp[s]), f == 0, f == FT - 1)
        mm.then_inc(self.used, 1)
        return mm

    def down_tokens(self, pe, n, f, w, banks):
        s = f % RING
        pe.wait_ge(self.lo_done, n + 1)
        for t in range(TT):
            out = banks[t // 2][:, (t % 2) * D:(t % 2 + 1) * D]
            ts = slice(t * P, (t + 1) * P)
            (xh, xl), (wh, wl) = (x[:, ts] for x in self.gp[s]), (x[:, f, :] for x in w)
            first = f == 0 and t % 2 == 0
            pe.matmul(out, xl, wh, start=first, stop=False, skip_group_check=True)
            pe.matmul(out, xh, wl, start=False, stop=False, skip_group_check=True)
            mm = pe.matmul(out, xh, wh, start=False, stop=f == FT - 1, skip_group_check=True)
        mm.then_inc(self.used, 1)
        return mm


LEVELS = 3


def gelu_levels(nc, x_dram, n_dram, y_dram, consts, ln_g, ln_b, w1_d, b1_d, w2_d, b2_d, b2row_d):
    with ExitStack() as ctx:
        ph = Phase(nc, ctx, "gl")
        w1 = [ph.pair(f"w1_{l}", [P, DH, HID]) for l in range(LEVELS)]
        w2 = [ph.pair(f"w2_{l}", [P, FT, D]) for l in range(LEVELS)]
        gb = ph.sb("gb", [P, 2, DH])
        b1 = ph.sb("b1", [P, LEVELS, FT])
        b2 = ph.sb("b2", [P, LEVELS, DH])
        b2row = ph.sb("b2row", [P, D])
        flat = lambda t: tuple(x[:, :, :].rearrange("p a b -> p (a b)") for x in t)
        split = []
        for l in range(LEVELS):
            split += [(flat(w1[l]), w1_d[l]), (flat(w2[l]), w2_d[l])]
        load_weights(nc, "gll",
                     [(gb[:, 0, :], ln_g), (gb[:, 1, :], ln_b),
                      (b1[:, :, :].rearrange("p a b -> p (a b)"), b1_d),
                      (b2[:, :, :].rearrange("p a b -> p (a b)"), b2_d),
                      (b2row[:, :], b2row_d.unsqueeze(0).broadcast_to([P, D]))], split)
        front = Front(ph, n_dram, consts["ident"])
        back = Back(ph, front, y_dram)
        back.front = None
        xres = [ph.sb(f"xres{b}", [P, TT, D]) for b in range(2)]
        hf = [ph.sb(f"hf{b}", [P, DH, BLK]) for b in range(2)]
        hp = [ph.pair(f"hp{b}", [P, DH, BLK]) for b in range(2)]
        hid = Hidden(ph)
        pT = [ph.ps(f"pT{h}", [P, BLK]) for h in range(DH)]
        pH = [ph.ps(f"pH{h}", [P, BLK]) for h in range(DH)]
        xres_loaded = [ph.sem(f"xres_loaded{b}") for b in range(2)]
        moved = ph.sem("moved")
        hf_done = [ph.sem(f"hf{b}") for b in range(2)]
        hhi_done = [ph.sem(f"hhi{b}") for b in range(2)]
        hlo_done = [ph.sem(f"hlo{b}") for b in range(2)]
        z_done = ph.sem("z")
        block = ctx.enter_context(nc.Block())
        PAIRSOF = NBLK // 2

        def passes(eng, body):
            body(0, True, False)
            with eng.Fori(1, PAIRSOF - 1) as p:
                body(p, False, False)
            body(PAIRSOF - 1, False, True)

        def order(p):
            for l in range(LEVELS):
                for b in range(2):
                    yield 2 * LEVELS * p + 2 * l + b, l, b

        @block.sync
        def _(sp):
            def load_res(p, b):
                src = x_dram[bass.ds((2 * p + b) * BLK, BLK), :].rearrange("(t p) d -> p t d", p=P)
                sp.dma_start(xres[b][:, :, :], src).then_inc(xres_loaded[b], 16)

            for b in range(2):
                front.load(sp, 0, b)
            for b in range(2):
                load_res(0, b)

            def body(p, first, last):
                if not first:
                    back.store(sp, p - 1, 1)
                    load_res(p, 1)
                if not last:
                    for b in range(2):
                        sp.wait_ge(moved, 2 * p + b + 1)
                        front.load(sp, p + 1, b)
                back.store(sp, p, 0)
                if not last:
                    load_res(p + 1, 0)

            passes(sp, body)
            back.store(sp, PAIRSOF - 1, 1)
            back.all_stored(sp)

        @block.gpsimd
        def _(pool):
            def finish(p, b):
                back.rstd(pool, consts, p, b)
                pool.wait_ge(back.zn_done, 2 * p + b + 1)
                pool.wait_ge(xres_loaded[b], 16 * (p + 1))
                pool.tensor_tensor(back.z[b][:, :, :], back.z[b][:, :, :], xres[b][:, :, :],
                                   ALU.add).then_inc(back.added, 1)

            for b in range(2):
                front.rstd(pool, consts, 0, b)

            def body(p, first, last):
                if not first:
                    finish(p - 1, 1)
                for b in range(2):
                    pool.wait_ge(front.loaded[b], 16 * (p + 1))
                    back.z_free(pool, p, b)
                    pool.wait_ge(front.xn_done, 2 * p + b + 1)
                    pool.tensor_tensor(back.z[b][:, :, :], front.x[b][:, :, :],
                                       b2row[:, :].unsqueeze(1).broadcast_to([P, TT, D]), ALU.add).then_inc(moved, 1)
                if not last:
                    for b in range(2):
                        front.rstd(pool, consts, p + 1, b)
                finish(p, 0)

            passes(pool, body)
            finish(PAIRSOF - 1, 1)

        @block.scalar
        def _(act):
            def take(p, l, b):
                n = 3 * p + l
                if l == 0:
                    act.wait_ge(front.turned, 2 * p + b + 1)
                    banks = pT
                else:
                    act.wait_ge(hid.used, FT * (6 * p + 2 * (l - 1) + b + 1))
                    banks = pH
                wait(act, hlo_done[b], n)
                for h in range(DH):
                    if l == 0:
                        last_ = act.activation(hf[b][:, h, :], banks[h][:, :], ACT.Identity,
                                               bias=gb[:, 1, h:h + 1], scale=gb[:, 0, h:h + 1])
                    else:
                        last_ = act.activation(hf[b][:, h, :], banks[h][:, :], ACT.Identity,
                                               bias=b2[:, l - 1, h:h + 1])
                last_.then_inc(hf_done[b], 1)

            def high(p, l, b):
                n = 3 * p + l
                act.wait_ge(hf_done[b], n + 1)
                wait(act, hid.mm, FT * (2 * (3 * p + l - 1) + b + 1))
                act.activation(hp[b][0][:, :, :], hf[b][:, :, :], ACT.Identity).then_inc(hhi_done[b], 1)

            def body(p, first, last):
                if first:
                    take(0, 0, 0)
                    high(0, 0, 0)
                for o, l, b in order(p):
                    prev = (l, 0) if b else (l - 1, 1)
                    moves = prev[0] in range(LEVELS - 1)
                    if moves:
                        take(p, prev[0] + 1, prev[1])
                    for f in range(FT):
                        hid.gelu(act, FT * o + f, f, b1[:, l, f:f + 1])
                        hid.high(act, FT * o + f, f)
                        if f == 0 and moves:
                            high(p, prev[0] + 1, prev[1])
                        if f == 1 and (l, b) == (0, 0):
                            take(p, 0, 1)
                            high(p, 0, 1)
                        if f == 1 and (l, b) == (LEVELS - 1, 1) and not last:
                            take(p + 1, 0, 0)
                            high(p + 1, 0, 0)

            passes(act, body)

        @block.vector
        def _(dve):
            def halves(p, l, b):
                n = 3 * p + l
                dve.wait_ge(hf_done[b], n + 1)
                dve.wait_ge(hhi_done[b], n + 1)
                wait(dve, hid.mm, FT * (2 * (3 * p + l - 1) + b + 1))
                dve.tensor_tensor(hp[b][1][:, :, :], hf[b][:, :, :], hp[b][0][:, :, :].bitcast(F32),
                                  ALU.subtract).then_inc(hlo_done[b], 1)

            def out(p, b):
                dve.wait_ge(hid.used, FT * (6 * p + 4 + b + 1))
                dve.wait_ge(moved, 2 * p + b + 1)
                for h in range(2):
                    zz = back.z[b][:, 2 * h:2 * h + 2, :]
                    last_ = dve.tensor_tensor(zz, pH[h][:, :].rearrange("p (a b) -> p a b", a=2), zz, ALU.add)
                last_.then_inc(z_done, 1)

            def body(p, first, last):
                if first:
                    for b in range(2):
                        front.stats(dve, 0, b)
                        front.norm(dve, 0, b)
                    halves(0, 0, 0)
                for o, l, b in order(p):
                    prev = (l, 0) if b else (l - 1, 1)
                    ends = None
                    if (l, b) == (0, 0) and not first:
                        ends = (p - 1, 1)
                    if (l, b) == (LEVELS - 1, 1):
                        ends = (p, 0)
                    if ends:
                        out(*ends)
                    for f in range(FT):
                        hid.low(dve, FT * o + f, f)
                        if f == 0 and prev[0] in range(LEVELS - 1):
                            halves(p, prev[0] + 1, prev[1])
                        if f == 1 and ends:
                            back.stats(dve, z_done, 2 * ends[0] + ends[1] + 1, *ends)
                        if f == 2 and (l, b) == (0, 0):
                            halves(p, 0, 1)
                        if f == 2 and (l, b) == (LEVELS - 1, 1) and not last:
                            halves(p + 1, 0, 0)
                        if f == 4 and ends:
                            back.norm(dve, *ends)
                        if l == 1 and f == 2 and not last:
                            front.stats(dve, p + 1, b)
                        if l == 1 and f == 5 and not last:
                            front.norm(dve, p + 1, b)

            passes(dve, body)
            out(PAIRSOF - 1, 1)
            back.stats(dve, z_done, 2 * PAIRSOF, PAIRSOF - 1, 1)
            back.norm(dve, PAIRSOF - 1, 1)

        @block.tensor
        def _(pe):
            LAG = 3

            def body(p, first, last):
                if first:
                    front.turn(pe, pT, 0, 0)
                    pe.wait_ge(hf_done[0], 1)
                    front.turn(pe, pT, 0, 1)
                for o, l, b in order(p):
                    for f in range(FT + LAG):
                        if f == 4 and l == LEVELS - 1 and not last:
                            if b == 0:
                                pe.wait_ge(hf_done[1], 3 * p + 1)
                            else:
                                pe.wait_ge(hf_done[0], 3 * (p + 1) + 1)
                            front.turn(pe, pT, p + 1, b)
                        if f < FT:
                            waits = [(hf_done[b], 3 * p + l + 1), (hlo_done[b], 3 * p + l + 1)] if f == 0 else []
                            hid.up(pe, FT * o + f, f, w1[l], hp[b], waits)
                        g = f - LAG
                        if g == 0:
                            if (l, b) == (0, 0):
                                wait(pe, z_done, 2 * p)
                            elif (l, b) == (LEVELS - 1, 1):
                                pe.wait_ge(z_done, 2 * p + 1)
                            elif b == 1:
                                pe.wait_ge(hf_done[0], 3 * p + l + 2)
                            else:
                                pe.wait_ge(hf_done[1], 3 * p + l + 1)
                        if g >= 0:
                            if l < LEVELS - 1:
                                hid.down(pe, FT * o + g, g, w2[l], pH)
                            else:
                                hid.down_tokens(pe, FT * o + g, g, w2[l], pH)

            passes(pe, body)


EXPERTS = 8
GROUP = P // EXPERTS
GROUPS = 2 * D * HID // (GROUP * HID)


def expert_weights(nc, x_dram, consts, shared, mw_dram, tw_d, base_d, gw1_d, gb1_d, gw2_d, gb2_d, esel_d,
                   delta_d, spread_d, tb1_d, b1_d, tb2_d, b2_d):
    mb1, mb2 = shared
    with ExitStack() as ctx:
        ph = Phase(nc, ctx, "eg")
        gw1 = ph.sb("gw1", [P, DH, D])
        gb1 = ph.sb("gb1", [P, DH])
        gw2 = ph.sb("gw2", [P, DH, EXPERTS])
        gb2 = ph.sb("gb2", [EXPERTS, 1])
        esel = ph.sb("esel", [EXPERTS, P])
        delta = ph.sb("delta", [P, GROUP])
        spread = ph.sb("spread", [GROUP, P])
        tb1 = ph.sb("tb1", [EXPERTS, HID])
        b1 = ph.sb("b1", [P, FT])
        tb2 = ph.sb("tb2", [EXPERTS, D])
        b2 = ph.sb("b2", [1, D])
        hsum = ph.sb("hsum", [P, NBLK, DH])
        mix = ph.sb("mix", [P, BATCH, GROUP])
        load_weights(nc, "egl", [
            (gw1[:, :, :].rearrange("p a b -> p (a b)"), gw1_d), (gb1[:, :], gb1_d),
            (gw2[:, :, :].rearrange("p a b -> p (a b)"), gw2_d), (gb2[:, :], gb2_d), (esel[:, :], esel_d),
            (delta[:, :], delta_d), (spread[:, :], spread_d), (tb1[:, :], tb1_d), (b1[:, :], b1_d),
            (tb2[:, :], tb2_d), (b2[:, :], b2_d)], [])

        with ExitStack() as inner:
            gp = Phase(nc, inner, "g1")
            front = Front(gp, x_dram, consts["ident"])
            xT = [gp.sb(f"xT{b}", [P, DH, BLK]) for b in range(2)]
            junk = [gp.sb(f"junk{n}", [P, BLK]) for n in range(2 * DH)]
            accs = [gp.sb(f"acc{b}", [P, DH]) for b in range(2)]
            pT = [gp.ps(f"pT{h}", [P, BLK]) for h in range(DH)]
            pG = [gp.ps(f"pG{h}", [P, BLK]) for h in range(2 * DH)]
            xT_done, g_mm, summed, kept = gp.sem("xT"), gp.sem("g_mm"), gp.sem("summed"), gp.sem("kept")
            block = inner.enter_context(nc.Block())

            @block.sync
            def _(sp):
                front.load(sp, 0, 0)
                front.load(sp, 0, 1)

                def body(p, par, first, last):
                    if not (isinstance(p, int) and p == NBLK // 2 - 1):
                        sp.wait_ge(front.xn_done, 2 * p + par + 1)
                        front.load(sp, p + 1, par)

                rounds(sp, NBLK, body)

            @block.gpsimd
            def _(pool):
                rounds(pool, NBLK, lambda p, par, first, last: front.rstd(pool, consts, p, par))

            @block.scalar
            def _(act):
                def take(p, par):
                    i = 2 * p + par
                    act.wait_ge(front.turned, i + 1)
                    wait(act, g_mm, i - 1)
                    for h in range(DH):
                        last_ = act.activation(xT[par][:, h, :], pT[h][:, :], ACT.Identity)
                    last_.then_inc(xT_done, 1)

                take(0, 0)

                def body(p, par, first, last):
                    i = 2 * p + par
                    if not last:
                        take(*after(p, par))
                    act.wait_ge(g_mm, i + 1)
                    wait(act, kept, i - 1)
                    for h in range(DH):
                        last_ = act.activation(junk[DH * par + h][:, :], pG[DH * par + h][:, :], ACT.Relu, bias=gb1[:, h:h + 1],
                                               accum_out=accs[par][:, h:h + 1])
                    last_.then_inc(summed, 1)

                rounds(act, NBLK, body)

            @block.vector
            def _(dve):
                front.stats(dve, 0, 0)
                front.norm(dve, 0, 0)

                def body(p, par, first, last):
                    i = 2 * p + par
                    if not last:
                        front.stats(dve, *after(p, par))
                        front.norm(dve, *after(p, par))
                    dve.wait_ge(summed, i + 1)
                    dve.tensor_copy(hsum[:, bass.ds(i, 1), :], accs[par][:, :].unsqueeze(1)).then_inc(kept, 1)

                rounds(dve, NBLK, body)

            @block.tensor
            def _(pe):
                front.turn(pe, pT, 0, 0)

                def body(p, par, first, last):
                    i = 2 * p + par
                    pe.wait_ge(xT_done, i + 1)
                    if not last:
                        front.turn(pe, pT, *after(p, par))
                    wait(pe, summed, i - 1)
                    for m in range(DH):
                        for k in range(DH):
                            mm = pe.matmul(pG[DH * par + m][:, :], gw1[:, k, m * P:(m + 1) * P], xT[par][:, k, :],
                                           start=k == 0, stop=k == DH - 1)
                    mm.then_inc(g_mm, 1)

                rounds(pe, NBLK, body)

        with ExitStack() as inner:
            gp = Phase(nc, inner, "g2")
            hm = gp.sb("hm", [P, DH, BATCH])
            gT = gp.sb("gT", [EXPERTS, BATCH])
            gP = gp.sb("gP", [P, BATCH])
            gB = gp.sb("gB", [EXPERTS, BATCH, P])
            ones = gp.sb("ones", [EXPERTS, P])
            pg = gp.ps("pg", [P, BATCH])
            pe_ = gp.ps("pe", [P, BATCH])
            pb = gp.ps("pb", [P, FT, BATCH])
            pc = [gp.ps(f"pc{n}", [P, 2, D]) for n in range(BATCH // 2)]
            v, t = gp.sem("v"), gp.sem("t")
            block = inner.enter_context(nc.Block())

            @block.vector
            def _(dve):
                dve.memset(ones[:, :], 1.0).then_inc(v, 1)
                pairs = hsum[:, :, :].rearrange("p (b two) h -> p h b two", two=SEQ // BLK)
                dve.tensor_tensor(hm[:, :, :], pairs[:, :, :, 0], pairs[:, :, :, 1], ALU.add).then_inc(v, 1)
                dve.wait_ge(t, 1)
                dve.tensor_scalar(gT[:, :], pg[0:EXPERTS, :], 1.0 / SEQ, gb2[:, 0:1], ALU.mult,
                                  ALU.add).then_inc(v, 1)
                dve.wait_ge(v, 3)
                for b in range(BATCH):
                    last = dve.tensor_scalar(gB[:, b, :], ones[:, :], gT[:, b:b + 1], None, ALU.mult)
                last.then_inc(v, 1)
                dve.wait_ge(t, 2)
                dve.tensor_copy(gP[:, :], pe_[:, :]).then_inc(v, 1)
                dve.wait_ge(v, 5)
                for b in range(BATCH):
                    last = dve.tensor_scalar(mix[:, b, :], delta[:, :], gP[:, b:b + 1], None, ALU.mult)
                last.then_inc(v, 1)
                dve.wait_ge(t, 3)
                dve.tensor_tensor(mb1[:, :, :], pb[:, :, :].rearrange("p f b -> p b f"),
                                  b1[:, :].unsqueeze(1).broadcast_to([P, BATCH, FT]), ALU.add).then_inc(v, 1)
                dve.wait_ge(t, 4)
                for n in range(BATCH // 2):
                    last = dve.tensor_copy(mb2[:, 2 * n:2 * n + 2, :], pc[n][:, :, :])
                last.then_inc(v, 1)

            @block.tensor
            def _(pe):
                pe.wait_ge(v, 2)
                for h in range(DH):
                    mm = pe.matmul(pg[0:EXPERTS, :], gw2[:, h, :], hm[:, h, :], start=h == 0, stop=h == DH - 1)
                mm.then_inc(t, 1)
                pe.wait_ge(v, 3)
                pe.matmul(pe_[:, :], esel[:, :], gT[:, :], start=True, stop=True).then_inc(t, 1)
                for f in range(FT):
                    mm = pe.matmul(pb[:, f, :], tb1[:, f * P:(f + 1) * P], gT[:, :], start=True, stop=True)
                mm.then_inc(t, 1)
                pe.wait_ge(v, 4)
                for b in range(BATCH):
                    out = pc[b // 2][:, b % 2, :]
                    pe.matmul(out, gB[:, b, :], tb2[:, :], start=True, stop=False)
                    mm = pe.matmul(out, ones[0:1, :], b2[:, :], start=False, stop=True)
                mm.then_inc(t, 1)

        with ExitStack() as inner:
            gp = Phase(nc, inner, "g3")
            tw = [gp.sb(f"tw{b}", [P, HID]) for b in range(2)]
            base = [gp.sb(f"base{b}", [GROUP, HID]) for b in range(2)]
            mw = [gp.sb(f"mw{b}", [P, HID]) for b in range(2)]
            pw = [gp.ps(f"pw{n}", [P, BLK]) for n in range(4)]
            loaded = [gp.sem(f"loaded{b}") for b in range(2)]
            stored = [gp.sem(f"stored{b}") for b in range(2)]
            mm_done, ev_act, ev_dve = gp.sem("mm"), gp.sem("ev_act"), gp.sem("ev_dve")
            block = inner.enter_context(nc.Block())

            @block.sync
            def _(sp):
                def body(p, par, first, last):
                    i = 2 * p + par
                    wait(sp, mm_done, i - 1)
                    sp.dma_start(tw[par][:, :], tw_d[bass.ds(i * P, P), :]).then_inc(loaded[par], 16)
                    sp.dma_start(base[par][:, :], base_d[bass.ds(i * GROUP, GROUP), :]).then_inc(loaded[par], 16)

                rounds(sp, GROUPS, body)

            @block.gpsimd
            def _(pool):
                def body(p, par, first, last):
                    i = 2 * p + par
                    pool.wait_ge(ev_act, i + 1)
                    pool.wait_ge(ev_dve, i + 1)
                    dst = mw_dram[:, bass.ds(i * GROUP, GROUP), :]
                    pool.dma_start(dst, mw[par][:, :]).then_inc(stored[par], 16)

                rounds(pool, GROUPS, body)
                for s in stored:
                    pool.wait_ge(s, 16 * GROUPS // 2)

            @block.scalar
            def _(act):
                def body(p, par, first, last):
                    i = 2 * p + par
                    act.wait_ge(mm_done, i + 1)
                    wait(act, stored[par], 16 * p)
                    act.activation(mw[par][:, 0:BLK], pw[2 * par][:, :], ACT.Identity).then_inc(ev_act, 1)

                rounds(act, GROUPS, body)

            @block.vector
            def _(dve):
                def body(p, par, first, last):
                    i = 2 * p + par
                    dve.wait_ge(mm_done, i + 1)
                    wait(dve, stored[par], 16 * p)
                    dve.tensor_copy(mw[par][:, BLK:HID], pw[2 * par + 1][:, :]).then_inc(ev_dve, 1)

                rounds(dve, GROUPS, body)

            @block.tensor
            def _(pe):
                def body(p, par, first, last):
                    i = 2 * p + par
                    pe.wait_ge(loaded[par], 32 * (p + 1))
                    wait(pe, ev_act, i - 1)
                    wait(pe, ev_dve, i - 1)
                    for n in range(2):
                        ns = slice(n * BLK, (n + 1) * BLK)
                        pe.matmul(pw[2 * par + n][:, :], mix[:, :, :].rearrange("p b h -> p (b h)"),
                                  tw[par][:, ns], start=True, stop=False)
                        mm = pe.matmul(pw[2 * par + n][:, :], spread[:, :], base[par][:, ns], start=False, stop=True)
                    mm.then_inc(mm_done, 1)

                rounds(pe, GROUPS, body)


def batch_mlp(nc, x_dram, y_dram, consts, shared, mw_dram):
    mb1, mb2 = shared
    with ExitStack() as ctx:
        ph = Phase(nc, ctx, "bm")
        front = Front(ph, x_dram, consts["ident"])
        back = Back(ph, front, y_dram)
        xres = [ph.sb(f"xres{b}", [P, TT, D]) for b in range(2)]
        hf = [ph.sb(f"hf{b}", [P, DH, BLK]) for b in range(2)]
        hp = [ph.pair(f"hp{b}", [P, DH, BLK]) for b in range(2)]
        raw = ph.sb("raw", [P, 4, HID])
        w1 = [ph.pair(f"w1{b}", [P, DH, HID]) for b in range(2)]
        w2 = [ph.pair(f"w2{b}", [P, FT, D]) for b in range(2)]
        hid = Hidden(ph)
        pT = [ph.ps(f"pT{h}", [P, BLK]) for h in range(DH)]
        pH = [ph.ps(f"pH{h}", [P, BLK]) for h in range(DH)]
        raw_loaded = ph.sem("raw_loaded")
        whi_done, wlo_done = ph.sem("whi"), ph.sem("wlo")
        kept = ph.sem("kept")
        bias = [ph.sb(f"bias{b}", [P, FT]) for b in range(2)]
        bias_done = ph.sem("bias")
        hf_done, hhi_done, hlo_done = ph.sem("hf"), ph.sem("hhi"), ph.sem("hlo")
        z_done = ph.sem("z")
        block = ctx.enter_context(nc.Block())
        PER = SEQ // BLK
        Q = 2 * PER
        PASSES = NBLK // Q

        def passes(eng, body):
            body(0, True, False)
            with eng.Fori(1, PASSES - 1) as p:
                body(p, False, False)
            body(PASSES - 1, False, True)

        def at(p, q):
            return 2 * p + q // 2, q % 2

        def pieces(b):
            out = []
            for h in range(DH):
                out.append(tuple(x[:, h, :] for x in w1[b]))
            for h in range(2):
                out.append(tuple(x[:, h * 4:(h + 1) * 4, :].rearrange("p a b -> p (a b)") for x in w2[b]))
            return out

        @block.sync
        def _(sp):
            def load_w(b):
                src = mw_dram[b, 0:D, :].rearrange("(k p) n -> p k n", p=P)
                sp.dma_start(raw[:, 0:2, :], src).then_inc(raw_loaded, 16)
                src = mw_dram[b, D:2 * D, :].rearrange("r (q d) -> (r q) d", d=D)
                src = src.rearrange("(f p) d -> p f d", p=P)
                dst = raw[:, 2:4, :].rearrange("p a (f d) -> p (a f) d", d=D)
                sp.dma_start(dst, src).then_inc(raw_loaded, 16)

            load_w(0)
            front.load(sp, 0, 0)
            front.load(sp, 0, 1)

            def body(p, first, last):
                for q in range(Q):
                    i = Q * p + q
                    if q % PER == 0 and not (last and q == PER):
                        sp.wait_ge(wlo_done, 4 * (2 * p + q // PER + 1))
                        load_w(2 * p + q // PER + 1)
                    if not (last and q >= Q - 2):
                        sp.wait_ge(kept, i + 1)
                        sp.wait_ge(front.xn_done, i + 1)
                        front.load(sp, at(p, q)[0] + 1, q % 2)
                    if not (first and q == 0):
                        back.store(sp, *before(*at(p, q)))

            passes(sp, body)
            back.store(sp, NBLK // 2 - 1, 1)
            back.all_stored(sp)

        @block.gpsimd
        def _(pool):
            front.rstd(pool, consts, 0, 0)
            front.rstd(pool, consts, 0, 1)

            def finish(pp, par):
                back.rstd(pool, consts, pp, par)
                pool.wait_ge(back.zn_done, 2 * pp + par + 1)
                pool.tensor_tensor(back.z[par][:, :, :], back.z[par][:, :, :], xres[par][:, :, :],
                                   ALU.add).then_inc(back.added, 1)

            def body(p, first, last):
                for q in range(Q):
                    i = Q * p + q
                    pp, par = at(p, q)
                    pool.wait_ge(front.loaded[par], 16 * (pp + 1))
                    wait(pool, back.added, i - 1)
                    pool.tensor_tensor(xres[par][:, :, :], front.x[par][:, :, :],
                                       consts["one"].unsqueeze(2).broadcast_to([P, TT, D]), ALU.mult).then_inc(kept, 1)
                    if not (first and q == 0):
                        finish(*before(pp, par))
                    if not (last and q >= Q - 2):
                        front.rstd(pool, consts, pp + 1, par)

            passes(pool, body)
            finish(NBLK // 2 - 1, 1)

        @block.scalar
        def _(act):
            def take(i, par):
                act.wait_ge(front.turned, i + 1)
                wait(act, hlo_done, i - 1)
                for h in range(DH):
                    last_ = act.activation(hf[par][:, h, :], pT[h][:, :], ACT.Identity)
                last_.then_inc(hf_done, 1)
                act.wait_ge(hf_done, i + 1)
                wait(act, hid.mm, FT * (i - 1))
                act.activation(hp[par][0][:, :, :], hf[par][:, :, :], ACT.Identity).then_inc(hhi_done, 1)

            def piece(batch, b, k):
                if k == 0:
                    act.wait_ge(raw_loaded, 32 * (batch + 1))
                    wait(act, hid.used, FT * PER * (batch - 1))
                act.activation(pieces(b)[k][0], raw[:, k, :], ACT.Identity).then_inc(whi_done, 1)

            for k in range(4):
                piece(0, 0, k)
            take(0, 0)

            def body(p, first, last):
                for q in range(Q):
                    i = Q * p + q
                    batch = 2 * p + q // PER
                    for f in range(FT):
                        if f == 0 and q % PER == 0:
                            act.wait_ge(bias_done, batch + 1)
                        hid.gelu(act, FT * i + f, f, bias[q // PER][:, f:f + 1])
                        hid.high(act, FT * i + f, f)
                        if f < 4 and q % PER == PER - 1 and not (last and q == Q - 1):
                            piece(batch + 1, (q // PER + 1) % 2, f)
                        if f == 5 and not (last and q == Q - 1):
                            take(i + 1, (q + 1) % 2)

            passes(act, body)

        @block.vector
        def _(dve):
            def halves(i, par):
                dve.wait_ge(hf_done, i + 1)
                dve.wait_ge(hhi_done, i + 1)
                wait(dve, hid.mm, FT * (i - 1))
                dve.tensor_tensor(hp[par][1][:, :, :], hf[par][:, :, :], hp[par][0][:, :, :].bitcast(F32),
                                  ALU.subtract).then_inc(hlo_done, 1)

            def piece(batch, b, k):
                dve.wait_ge(whi_done, 4 * batch + k + 1)
                if k == 0:
                    wait(dve, hid.used, FT * PER * (batch - 1))
                hi, lo = pieces(b)[k]
                dve.tensor_tensor(lo, raw[:, k, :], hi.bitcast(F32), ALU.subtract).then_inc(wlo_done, 1)

            def hidden_bias(batch, b):
                wait(dve, hid.g_done, FT * PER * (batch - 1))
                src = mb1[:, bass.ds(batch, 1), :].rearrange("p a f -> p (a f)")
                dve.tensor_tensor(bias[b][:, :], src, src, ALU.max).then_inc(bias_done, 1)

            def out(i, pp, par, batch):
                dve.wait_ge(hid.used, FT * (i + 1))
                back.z_free(dve, pp, par)
                for h in range(2):
                    bias = mb2[:, bass.ds(batch, 1), :] if not isinstance(batch, int) else mb2[:, batch:batch + 1, :]
                    last_ = dve.tensor_tensor(back.z[par][:, 2 * h:2 * h + 2, :],
                                              pH[h][:, :].rearrange("p (a b) -> p a b", a=2),
                                              bias.broadcast_to([P, 2, D]), ALU.add)
                last_.then_inc(z_done, 1)

            hidden_bias(0, 0)
            for k in range(4):
                piece(0, 0, k)
            for b in range(2):
                front.stats(dve, 0, b)
                front.norm(dve, 0, b)
            halves(0, 0)

            def body(p, first, last):
                for q in range(Q):
                    i = Q * p + q
                    pp, par = at(p, q)
                    ends = None if first and q == 0 else before(pp, par)
                    if q % PER == PER - 1 and not (last and q == Q - 1):
                        hidden_bias(2 * p + q // PER + 1, (q // PER + 1) % 2)
                    if ends:
                        out(i - 1, *ends, 2 * p + (q - 1) // PER)
                    for f in range(FT):
                        hid.low(dve, FT * i + f, f)
                        if f < 4 and q % PER == PER - 1 and not (last and q == Q - 1):
                            piece(2 * p + q // PER + 1, (q // PER + 1) % 2, f)
                        if f == 1 and ends:
                            back.stats(dve, z_done, i, *ends)
                        if f == 4 and ends:
                            back.norm(dve, *ends)
                        if f == 5 and not (last and q == Q - 1):
                            halves(i + 1, (q + 1) % 2)
                        if not (last and q >= Q - 2):
                            if f == 3:
                                front.stats(dve, pp + 1, par)
                            if f == 6:
                                front.norm(dve, pp + 1, par)

            passes(dve, body)
            out(NBLK - 1, NBLK // 2 - 1, 1, BATCH - 1)
            back.stats(dve, z_done, NBLK, NBLK // 2 - 1, 1)
            back.norm(dve, NBLK // 2 - 1, 1)

        @block.tensor
        def _(pe):
            LAG = 3

            front.turn(pe, pT, 0, 0)

            def body(p, first, last):
                for q in range(Q):
                    i = Q * p + q
                    b = q // PER
                    for f in range(FT + LAG):
                        if f == 3 and not (last and q == Q - 1):
                            pe.wait_ge(hf_done, i + 1)
                            front.turn(pe, pT, *after(*at(p, q)))
                        if f < FT:
                            waits = [(hlo_done, i + 1), (wlo_done, 4 * (2 * p + b + 1))] if f == 0 else []
                            hid.up(pe, FT * i + f, f, w1[b], hp[q % 2], waits)
                        g = f - LAG
                        if g == 0:
                            wait(pe, z_done, i)
                        if g >= 0:
                            hid.down_tokens(pe, FT * i + g, g, w2[b], pH)

            passes(pe, body)


FILT = 64
EMB = 3
INNER = 3 * D
HALF = SEQ // 2
KT = HALF // P
IT = INNER // P
TWO_PI = 2 * np.pi
ROUND = 1.5 * 2.0 ** 23


def two_pi_parts():
    a = np.float32(6.28125)
    b = np.float32(round((TWO_PI - float(a)) * 2 ** 20) / 2 ** 20)
    return float(a), float(b), float(np.float32(TWO_PI - float(a) - float(b)))


def long_filter(nc, consts, shared, z_d, t_d, decay_d, w1_d, w2_d, w3_d, wo_d, b_d, freq_d, fb_d, half_d):
    cos_m, sin_m, ks = shared
    with ExitStack() as ctx:
        ph = Phase(nc, ctx, "lf")
        z = ph.sb("z", [EMB, SEQ])
        tcol = ph.sb("tcol", [P, KT, 2])
        dec = ph.sb("dec", [P, D])
        ws = [ph.sb("w1", [EMB, FILT]), ph.sb("w2", [FILT, FILT]), ph.sb("w3", [FILT, FILT])]
        wo = ph.sb("wo", [FILT, D])
        bs = ph.sb("bs", [FILT, 3])
        freq = ph.sb("freq", [FILT, 1])
        fb = ph.sb("fb", [1, D])
        hc = ph.sb("hc", [P, 3, KT])
        load_weights(nc, "lfl", [
            (z[:, :], z_d), (tcol[:, :, :].rearrange("p a b -> p (a b)"), t_d),
            (dec[:, :], decay_d.unsqueeze(0).broadcast_to([P, D])), (ws[0][:, :], w1_d), (ws[1][:, :], w2_d),
            (ws[2][:, :], w3_d), (wo[:, :], wo_d), (bs[:, :], b_d), (freq[:, :], freq_d), (fb[:, :], fb_d),
            (hc[:, :, :].rearrange("p a b -> p (a b)"), half_d)], [])
        h = [ph.sb(f"h{n}", [FILT, SEQ]) for n in range(3)]
        a, n, r = (ph.sb(x, [FILT, SEQ]) for x in "anr")
        env = ph.sb("env", [P, KT, 2, D])
        kf = ph.sb("kf", [P, KT, 2, D])
        kp = ph.pair("kp", [P, KT, 2, D])
        t1 = ph.sb("t1", [P, KT, 5, D])
        ph_ = [ph.ps(f"ph{x}", [P, HALF]) for x in range(2)]
        pk = [ph.ps(f"pk{x}", [P, 2, D]) for x in range(2)]
        pf = [ph.ps(f"pf{x}", [P, 2, D]) for x in range(4)]
        v, v3, s, t = ph.sem("v"), ph.sem("v3"), ph.sem("s"), ph.sem("t")
        block = ctx.enter_context(nc.Block())
        LAYER = 8

        @block.tensor
        def _(pe):
            for l in range(3):
                src = z if l == 0 else h[l - 1]
                if l:
                    pe.wait_ge(s, l)
                for c in range(2):
                    mm = pe.matmul(ph_[c][0:FILT, :], ws[l][:, :], src[:, c * HALF:(c + 1) * HALF],
                                   start=True, stop=True)
                mm.then_inc(t, 1)
            pe.wait_ge(s, 3)
            samples = h[2][:, :].rearrange("p (k s r) -> p k r s", k=KT, r=2)
            for k in range(KT):
                if k >= 2:
                    pe.wait_ge(v, 3 * LAYER + k - 1)
                for q in range(2):
                    mm = pe.matmul(pk[k % 2][:, q, :], samples[:, k, q, :], wo[:, :], start=True, stop=True)
                mm.then_inc(t, 1)
            pe.wait_ge(v, 3 * LAYER + KT + 2)
            for k in range(KT):
                if k >= 2:
                    pe.wait_ge(v, 3 * LAYER + KT + 2 + 3 * (k - 1))
                for x, m in enumerate((cos_m, sin_m)):
                    for q in range(KT):
                        out = pf[2 * (k % 2) + x][:, :, :].rearrange("p a b -> p (a b)")
                        mm = three_pass(pe, out, tuple(w[:, q, k * P:(k + 1) * P] for w in m),
                                        tuple(w[:, q, :, :].rearrange("p a b -> p (a b)") for w in kp),
                                        q == 0, q == KT - 1)
                mm.then_inc(t, 1)

        @block.scalar
        def _(act):
            for l in range(3):
                act.wait_ge(v, LAYER * (l + 1))
                act.activation(h[l][:, :], r[:, :], ACT.Sin).then_inc(s, 1)
            for k in range(KT):
                for q in range(2):
                    last = act.activation(env[:, k, q, :], dec[:, :], ACT.Exp, scale=tcol[:, k, q:q + 1])
            last.then_inc(s, 1)
            act.wait_ge(v, 3 * LAYER + KT + 1)
            act.activation(kp[0][:, :, :, :], kf[:, :, :, :], ACT.Identity).then_inc(s, 1)

        @block.vector
        def _(dve):
            p1, p2, p3 = two_pi_parts()
            count = [0]

            def step(ins):
                count[0] += 1
                ins.then_inc(v, 1)
                dve.wait_ge(v, count[0])

            for l in range(3):
                dve.wait_ge(t, l + 1)
                if l:
                    dve.wait_ge(s, l)
                for c in range(2):
                    cs = slice(c * HALF, (c + 1) * HALF)
                    step(dve.tensor_scalar(a[:, cs], ph_[c][0:FILT, :], bs[:, l:l + 1], freq[:, 0:1], ALU.add, ALU.mult))
                step(dve.tensor_scalar(n[:, :], a[:, :], 1 / TWO_PI, ROUND, ALU.mult, ALU.add))
                step(dve.tensor_scalar(n[:, :], n[:, :], ROUND, None, ALU.subtract))
                step(dve.scalar_tensor_tensor(a[:, :], n[:, :], -p1, a[:, :], ALU.mult, ALU.add))
                step(dve.scalar_tensor_tensor(a[:, :], n[:, :], -p2, a[:, :], ALU.mult, ALU.add))
                step(dve.scalar_tensor_tensor(r[:, :], n[:, :], -p3, a[:, :], ALU.mult, ALU.add))
                step(dve.tensor_scalar(r[:, :], r[:, :], 3.1415925, -3.1415925, ALU.min, ALU.max))
            dve.wait_ge(s, 4)
            for k in range(KT):
                dve.wait_ge(t, 3 + k + 1)
                step(dve.tensor_tensor(kf[:, k, :, :], pk[k % 2][:, :, :], env[:, k, :, :], ALU.mult))
            step(dve.tensor_tensor(kf[0:1, 0, 0, :], kf[0:1, 0, 0, :], fb[:, :], ALU.add))
            dve.wait_ge(s, 5)
            step(dve.tensor_tensor(kp[1][:, :, :, :], kf[:, :, :, :], kp[0][:, :, :, :].bitcast(F32), ALU.subtract))
            for k in range(KT):
                dve.wait_ge(t, 3 + KT + k + 1)
                re, im = pf[2 * (k % 2)], pf[2 * (k % 2) + 1]
                c_, s_, ms = (hc[:, x, k:k + 1] for x in range(3))
                dve.tensor_scalar(t1[:, k, 0, :], re[:, 0, :], ms, None, ALU.mult)
                dve.tensor_scalar(t1[:, k, 1, :], im[:, 0, :], s_, None, ALU.mult)
                dve.tensor_scalar(t1[:, k, 2, :], re[:, 1, :], s_, None, ALU.mult)
                dve.tensor_scalar(t1[:, k, 3, :], im[:, 1, :], s_, None, ALU.mult)
                step(dve.tensor_scalar(t1[:, k, 4, :], im[:, 1, :], ms, None, ALU.mult))
                stt = dve.scalar_tensor_tensor
                stt(ks[:, k, 0, 1, :], re[:, 0, :], c_, t1[:, k, 1, :], ALU.mult, ALU.add)
                stt(ks[:, k, 1, 1, :], im[:, 0, :], c_, t1[:, k, 0, :], ALU.mult, ALU.add)
                stt(ks[:, k, 0, 2, :], re[:, 1, :], c_, t1[:, k, 4, :], ALU.mult, ALU.add)
                stt(ks[:, k, 1, 2, :], im[:, 1, :], c_, t1[:, k, 2, :], ALU.mult, ALU.add)
                step(stt(ks[:, k, 0, 0, :], re[:, 1, :], c_, t1[:, k, 3, :], ALU.mult, ALU.add))
                dve.tensor_scalar(t1[:, k, 2, :], re[:, 1, :], ms, None, ALU.mult).then_inc(v3, 1)
                dve.wait_ge(v3, k + 1)
                step(stt(ks[:, k, 1, 0, :], im[:, 1, :], c_, t1[:, k, 2, :], ALU.mult, ALU.add))


def hyena(nc, x_dram, y_dram, consts, cos_d, sin_d, filter_args, in_w, in_b, sw_d, sb_d, out_w, outb_d):
    with ExitStack() as ctx:
        ph = Phase(nc, ctx, "hy")
        cos_m = ph.pair("cos", [P, KT, HALF])
        sin_m = ph.pair("sin", [P, KT, HALF])
        ks = ph.sb("ks", [P, KT, 2, 3, D])
        flat = lambda t: tuple(x[:, :, :].rearrange("p a b -> p (a b)") for x in t)
        load_weights(nc, "hym", [], [(flat(cos_m), cos_d), (flat(sin_m), sin_d)])
        long_filter(nc, consts, (cos_m, sin_m, ks), *filter_args)
        wi = ph.pair("wi", [P, DH, INNER])
        wo = ph.pair("wo", [P, DH, D])
        inb = ph.sb("inb", [P, IT])
        sw = ph.sb("sw", [P, 3, IT])
        sbias = ph.sb("sbias", [P, IT])
        outb = ph.sb("outb", [P, D])
        load_weights(nc, "hyl",
                     [(inb[:, :], in_b), (sw[:, :, :].rearrange("p a b -> p (a b)"), sw_d), (sbias[:, :], sb_d),
                      (outb[:, :], outb_d.unsqueeze(0).broadcast_to([P, D]))],
                     [(flat(wi), in_w), (flat(wo), out_w)], chunk=1536)
        front = Front(ph, x_dram, consts["ident"], in_place=True)
        xres = ph.sb("xres", [P, 2 * TT, D])
        hp = [ph.pair(f"hp{b}", [P, DH, BLK]) for b in range(2)]
        up = [ph.sb(f"up{b}", [P, SEQ + 2]) for b in range(2)]
        acc = ph.sb("acc", [P, SEQ])
        x1 = ph.sb("x1", [P, SEQ])
        x0 = ph.sb("x0", [P, DH, SEQ])
        vx = ph.sb("vx", [P, DH, SEQ])
        both = ph.pair("both", [P, 2 * SEQ])
        vT = [x[:, :].rearrange("p (k r c) -> p k r c", k=KT, r=2) for x in both]
        yp = [x[:, :].rearrange("p (h t) -> p h t", h=DH) for x in both]
        NPM = 3
        pm = [ph.sb(f"pm{n}", [P, 2, 2, D]) for n in range(NPM)]
        yf = ph.sb("yf", [P, 4, D])
        yk = [ph.pair(f"yk{b}", [P, 4, D]) for b in range(2)]
        zy = ph.sb("zy", [P, 2 * SEQ])
        yv = zy[:, :].rearrange("p (h t r) -> p h r t", h=DH, r=2)
        z = zy[:, :].rearrange("p (t d) -> p t d", d=D)
        st = ph.sb("st", [P, 2 * TT, 6])
        mv = ph.sb("mv", [P, 2 * TT, 2])
        rs = ph.sb("rs", [P, 2 * TT])
        ve = ph.sb("ve", [P, 2 * TT])
        tick = ph.sb("tick", [P, 1])
        pF = [ph.ps(f"pF{n}", [P, BLK]) for n in range(4)]
        pG = [ph.ps(f"pG{n}", [P, BLK]) for n in range(4)]
        padded = ph.sem("padded")
        hhi, hlo = ph.sem("hhi"), ph.sem("hlo")
        in_mm, up_done, t0_done = ph.sem("in_mm"), ph.sem("up"), ph.sem("t0")
        cv = ph.sem("cv")
        vT_mm, vT_hi, vT_lo = ph.sem("vT_mm"), ph.sem("vT_hi"), ph.sem("vT_lo")
        f_mm, i_mm = ph.sem("f_mm"), ph.sem("i_mm")
        mul = ph.sem("mul")
        comb = ph.sem("comb")
        half = ph.sem("half")
        y_hi, y_lo = ph.sem("y_hi"), ph.sem("y_lo")
        yv_done, yv_hi, yv_lo = ph.sem("yv"), ph.sem("yv_hi"), ph.sem("yv_lo")
        e_mm = ph.sem("e_mm")
        z_done, st_done, mv_done, ve_done, rs_done = (ph.sem(x) for x in ("z", "st", "mv", "ve", "rs"))
        zn_done, added = ph.sem("zn"), ph.sem("added")
        stored, res_loaded = ph.sem("stored"), ph.sem("res_loaded")
        block = ctx.enter_context(nc.Block())

        ORDER = [(DH, "x1", 0), (2 * DH, "v", 0), (DH + 1, "x1", 1), (2 * DH + 1, "v", 1), (0, "x0", 0), (1, "x0", 1)]
        STEPS = [2, 3, 2, 3, 2, 2]
        CV = sum(STEPS)

        def cv_at(i, n):
            return CV * i + sum(STEPS[:n + 1])

        def batches(eng, body):
            rounds(eng, BATCH, lambda p, par, first, last: body(2 * p + par, first, last))

        def tokens(dram, i):
            return dram[bass.ds(i * SEQ, SEQ), :].rearrange("(t p) d -> p t d", p=P)

        @block.sync
        def _(sp):
            front.load(sp, 0, 0)
            front.load(sp, 0, 1)

            def body(i, first, last):
                wait(sp, added, i)
                sp.dma_start(xres[:, :, :], tokens(x_dram, i)).then_inc(res_loaded, 16)
                if not last:
                    for b in range(2):
                        sp.wait_ge(front.turned, 2 * i + b + 1)
                        front.load(sp, i + 1, b)
                sp.wait_ge(added, i + 1)
                sp.dma_start(tokens(y_dram, i), z).then_inc(stored, 16)

            batches(sp, body)
            sp.wait_ge(stored, 16 * BATCH)

        @block.gpsimd
        def _(pool):
            front.rstd(pool, consts, 0, 0)
            front.rstd(pool, consts, 0, 1)

            def body(i, first, last):
                for k in range(KT):
                    for o in range(4):
                        n = 16 * i + 4 * k + o
                        pool.wait_ge(comb, n + 1)
                        if o == 0:
                            wait(pool, y_lo, 4 * i + k)
                        m = pm[(4 * k + o) % NPM]
                        pool.tensor_tensor(yf[:, o, :], m[:, 0, 0, :], m[:, 0, 1, :], ALU.add).then_inc(half, 1)
                    if k == 1 and not last:
                        front.rstd(pool, consts, i + 1, 0)
                        front.rstd(pool, consts, i + 1, 1)
                pool.wait_ge(mv_done, i + 1)
                wait(pool, zn_done, i)
                pool.tensor_tensor(ve[:, :], mv[:, :, 1], consts["eps"][:, 0:1].broadcast_to([P, 2 * TT]),
                                   ALU.add).then_inc(ve_done, 1)
                pool.wait_ge(ve_done, i + 1)
                pool.tensor_tensor(rs[:, :], ve[:, :], consts["mhalf"][:, 0:1].broadcast_to([P, 2 * TT]),
                                   ALU.pow).then_inc(rs_done, 1)
                pool.wait_ge(zn_done, i + 1)
                pool.wait_ge(res_loaded, 16 * (i + 1))
                pool.tensor_tensor(z, z, xres[:, :, :], ALU.add).then_inc(added, 1)

            batches(pool, body)

        @block.scalar
        def _(act):
            def high(i, b):
                act.wait_ge(front.turned, 2 * i + b + 1)
                wait(act, in_mm, 12 * i)
                for h in range(DH):
                    last_ = act.activation(hp[b][0][:, h, :], pF[h][:, :], ACT.Identity)
                last_.then_inc(hhi, 1)

            def project(i):
                for n, (m, _, _) in enumerate(ORDER):
                    u = up[n % 2]
                    if n >= 2:
                        act.wait_ge(cv, cv_at(i, n - 2))
                    elif not (isinstance(i, int) and i == 0):
                        act.wait_ge(cv, cv_at(i - 1, n + len(ORDER) - 2))
                    for b in range(2):
                        act.wait_ge(in_mm, 12 * i + 2 * n + b + 1)
                        act.activation(u[:, 2 + b * BLK:2 + (b + 1) * BLK], pF[2 + b][:, :], ACT.Identity,
                                       bias=inb[:, m:m + 1]).then_inc(up_done, 1)
                    act.wait_ge(up_done, 12 * i + 2 * n + 2)
                    wait(act, cv, cv_at(i, n - 1) if n else CV * i)
                    act.activation(acc[:, :], u[:, 2:SEQ + 2], ACT.Identity, bias=sbias[:, m:m + 1],
                                   scale=sw[:, 2, m:m + 1]).then_inc(t0_done, 1)

            def vt_high(i):
                for q in range(KT):
                    act.wait_ge(vT_mm, 4 * i + q + 1)
                    if q == 0:
                        wait(act, e_mm, i)
                    act.activation(vT[0][:, q, :, :], pG[q][:, :].rearrange("p (r c) -> p r c", r=2),
                                   ACT.Identity).then_inc(vT_hi, 1)

            high(0, 0)
            high(0, 1)
            act.wait_ge(padded, 1)
            project(0)
            vt_high(0)

            def body(i, first, last):
                for k in range(KT):
                    act.wait_ge(half, 16 * i + 4 * (k + 1))
                    wait(act, i_mm, 4 * i + k - 1)
                    act.activation(yk[k % 2][0][:, :, :], yf[:, :, :], ACT.Identity).then_inc(y_hi, 1)
                if not last:
                    high(i + 1, 0)
                act.wait_ge(yv_done, 4 * (i + 1))
                act.activation(yp[0], zy[:, :].rearrange("p (h t) -> p h t", h=DH), ACT.Identity).then_inc(yv_hi, 1)
                if not last:
                    high(i + 1, 1)
                    project(i + 1)
                    vt_high(i + 1)

            batches(act, body)

        @block.vector
        def _(dve):
            def low(i, b):
                dve.wait_ge(hhi, 2 * i + b + 1)
                wait(dve, in_mm, 12 * i)
                for h in range(DH):
                    last_ = dve.tensor_tensor(hp[b][1][:, h, :], pF[h][:, :], hp[b][0][:, h, :].bitcast(F32),
                                              ALU.subtract)
                last_.then_inc(hlo, 1)

            def short_conv(i):
                for n, (m, kind, h) in enumerate(ORDER):
                    u = up[n % 2]
                    base = CV * i + sum(STEPS[:n])
                    dve.wait_ge(t0_done, 6 * i + n + 1)
                    dve.scalar_tensor_tensor(acc[:, :], u[:, 1:SEQ + 1], sw[:, 1, m:m + 1], acc[:, :],
                                             ALU.mult, ALU.add).then_inc(cv, 1)
                    dve.wait_ge(cv, base + 1)
                    dst = {"x1": x1[:, :], "v": acc[:, :], "x0": x0[:, h, :]}[kind]
                    dve.scalar_tensor_tensor(dst, u[:, 0:SEQ], sw[:, 0, m:m + 1], acc[:, :],
                                             ALU.mult, ALU.add).then_inc(cv, 1)
                    if kind == "v":
                        dve.wait_ge(cv, base + 2)
                        dve.tensor_tensor(vx[:, h, :], acc[:, :], x1[:, :], ALU.mult).then_inc(cv, 1)

            def vt_low(i):
                for q in range(KT):
                    dve.wait_ge(vT_hi, 4 * i + q + 1)
                    dve.tensor_tensor(vT[1][:, q, :, :], pG[q][:, :].rearrange("p (r c) -> p r c", r=2),
                                      vT[0][:, q, :, :].bitcast(F32), ALU.subtract).then_inc(vT_lo, 1)

            def y_low(i, k):
                dve.wait_ge(y_hi, 4 * i + k + 1)
                dve.tensor_tensor(yk[k % 2][1][:, :, :], yf[:, :, :], yk[k % 2][0][:, :, :].bitcast(F32),
                                  ALU.subtract).then_inc(y_lo, 1)

            def products(i, k):
                re, im = (pF[2 * (k % 2) + x][:, :].rearrange("p (r c) -> p r c", r=2) for x in range(2))

                def combine(o):
                    n = 16 * i + 4 * k + o
                    m = pm[(4 * k + o) % NPM]
                    dve.wait_ge(mul, n + 1)
                    dve.tensor_tensor(m[:, 0, :, :], m[:, 0, :, :], m[:, 1, :, :],
                                      ALU.subtract if o % 2 == 0 else ALU.add).then_inc(comb, 1)

                dve.wait_ge(f_mm, 4 * i + k + 1)
                for o in range(4):
                    n = 16 * i + 4 * k + o
                    m = pm[(4 * k + o) % NPM]
                    slot = slice(1, 3) if o < 2 else slice(0, 2)
                    a, b = (re, im) if o % 2 == 0 else (im, re)
                    wait(dve, half, n - NPM + 1)
                    dve.tensor_tensor(m[:, 0, :, :], a, ks[:, k, 0, slot, :], ALU.mult)
                    dve.tensor_tensor(m[:, 1, :, :], b, ks[:, k, 1, slot, :], ALU.mult).then_inc(mul, 1)
                    if o:
                        combine(o - 1)
                    if o == 1 and k:
                        y_low(i, k - 1)
                combine(3)

            dve.memset(up[0][:, 0:2], 0.0)
            dve.memset(up[1][:, 0:2], 0.0).then_inc(padded, 1)
            for b in range(2):
                front.stats(dve, 0, b)
                front.norm(dve, 0, b)
            low(0, 0)
            low(0, 1)
            short_conv(0)
            vt_low(0)

            def body(i, first, last):
                for k in range(KT):
                    products(i, k)
                    for b in range(2):
                        if k == 0 and not last:
                            front.stats(dve, i + 1, b)
                        if k == 2 and not last:
                            front.norm(dve, i + 1, b)
                y_low(i, KT - 1)
                dve.wait_ge(i_mm, 4 * (i + 1))
                wait(dve, stored, 16 * i)
                for h in range(DH):
                    for r in range(2):
                        dve.tensor_tensor(yv[:, h, r, :], pG[2 * h + r][:, :],
                                          x0[:, h, :].rearrange("p (t r) -> p r t", r=2)[:, r, :],
                                          ALU.mult).then_inc(yv_done, 1)
                if not last:
                    low(i + 1, 0)
                dve.wait_ge(yv_hi, i + 1)
                dve.wait_ge(yv_done, 4 * (i + 1))
                dve.tensor_tensor(yp[1], zy[:, :].rearrange("p (h t) -> p h t", h=DH), yp[0].bitcast(F32),
                                  ALU.subtract).then_inc(yv_lo, 1)
                if not last:
                    low(i + 1, 1)
                    short_conv(i + 1)
                dve.wait_ge(e_mm, i + 1)
                dve.wait_ge(yv_lo, i + 1)
                for n in range(4):
                    last_ = dve.tensor_tensor(z[:, 2 * n:2 * n + 2, :],
                                              pF[n][:, :].rearrange("p (t d) -> p t d", t=2),
                                              outb[:, :].unsqueeze(1).broadcast_to([P, 2, D]), ALU.add)
                last_.then_inc(z_done, 1)
                dve.wait_ge(z_done, i + 1)
                for t in range(2 * TT):
                    last_ = dve.bn_stats(st[:, t, :], z[:, t, :])
                last_.then_inc(st_done, 1)
                dve.wait_ge(st_done, i + 1)
                wait(dve, rs_done, i)
                dve.memset(tick[:, :], 0.0)
                for t in range(2 * TT):
                    last_ = dve.bn_aggr(mv[:, t, :], st[:, t, :])
                last_.then_inc(mv_done, 1)
                if not last:
                    vt_low(i + 1)
                dve.wait_ge(rs_done, i + 1)
                for t in range(2 * TT):
                    last_ = dve.tensor_scalar(z[:, t, :], z[:, t, :], mv[:, t, 0:1], rs[:, t:t + 1],
                                              ALU.subtract, ALU.mult)
                last_.then_inc(zn_done, 1)

            batches(dve, body)

        @block.tensor
        def _(pe):
            def project(i):
                wait(pe, mul, 16 * i)
                front.turn(pe, pF, i, 0)
                pe.wait_ge(hlo, 2 * i + 1)
                front.turn(pe, pF, i, 1)
                pe.wait_ge(hlo, 2 * i + 2)
                for n, (m, _, _) in enumerate(ORDER):
                    for b in range(2):
                        wait(pe, up_done, 12 * i + 2 * n + b - 1)
                        for k in range(DH):
                            mm = three_pass(pe, pF[2 + b][:, :], tuple(w[:, k, m * P:(m + 1) * P] for w in wi),
                                            tuple(x[:, k, :] for x in hp[b]), k == 0, k == DH - 1)
                        mm.then_inc(in_mm, 1)

            def turn_vx(i):
                pe.wait_ge(cv, cv_at(i, 3))
                wait(pe, yv_done, 4 * i)
                for q in range(KT):
                    for r in range(2):
                        for h in range(DH):
                            src = vx[:, h, :].rearrange("p (q s r) -> p q r s", q=KT, r=2)[:, q, r, :]
                            mm = pe.transpose(pG[q][:, r * D + h * P:r * D + (h + 1) * P], src, consts["ident"][:, :])
                    mm.then_inc(vT_mm, 1)

            def forward(i, k):
                if k == 0:
                    pe.wait_ge(vT_lo, 4 * (i + 1))
                    wait(pe, z_done, i)
                    pe.wait_ge(up_done, 12 * (i + 1))
                if k >= 2:
                    pe.wait_ge(mul, 16 * i + 4 * (k - 1))
                for x, m in enumerate((cos_m, sin_m)):
                    for q in range(KT):
                        mm = three_pass(pe, pF[2 * (k % 2) + x][:, :], tuple(w[:, q, k * P:(k + 1) * P] for w in m),
                                        tuple(v[:, q, :, :].rearrange("p r c -> p (r c)") for v in vT),
                                        q == 0, q == KT - 1)
                mm.then_inc(f_mm, 1)

            def inverse(i, k):
                pe.wait_ge(y_lo, 4 * i + k + 1)
                for h in range(DH):
                    for r in range(2):
                        for x, m in enumerate((cos_m, sin_m)):
                            mm = three_pass(pe, pG[2 * h + r][:, :],
                                            tuple(y[:, 2 * r + x, h * P:(h + 1) * P] for y in yk[k % 2]),
                                            tuple(w[:, k, :] for w in m), k == 0 and x == 0,
                                            k == KT - 1 and x == 1)
                mm.then_inc(i_mm, 1)

            def project_out(i, last):
                pe.wait_ge(yv_lo, i + 1)
                if last:
                    pe.wait_ge(mul, 16 * (i + 1))
                else:
                    pe.wait_ge(up_done, 12 * (i + 2))
                for t in range(2 * TT):
                    for h in range(DH):
                        mm = three_pass(pe, pF[t // 2][:, (t % 2) * D:(t % 2 + 1) * D],
                                        tuple(y[:, h, t * P:(t + 1) * P] for y in yp),
                                        tuple(w[:, h, :] for w in wo), h == 0, h == DH - 1)
                mm.then_inc(e_mm, 1)

            project(0)
            turn_vx(0)

            def body(i, first, last):
                for k in range(KT + 1):
                    if k < KT:
                        forward(i, k)
                    if k:
                        inverse(i, k - 1)
                if not last:
                    project(i + 1)
                project_out(i, last)
                if not last:
                    turn_vx(i + 1)

            batches(pe, body)


def program(nc, t, out):
    def scratch(name, shape):
        return nc.dram_tensor(name, shape, F32, kind="Internal").ap()

    xs = [scratch(f"x_after_{n}", (TOKENS, D)) for n in range(3)]
    mid = scratch("x_mid", (TOKENS, D))
    mw = scratch("batch_weights", (BATCH, 2 * D, HID))
    with ExitStack() as ctx:
        consts = make_consts(nc, ctx, t["identity"])
        hyena(nc, t["u"], xs[0], consts, t["cos"], t["sin"],
              tuple(t[n] for n in ("pos", "times", "decay", "mlp_w1", "mlp_w2", "mlp_w3", "mlp_wo", "mlp_b", "freq",
                                   "filt_bias", "half_angle")),
              t["in_w"], t["in_b"], t["short_w"], t["short_b"], t["out_w"], t["out_b"])
        channel_mix(nc, xs[0], xs[1], consts, t["W_r"], t["W_k"], t["W_v"], t["mu_r"], t["mu_k"])
        linear_attention(nc, xs[1], mid, consts, t["wq"], t["wk"], t["wv"], t["wo"], t["ln1_g"], t["ln1_b"],
                         t["head_parity"], t["causal"], t["same_head"])
        gelu_levels(nc, xs[1], mid, xs[2], consts, t["ln2_g"], t["ln2_b"], t["cms_w1"], t["cms_b1"], t["cms_w2"],
                    t["cms_b2"], t["cms_b2_last"])
        ph = Phase(nc, ctx, "shared")
        shared = ph.sb("mb1", [P, BATCH, FT]), ph.sb("mb2", [P, BATCH, D])
        expert_weights(nc, xs[2], consts, shared, mw, t["expert_rows"], t["base_rows"], t["gate_w1"], t["gate_b1"],
                       t["gate_w2"], t["gate_b2"], t["expert_select"], t["row_select"], t["row_spread"],
                       t["Tb1"], t["b1"], t["Tb2"], t["b2"])
        batch_mlp(nc, xs[2], out, consts, shared, mw)


def tables():
    f = np.float32

    def columns(v):
        return v.reshape(-1, P).T

    def rows(w):
        return w.reshape(w.shape[0] // P, P, -1).transpose(1, 0, 2).reshape(P, -1)

    time = np.linspace(0.0, 1.0, SEQ).astype(f)
    angle = (f(1e-4) * (f(TWO_PI) * np.linspace(0.0, SEQ - 1.0, SEQ).astype(f) / f(SEQ))).astype(f)
    deltas = np.linspace(np.log(0.01) / 1.5, np.log(0.01) / 0.3, D).astype(f)
    k = np.arange(HALF) + 0.5
    grid = TWO_PI / SEQ * np.outer(k, k)
    half = np.pi * k / SEQ
    head = np.arange(P) // HD
    got = {
        "identity": np.eye(P), "cos": rows(np.cos(grid)), "sin": rows(np.sin(grid)),
        "pos": np.stack([time, np.cos(angle), -np.sin(angle)]),
        "times": time.reshape(KT, P, 2).transpose(1, 0, 2).reshape(P, 2 * KT), "decay": -np.abs(deltas),
        "half_angle": np.concatenate([columns(g / HALF) for g in (np.cos(half), np.sin(half), -np.sin(half))], 1),
        "head_parity": np.stack([head % 2 == 0, head % 2 == 1], 1), "causal": np.triu(np.ones((P, P))),
        "same_head": head[:, None] == head[None, :], "expert_select": np.repeat(np.eye(EXPERTS), GROUP, 1),
        "row_select": np.tile(np.eye(GROUP), (EXPERTS, 1)), "row_spread": np.tile(np.eye(GROUP), (1, BATCH)),
    }
    return {n: np.ascontiguousarray(a, dtype=f) for n, a in got.items()}


def kernel(**inputs):
    import concourse.bacc as bacc
    from concourse.bass_utils import run_bass_kernel_spmd

    def columns(v):
        return v.reshape(-1, P).T

    def rows(w):
        return w.reshape(w.shape[0] // P, P, -1).transpose(1, 0, 2).reshape(P, -1)

    def part(prefix):
        return lambda name: np.asarray(inputs[f"{prefix}_{name}"])

    a, c, l, g = part("L0_attn"), part("L0_ffn"), part("L1_attn"), part("L1_ffn")
    sw = a("short_w")
    w2_rows = g("TW2").transpose(0, 2, 1).reshape(EXPERTS, D, HID)
    experts = np.concatenate([g("TW1").transpose(0, 2, 1), w2_rows], 1)
    given = {
        "u": a("u").reshape(TOKENS, D), "in_w": rows(a("in_w")), "in_b": columns(a("in_b")),
        "short_w": np.concatenate([columns(sw[:, j]) for j in range(3)], 1), "short_b": columns(a("short_b")),
        "mlp_w1": a("mlp_w1"), "mlp_w2": a("mlp_w2"), "mlp_w3": a("mlp_w3"), "mlp_wo": a("mlp_wo"),
        "mlp_b": np.stack([a("mlp_b1"), a("mlp_b2"), a("mlp_b3")], 1), "freq": a("freq").T,
        "filt_bias": a("filt_bias").reshape(1, D), "out_w": rows(a("out_w")), "out_b": a("out_b"),
        "W_r": rows(c("W_r").T), "W_k": rows(c("W_k").T), "W_v": rows(c("W_v").T),
        "mu_r": columns(c("mu_r")), "mu_k": columns(c("mu_k")),
        "wq": rows(l("wq")), "wk": rows(l("wk")), "wv": rows(l("wv")), "wo": rows(l("wo")),
        "ln1_g": columns(l("ln1_g")), "ln1_b": columns(l("ln1_b")),
        "ln2_g": columns(l("ln2_g")), "ln2_b": columns(l("ln2_b")),
        "cms_w1": np.stack([rows(w) for w in l("cms_w1")]), "cms_w2": np.stack([rows(w) for w in l("cms_w2")]),
        "cms_b1": columns(l("cms_b1")), "cms_b2": columns(l("cms_b2")), "cms_b2_last": l("cms_b2")[-1],
        "gate_w1": rows(g("gate_w1").T), "gate_b1": columns(g("gate_b1")), "gate_w2": rows(g("gate_w2").T),
        "gate_b2": g("gate_b2").reshape(EXPERTS, 1),
        "expert_rows": experts.reshape(EXPERTS, GROUPS, GROUP, HID).transpose(1, 0, 2, 3).reshape(GROUPS * P, HID),
        "base_rows": np.concatenate([g("W1").T, g("W2").T.reshape(D, HID)], 0),
        "b1": columns(g("b1")), "b2": g("b2").reshape(1, D), "Tb1": g("Tb1"), "Tb2": g("Tb2"),
    }
    nc = bacc.Bacc("TRN2", target_bir_lowering=False, num_devices=1)
    arrays, views = {}, {}
    for name, value in {**given, **tables()}.items():
        arrays[f"{name}_dram"] = np.ascontiguousarray(value)
        views[name] = nc.dram_tensor(f"{name}_dram", value.shape, F32, kind="ExternalInput").ap()
    out = nc.dram_tensor("out_dram", (TOKENS, D), F32, kind="ExternalOutput").ap()
    program(nc, views, out)
    result = run_bass_kernel_spmd(nc, [arrays], core_ids=[0])
    return result.results[0]["out_dram"].reshape(BATCH, SEQ, D)
```

```python
from contextlib import ExitStack

import numpy as np

import concourse.bass as bass
from concourse import mybir

P = 128
EPS = 1e-5
F32 = mybir.dt.float32
F32R = mybir.dt.float32r
ALU = mybir.AluOpType
ACT = mybir.ActivationFunctionType

BATCH, SEQ, D = 8, 1024, 256
TOKENS = BATCH * SEQ
DH = D // P
BLK = 512
NBLK = TOKENS // BLK
TT = BLK // P


def wait(eng, sem, value):
    if isinstance(value, int) and value <= 0:
        return
    eng.wait_ge(sem, value)


def rounds(eng, n, body):
    body(0, 0, True, False)
    body(0, 1, False, False)
    if n > 4:
        with eng.Fori(1, n // 2 - 1) as p:
            body(p, 0, False, False)
            body(p, 1, False, False)
    body(n // 2 - 1, 0, False, False)
    body(n // 2 - 1, 1, False, True)


def after(p, par):
    return (p, 1) if par == 0 else (p + 1, 0)


def before(p, par):
    return (p, 0) if par == 1 else (p - 1, 1)


def skewed(eng, n, ahead, behind, body):
    def run(p, par):
        def do(d, stage):
            q, b = p + (par + d) // 2, (par + d) % 2
            if not isinstance(p, int) or 0 <= 2 * q + b < n:
                stage(q, b)
        body(do)

    first, lo, hi, end = -((ahead + 1) // 2), behind // 2 + 1, (n - ahead) // 2, (n + behind + 1) // 2
    for p in range(first, lo):
        run(p, 0)
        run(p, 1)
    with eng.Fori(lo, hi) as p:
        run(p, 0)
        run(p, 1)
    for p in range(hi, end):
        run(p, 0)
        run(p, 1)


def three_pass(pe, out, w, x, start, stop):
    (w_hi, w_lo), (x_hi, x_lo) = w, x
    pe.matmul(out, w_lo, x_hi, start=start, stop=False)
    pe.matmul(out, w_hi, x_lo, start=False, stop=False)
    return pe.matmul(out, w_hi, x_hi, start=False, stop=stop)


class Phase:

    def __init__(self, nc, ctx, name):
        self.nc, self.ctx, self.name, self.sems = nc, ctx, name, []
        ctx.callback(self.close)

    def close(self):
        if self.sems:
            self.nc.clear_and_free_semaphores(self.sems)
            self.nc.all_engine_barrier()

    def sb(self, name, shape, dt=F32):
        return self.ctx.enter_context(self.nc.sbuf_tensor(f"{self.name}_{name}", shape, dt))

    def ps(self, name, shape, dt=F32):
        return self.ctx.enter_context(self.nc.psum_tensor(f"{self.name}_{name}", shape, dt))

    def sem(self, name):
        self.sems.append(self.nc.alloc_semaphore(name=f"{self.name}_{name}"))
        return self.sems[-1]

    def pair(self, name, shape):
        return self.sb(name + "_hi", shape, F32R), self.sb(name + "_lo", shape, F32R)


def load_weights(nc, name, plain, split, chunk=2048):
    with ExitStack() as ctx:
        ph = Phase(nc, ctx, name)
        n_bufs = 3
        raw = [ph.sb(f"raw{b}", [P, chunk]) for b in range(n_bufs)] if split else []
        loaded_plain = ph.sem("loaded_plain")
        loaded = [ph.sem(f"loaded{b}") for b in range(n_bufs)]
        hi_done = ph.sem("hi_done")
        lo_done = ph.sem("lo_done")
        pieces = []
        for (hi, lo), src in split:
            rows, n = src.shape
            for c in range(0, n, chunk):
                m = min(chunk, n - c)
                pieces.append((rows, m, hi[:, c:c + m], lo[:, c:c + m], src[:, c:c + m]))
        block = ctx.enter_context(nc.Block())

        @block.sync
        def _(sp):
            for n, (rows, m, _, _, src) in enumerate(pieces):
                wait(sp, lo_done, n - n_bufs + 1)
                sp.dma_start(raw[n % n_bufs][0:rows, 0:m], src).then_inc(loaded[n % n_bufs], 16)

        @block.gpsimd
        def _(pool):
            for dst, src in plain:
                pool.dma_start(dst, src).then_inc(loaded_plain, 16)
            if plain:
                pool.wait_ge(loaded_plain, 16 * len(plain))

        @block.scalar
        def _(act):
            for n, (rows, m, hi, _, _) in enumerate(pieces):
                act.wait_ge(loaded[n % n_bufs], 16 * (n // n_bufs + 1))
                act.activation(hi, raw[n % n_bufs][0:rows, 0:m], ACT.Identity).then_inc(hi_done, 1)

        @block.vector
        def _(dve):
            for n, (rows, m, hi, lo, _) in enumerate(pieces):
                dve.wait_ge(hi_done, n + 1)
                dve.tensor_tensor(lo, raw[n % n_bufs][0:rows, 0:m], hi.bitcast(F32),
                                  ALU.subtract).then_inc(lo_done, 1)


class Front:

    def __init__(self, ph, x_dram, ident, in_place=False):
        self.ph, self.x_dram, self.ident = ph, x_dram, ident
        self.x = [ph.sb(f"f_x{b}", [P, TT, D]) for b in range(2)]
        self.xn = self.x if in_place else [ph.sb(f"f_xn{b}", [P, TT, D]) for b in range(2)]
        self.st = [ph.sb(f"f_st{b}", [P, TT, 6]) for b in range(2)]
        self.mv = [ph.sb(f"f_mv{b}", [P, TT, 2]) for b in range(2)]
        self.rs = [ph.sb(f"f_rs{b}", [P, TT]) for b in range(2)]
        self.ve = [ph.sb(f"f_ve{b}", [P, TT]) for b in range(2)]
        self.tick = ph.sb("f_tick", [P, 1])
        self.loaded = [ph.sem(f"x_loaded{b}") for b in range(2)]
        self.st_done = ph.sem("f_stats")
        self.mv_done = ph.sem("f_mv")
        self.ve_done = ph.sem("f_ve")
        self.rs_done = ph.sem("f_rstd")
        self.xn_done = ph.sem("f_xn")
        self.turned = ph.sem("f_turned")

    def load(self, sp, p, par):
        i = 2 * p + par
        src = self.x_dram[bass.ds(i * BLK, BLK), :].rearrange("(t p) d -> p t d", p=P)
        sp.dma_start(self.x[par][:, :, :], src).then_inc(self.loaded[par], 16)

    def stats(self, dve, p, par):
        i = 2 * p + par
        dve.wait_ge(self.loaded[par], 16 * (p + 1))
        for t in range(TT):
            last = dve.bn_stats(self.st[par][:, t, :], self.x[par][:, t, :])
        last.then_inc(self.st_done, 1)
        dve.wait_ge(self.st_done, i + 1)
        wait(dve, self.rs_done, i - 1)
        dve.memset(self.tick[:, :], 0.0)
        for t in range(TT):
            last = dve.bn_aggr(self.mv[par][:, t, :], self.st[par][:, t, :])
        last.then_inc(self.mv_done, 1)

    def rstd(self, pool, consts, p, par):
        i = 2 * p + par
        pool.wait_ge(self.mv_done, i + 1)
        wait(pool, self.xn_done, i - 1)
        pool.tensor_tensor(self.ve[par][:, :], self.mv[par][:, :, 1], consts["eps"], ALU.add).then_inc(self.ve_done, 1)
        pool.wait_ge(self.ve_done, i + 1)
        pool.tensor_tensor(self.rs[par][:, :], self.ve[par][:, :], consts["mhalf"], ALU.pow).then_inc(self.rs_done, 1)

    def norm(self, dve, p, par):
        i = 2 * p + par
        dve.wait_ge(self.rs_done, i + 1)
        wait(dve, self.turned, i - 1)
        for t in range(TT):
            last = dve.tensor_scalar(self.xn[par][:, t, :], self.x[par][:, t, :], self.mv[par][:, t, 0:1],
                                     self.rs[par][:, t:t + 1], ALU.subtract, ALU.mult)
        last.then_inc(self.xn_done, 1)

    def turn(self, pe, banks, p, par):
        pe.wait_ge(self.xn_done, 2 * p + par + 1)
        for h in range(DH):
            for t in range(TT):
                last = pe.transpose(banks[h][:, t * P:(t + 1) * P], self.xn[par][:, t, h * P:(h + 1) * P],
                                    self.ident[:, :])
        last.then_inc(self.turned, 1)


class TokenNorm:

    def __init__(self, ph, name, tiles=TT):
        self.tiles = tiles
        self.st = [ph.sb(f"{name}_st{b}", [P, tiles, 6]) for b in range(2)]
        self.mv = [ph.sb(f"{name}_mv{b}", [P, tiles, 2]) for b in range(2)]
        self.tmp = [ph.sb(f"{name}_tmp{b}", [P, 2, tiles]) for b in range(2)]
        self.scale = [ph.sb(f"{name}_scale{b}", [P, tiles]) for b in range(2)]
        self.shift = [ph.sb(f"{name}_shift{b}", [P, tiles]) for b in range(2)]
        self.tick = ph.sb(f"{name}_tick", [P, 1])
        self.st_done = ph.sem(f"{name}_stats")
        self.mv_done = ph.sem(f"{name}_mv")
        self.step = ph.sem(f"{name}_step")
        self.factors_done = ph.sem(f"{name}_factors")
        self.done = ph.sem(f"{name}_normed")

    def stats(self, dve, x, p, par):
        i = 2 * p + par
        for t in range(self.tiles):
            last = dve.bn_stats(self.st[par][:, t, :], x[:, t, :])
        last.then_inc(self.st_done, 1)
        dve.wait_ge(self.st_done, i + 1)
        wait(dve, self.factors_done, i - 1)
        dve.memset(self.tick[:, :], 0.0)
        for t in range(self.tiles):
            last = dve.bn_aggr(self.mv[par][:, t, :], self.st[par][:, t, :])
        last.then_inc(self.mv_done, 1)

    def factors(self, pool, consts, p, par):
        i = 2 * p + par
        mean, var = self.mv[par][:, :, 0], self.mv[par][:, :, 1]
        t0, t1, scale = self.tmp[par][:, 0, :], self.tmp[par][:, 1, :], self.scale[par][:, :]
        const = lambda name: consts[name][:, 0:1].broadcast_to([P, self.tiles])
        pool.wait_ge(self.mv_done, i + 1)
        wait(pool, self.done, i - 1)
        pool.tensor_tensor(t0, var, const("eps"), ALU.add).then_inc(self.step, 1)
        pool.wait_ge(self.step, 3 * i + 1)
        pool.tensor_tensor(scale, t0, const("mhalf"), ALU.pow).then_inc(self.step, 1)
        pool.wait_ge(self.step, 3 * i + 2)
        pool.tensor_tensor(t1, mean, scale, ALU.mult).then_inc(self.step, 1)
        pool.wait_ge(self.step, 3 * i + 3)
        pool.tensor_tensor(self.shift[par][:, :], t1, const("mone"), ALU.mult).then_inc(self.factors_done, 1)

    def apply(self, act, out, x, p, par):
        act.wait_ge(self.factors_done, 2 * p + par + 1)
        for t in range(self.tiles):
            last = act.activation(out[:, t, :], x[:, t, :], ACT.Identity, bias=self.shift[par][:, t:t + 1],
                                  scale=self.scale[par][:, t:t + 1])
        last.then_inc(self.done, 1)


class Back:

    def __init__(self, ph, front, y_dram):
        self.ph, self.front, self.y_dram = ph, front, y_dram
        self.z = [ph.sb(f"z{b}", [P, TT, D]) for b in range(2)]
        self.st = [ph.sb(f"b_st{b}", [P, TT, 6]) for b in range(2)]
        self.mv = [ph.sb(f"b_mv{b}", [P, TT, 2]) for b in range(2)]
        self.rs = [ph.sb(f"b_rs{b}", [P, TT]) for b in range(2)]
        self.ve = [ph.sb(f"b_ve{b}", [P, TT]) for b in range(2)]
        self.tick = ph.sb("b_tick", [P, 1])
        self.st_done = ph.sem("b_stats")
        self.mv_done = ph.sem("b_mv")
        self.ve_done = ph.sem("b_ve")
        self.rs_done = ph.sem("b_rstd")
        self.zn_done = ph.sem("b_zn")
        self.added = ph.sem("b_added")
        self.stored = [ph.sem(f"b_stored{b}") for b in range(2)]

    def z_free(self, eng, p, par):
        wait(eng, self.stored[par], 16 * p)

    def stats(self, dve, z_sem, z_count, p, par):
        i = 2 * p + par
        dve.wait_ge(z_sem, z_count)
        for t in range(TT):
            last = dve.bn_stats(self.st[par][:, t, :], self.z[par][:, t, :])
        last.then_inc(self.st_done, 1)
        dve.wait_ge(self.st_done, i + 1)
        wait(dve, self.rs_done, i - 1)
        dve.memset(self.tick[:, :], 0.0)
        for t in range(TT):
            last = dve.bn_aggr(self.mv[par][:, t, :], self.st[par][:, t, :])
        last.then_inc(self.mv_done, 1)

    def rstd(self, pool, consts, p, par):
        i = 2 * p + par
        pool.wait_ge(self.mv_done, i + 1)
        wait(pool, self.zn_done, i - 1)
        pool.tensor_tensor(self.ve[par][:, :], self.mv[par][:, :, 1], consts["eps"], ALU.add).then_inc(self.ve_done, 1)
        pool.wait_ge(self.ve_done, i + 1)
        pool.tensor_tensor(self.rs[par][:, :], self.ve[par][:, :], consts["mhalf"], ALU.pow).then_inc(self.rs_done, 1)

    def norm(self, dve, p, par):
        i = 2 * p + par
        dve.wait_ge(self.rs_done, i + 1)
        z = self.z[par]
        for t in range(TT):
            last = dve.tensor_scalar(z[:, t, :], z[:, t, :], self.mv[par][:, t, 0:1],
                                     self.rs[par][:, t:t + 1], ALU.subtract, ALU.mult)
        last.then_inc(self.zn_done, 1)

    def add(self, pool, p, par):
        pool.wait_ge(self.zn_done, 2 * p + par + 1)
        z = self.z[par]
        pool.tensor_tensor(z[:, :, :], z[:, :, :], self.front.x[par][:, :, :], ALU.add).then_inc(self.added, 1)

    def store(self, eng, p, par):
        i = 2 * p + par
        eng.wait_ge(self.added, i + 1)
        dst = self.y_dram[bass.ds(i * BLK, BLK), :].rearrange("(t p) d -> p t d", p=P)
        eng.dma_start(dst, self.z[par][:, :, :]).then_inc(self.stored[par], 16)

    def all_stored(self, eng):
        for s in self.stored:
            eng.wait_ge(s, 16 * NBLK // 2)


def channel_mix(nc, x_dram, y_dram, consts, W_r, W_k, W_v, mu_r, mu_k):
    with ExitStack() as ctx:
        ph = Phase(nc, ctx, "cm")
        wr = ph.pair("wr", [P, DH, D])
        wk = ph.pair("wk", [P, DH, D])
        wv = ph.pair("wv", [P, DH, D])
        mu = ph.sb("mu", [P, 2, DH])
        flat = lambda w: tuple(t[:, :, :].rearrange("p a b -> p (a b)") for t in w)
        load_weights(nc, "cml",
                     [(mu[:, 0, :], mu_r), (mu[:, 1, :], mu_k)],
                     [(flat(wr), W_r), (flat(wk), W_k), (flat(wv), W_v)])
        x, x_res, z, r = ([ph.sb(f"{n}{b}", [P, TT, D]) for b in range(2)] for n in ("x", "x_res", "z", "r"))
        xT = [ph.sb(f"xT{b}", [P, DH, BLK + 1]) for b in range(2)]
        dx, kr, ka = ([ph.sb(f"{n}{b}", [P, DH, BLK]) for b in range(2)] for n in ("dx", "kr", "ka"))
        mixed = {m: [ph.sb(f"mix_{m}{b}", [P, DH, BLK]) for b in range(2)] for m in "rk"}
        mixp = {m: [ph.pair(f"mixp_{m}{b}", [P, DH, BLK]) for b in range(2)] for m in "rk"}
        kap = [ph.pair(f"kap{b}", [P, DH, BLK]) for b in range(2)]
        front = TokenNorm(ph, "front")
        back = TokenNorm(ph, "back")
        pT = [ph.ps(f"pT{h}", [P, BLK]) for h in range(DH)]
        pK = [ph.ps(f"pK{h}", [P, BLK]) for h in range(DH)]
        pR = [ph.ps(f"pR{h}", [P, 2, D]) for h in range(2)]
        pV = [ph.ps(f"pV{h}", [P, 2, D]) for h in range(2)]
        x_loaded = [ph.sem(f"x_loaded{b}") for b in range(2)]
        res_loaded = [ph.sem(f"res_loaded{b}") for b in range(2)]
        stored = [ph.sem(f"stored{b}") for b in range(2)]
        zeroed = ph.sem("zeroed")
        turned = ph.sem("turned")
        xT_done = ph.sem("xT")
        dx_done = ph.sem("dx")
        mix_done = ph.sem("mix")
        hi_done = ph.sem("mix_hi")
        lo_done = ph.sem("mix_lo")
        k_done = ph.sem("k")
        kr_done = ph.sem("kr")
        ka_done = ph.sem("ka")
        kahi_done = ph.sem("kahi")
        kalo_done = ph.sem("kalo")
        r_done = ph.sem("r_mm")
        sig_done = ph.sem("r_sig")
        v_done = ph.sem("v_mm")
        z_done = ph.sem("z")
        added = ph.sem("added")
        block = ctx.enter_context(nc.Block())
        AHEAD, BEHIND = 4, 2

        def tokens(dram, i):
            return dram[bass.ds(i * BLK, BLK), :].rearrange("(t p) d -> p t d", p=P)

        @block.sync
        def _(sp):
            def load(p, par):
                wait(sp, turned, 2 * p + par - 1)
                sp.dma_start(x[par][:, :, :], tokens(x_dram, 2 * p + par)).then_inc(x_loaded[par], 16)

            def load_res(p, par):
                wait(sp, added, 2 * p + par - 1)
                sp.dma_start(x_res[par][:, :, :], tokens(x_dram, 2 * p + par)).then_inc(res_loaded[par], 16)

            def store(p, par):
                sp.wait_ge(added, 2 * p + par + 1)
                sp.dma_start(tokens(y_dram, 2 * p + par), z[par][:, :, :]).then_inc(stored[par], 16)

            def body(do):
                do(-1, load_res)
                do(4, load)
                do(-2, store)

            skewed(sp, NBLK, AHEAD, BEHIND, body)
            for s in stored:
                sp.wait_ge(s, 16 * NBLK // 2)

        @block.gpsimd
        def _(pool):
            pool.memset(xT[0][:, :, 0:1], 0.0).then_inc(zeroed, 1)
            pool.wait_ge(zeroed, 1)

            def difference(p, par):
                i = 2 * p + par
                pool.wait_ge(xT_done, i + 1)
                wait(pool, mix_done, 2 * (i - 1))
                pool.tensor_tensor(dx[par][:, :, :], xT[par][:, :, 1:BLK + 1], xT[par][:, :, 0:BLK],
                                   ALU.subtract).then_inc(dx_done, 1)

            def square(p, par):
                i = 2 * p + par
                pool.wait_ge(kr_done, i + 1)
                wait(pool, kalo_done, i - 1)
                pool.tensor_tensor(ka[par][:, :, :], kr[par][:, :, :], kr[par][:, :, :], ALU.mult).then_inc(ka_done, 1)

            def add(p, par):
                pool.wait_ge(back.done, 2 * p + par + 1)
                pool.wait_ge(res_loaded[par], 16 * (p + 1))
                pool.tensor_tensor(z[par][:, :, :], z[par][:, :, :], x_res[par][:, :, :], ALU.add).then_inc(added, 1)

            def body(do):
                do(1, difference)
                do(-2, lambda p, par: back.factors(pool, consts, p, par))
                do(0, square)
                do(-2, add)
                do(3, lambda p, par: front.factors(pool, consts, p, par))

            skewed(pool, NBLK, AHEAD, BEHIND, body)

        @block.scalar
        def _(act):
            def take(p, par):
                i = 2 * p + par
                act.wait_ge(turned, i + 1)
                wait(act, mix_done, 2 * (i - 1))
                for h in range(DH):
                    last = act.activation(xT[par][:, h, 1:BLK + 1], pT[h][:, :], ACT.Identity)
                if par:
                    act.wait_ge(xT_done, i)
                    last = act.activation(xT[1][:, :, 0:1], xT[0][:, :, BLK:BLK + 1], ACT.Identity)
                last.then_inc(xT_done, 1)

            def mix_high(m, n):
                def stage(p, par):
                    i = 2 * p + par
                    act.wait_ge(mix_done, 2 * i + n + 1)
                    wait(act, r_done if m == "r" else k_done, i - 1)
                    act.activation(mixp[m][par][0][:, :, :], mixed[m][par][:, :, :],
                                   ACT.Identity).then_inc(hi_done, 1)
                return stage

            def relu(p, par):
                i = 2 * p + par
                act.wait_ge(k_done, i + 1)
                wait(act, ka_done, i - 1)
                for h in range(DH):
                    last = act.activation(kr[par][:, h, :], pK[h][:, :], ACT.Relu)
                last.then_inc(kr_done, 1)

            def sigmoid(p, par):
                i = 2 * p + par
                act.wait_ge(r_done, i + 1)
                wait(act, z_done, i - 1)
                for h in range(2):
                    last = act.activation(r[par][:, 2 * h:2 * h + 2, :], pR[h][:, :, :], ACT.Sigmoid)
                last.then_inc(sig_done, 1)

            def squares_high(p, par):
                i = 2 * p + par
                act.wait_ge(ka_done, i + 1)
                wait(act, v_done, i - 1)
                act.activation(kap[par][0][:, :, :], ka[par][:, :, :], ACT.Identity).then_inc(kahi_done, 1)

            def body(do):
                do(1, take)
                do(0, relu)
                do(-2, lambda p, par: back.apply(act, z[par], z[par], p, par))
                do(1, mix_high("k", 0))
                do(1, mix_high("r", 1))
                do(0, sigmoid)
                do(2, lambda p, par: front.apply(act, x[par], x[par], p, par))
                do(0, squares_high)

            skewed(act, NBLK, AHEAD, BEHIND, body)

        @block.vector
        def _(dve):
            def mix(p, par):
                i = 2 * p + par
                dve.wait_ge(dx_done, i + 1)
                wait(dve, lo_done, 2 * (i - 1))
                for m in "kr":
                    for h in range(DH):
                        s = mu[:, 0 if m == "r" else 1, h:h + 1]
                        last = dve.scalar_tensor_tensor(mixed[m][par][:, h, :], dx[par][:, h, :], s,
                                                        xT[par][:, h, 0:BLK], ALU.mult, ALU.add)
                    last.then_inc(mix_done, 1)

            def mix_low(p, par):
                i = 2 * p + par
                for n, m in enumerate("kr"):
                    dve.wait_ge(hi_done, 2 * i + n + 1)
                    dve.wait_ge(mix_done, 2 * i + n + 1)
                    hi, lo = mixp[m][par]
                    dve.tensor_tensor(lo[:, :, :], mixed[m][par][:, :, :], hi[:, :, :].bitcast(F32),
                                      ALU.subtract).then_inc(lo_done, 1)

            def squares_low(p, par):
                dve.wait_ge(kahi_done, 2 * p + par + 1)
                hi, lo = kap[par]
                dve.tensor_tensor(lo[:, :, :], ka[par][:, :, :], hi[:, :, :].bitcast(F32),
                                  ALU.subtract).then_inc(kalo_done, 1)

            def front_stats(p, par):
                dve.wait_ge(x_loaded[par], 16 * (p + 1))
                front.stats(dve, x[par], p, par)

            def gate(p, par):
                i = 2 * p + par
                dve.wait_ge(v_done, i + 1)
                dve.wait_ge(sig_done, i + 1)
                wait(dve, stored[par], 16 * p)
                for h in range(2):
                    last = dve.tensor_tensor(z[par][:, 2 * h:2 * h + 2, :], pV[h][:, :, :],
                                             r[par][:, 2 * h:2 * h + 2, :], ALU.mult)
                last.then_inc(z_done, 1)
                dve.wait_ge(z_done, i + 1)
                back.stats(dve, z[par], p, par)

            def body(do):
                do(-1, squares_low)
                do(1, mix)
                do(3, front_stats)
                do(1, mix_low)
                do(-1, gate)

            skewed(dve, NBLK, AHEAD, BEHIND, body)

        @block.tensor
        def _(pe):
            def turn(p, par):
                i = 2 * p + par
                pe.wait_ge(front.done, i + 1)
                wait(pe, xT_done, i)
                for h in range(DH):
                    for t in range(TT):
                        last = pe.transpose(pT[h][:, t * P:(t + 1) * P], x[par][:, t, h * P:(h + 1) * P],
                                            consts["ident"][:, :])
                last.then_inc(turned, 1)

            def keys(p, par):
                i = 2 * p + par
                pe.wait_ge(lo_done, 2 * i + 1)
                wait(pe, kr_done, i)
                for m in range(DH):
                    for k in range(DH):
                        mm = three_pass(pe, pK[m][:, :], tuple(w[:, k, m * P:(m + 1) * P] for w in wk),
                                        tuple(h[:, k, :] for h in mixp["k"][par]), k == 0, k == DH - 1)
                mm.then_inc(k_done, 1)

            def token_major(banks, halves, weights, done):
                for t in range(TT):
                    ts = slice(t * P, (t + 1) * P)
                    for k in range(DH):
                        mm = three_pass(pe, banks[t // 2][:, t % 2, :], tuple(h[:, k, ts] for h in halves),
                                        tuple(w[:, k, :] for w in weights), k == 0, k == DH - 1)
                mm.then_inc(done, 1)

            def gates(p, par):
                i = 2 * p + par
                pe.wait_ge(lo_done, 2 * i + 2)
                wait(pe, sig_done, i)
                token_major(pR, mixp["r"][par], wr, r_done)

            def values(p, par):
                i = 2 * p + par
                pe.wait_ge(kalo_done, i + 1)
                wait(pe, z_done, i)
                token_major(pV, kap[par], wv, v_done)

            def body(do):
                do(0, keys)
                do(0, gates)
                do(-1, values)
                do(2, turn)

            skewed(pe, NBLK, AHEAD, BEHIND, body)


def make_consts(nc, ctx, ident_d):
    ph = Phase(nc, ctx, "c")
    ident = ph.sb("ident", [P, P])
    mhalf = ph.sb("mhalf", [P, TT])
    eps = ph.sb("eps", [P, TT])
    one = ph.sb("one", [P, TT])
    mone = ph.sb("mone", [P, TT])
    loaded = ph.sem("loaded")
    made = ph.sem("made")
    with nc.Block() as block:
        @block.sync
        def _(sp):
            sp.dma_start(ident[:, :], ident_d).then_inc(loaded, 16)
            sp.wait_ge(loaded, 16)

        @block.gpsimd
        def _(pool):
            pool.memset(mhalf[:, :], -0.5).then_inc(made, 1)
            pool.memset(eps[:, :], EPS).then_inc(made, 1)
            pool.memset(one[:, :], 1.0).then_inc(made, 1)
            pool.memset(mone[:, :], -1.0).then_inc(made, 1)
            pool.wait_ge(made, 4)
    return {"ident": ident, "mhalf": mhalf[:, :], "eps": eps[:, :], "one": one[:, :], "mone": mone[:, :]}


HEADS = 16
HD = D // HEADS
CHUNK = 128
QUAD = 4


def linear_attention(nc, x_dram, y_dram, consts, wq, wk, wv, wo, ln_g, ln_b, quarter_d, causal_d, same_d):
    with ExitStack() as ctx:
        ph = Phase(nc, ctx, "la")
        w = {n: ph.pair(f"w{n}", [P, DH, D]) for n in ("q", "k", "o")}
        wkv = ph.pair("wkv", [P, DH, 2 * D])
        gb = ph.sb("gb", [P, 2, DH])
        quarter = ph.sb("quarter", [P, QUAD])
        causal = ph.sb("causal", [P, P])
        same = ph.sb("same", [P, DH, P])
        flat = lambda t: tuple(x[:, :, :].rearrange("p a b -> p (a b)") for x in t)
        kvd = []
        for h in range(DH):
            for n, src in enumerate((wk, wv)):
                kvd.append((tuple(t[:, h, n * D:(n + 1) * D] for t in wkv), src[:, h * D:(h + 1) * D]))
        load_weights(nc, "lal",
                     [(gb[:, 0, :], ln_g), (gb[:, 1, :], ln_b), (quarter[:, :], quarter_d), (causal[:, :], causal_d),
                      (same[:, 0, :], same_d), (same[:, 1, :], same_d)],
                     [(flat(w["q"]), wq), (flat(w["k"]), wk), (flat(w["o"]), wo)] + kvd)
        front = Front(ph, x_dram, consts["ident"])
        tmp = [ph.sb(f"tmp{b}", [P, 5, TT]) for b in range(2)]
        res = [ph.sb(f"res{b}", [P, TT]) for b in range(2)]
        n_res = [ph.sb(f"n_res{b}", [P, TT, D]) for b in range(2)]
        hf = ph.sb("hf", [P, DH, BLK])
        hp = ph.pair("hp", [P, DH, BLK])
        qT = [ph.sb(f"qT{b}", [P, DH, BLK]) for b in range(2)]
        kE = [[ph.sb(f"kE{b}{o}", [P, DH, BLK]) for o in range(QUAD)] for b in range(2)]
        kv = [ph.sb(f"kv{b}", [P, TT, 2 * D]) for b in range(2)]
        sT = [ph.sb(f"sT{b}", [P, 4, QUAD, P]) for b in range(2)]
        state = [ph.sb(f"state{b}", [P, DH, P]) for b in range(2)]
        ys = ph.sb("ys", [P, TT, D])
        yp = ph.pair("yp", [P, DH, BLK])
        z = [ph.sb(f"z{b}", [P, TT, D]) for b in range(2)]
        pA = [ph.ps(f"pA{h}", [P, BLK]) for h in range(2)]
        pS = [ph.ps(f"pS{j}", [P, QUAD, P]) for j in range(4)]
        pY = ph.ps("pY", [P, 2 * D])
        pM = ph.ps("pM", [P, DH * P * 2])
        small = ph.sem("small")
        n_done = ph.sem("n_res")
        hf_done = ph.sem("hf")
        hhi_done = ph.sem("hhi")
        hlo_done = ph.sem("hlo")
        q_mm, k_mm, kv_mm = ph.sem("q_mm"), ph.sem("k_mm"), ph.sem("kv_mm")
        q_ev, k_ev, kv_ev = ph.sem("q_ev"), ph.sem("k_ev"), ph.sem("kv_ev")
        s_mm = ph.sem("s_mm")
        s_ev = ph.sem("s_ev")
        m_mm = ph.sem("m_mm")
        m_ev = ph.sem("m_ev")
        y_mm = ph.sem("y_mm")
        y_ev = ph.sem("y_ev")
        yT_mm = ph.sem("yT_mm")
        yhi_done = ph.sem("yhi")
        ylo_done = ph.sem("ylo")
        o_mm = ph.sem("o_mm")
        z_done = ph.sem("z")
        stored = [ph.sem(f"stored{b}") for b in range(2)]
        block = ctx.enter_context(nc.Block())
        STATES = 2 * TT - 1
        END = NBLK // 2

        def states(p, par, t):
            return STATES * p + TT * par + t

        @block.sync
        def _(sp):
            front.load(sp, 0, 0)
            front.load(sp, 0, 1)

            def store(p, par):
                i = 2 * p + par
                sp.wait_ge(z_done, i + 1)
                dst = y_dram[bass.ds(i * BLK, BLK), :].rearrange("(t p) d -> p t d", p=P)
                sp.dma_start(dst, z[par][:, :, :]).then_inc(stored[par], 16)

            def body(p, par, first, last):
                if not (isinstance(p, int) and p == END - 1):
                    sp.wait_ge(front.xn_done, 2 * p + par + 1)
                    front.load(sp, p + 1, par)
                if not first:
                    store(*before(p, par))

            rounds(sp, NBLK, body)
            store(END - 1, 1)
            for s in stored:
                sp.wait_ge(s, 16 * NBLK // 2)

        @block.gpsimd
        def _(pool):
            def rstd(p, par):
                i = 2 * p + par
                var = front.mv[par][:, :, 1]
                a, r1, r2, t1, t2 = (tmp[par][:, n, :] for n in range(5))
                count = [0]

                def step(ins):
                    count[0] += 1
                    ins.then_inc(small, 1)
                    pool.wait_ge(small, 7 * i + count[0])

                pool.wait_ge(front.mv_done, i + 1)
                wait(pool, front.xn_done, i - 1)
                wait(pool, n_done, i - 1)
                step(pool.tensor_tensor(a, var, consts["eps"], ALU.add))
                step(pool.tensor_tensor(r1, a, consts["mhalf"], ALU.pow))
                step(pool.tensor_tensor(t1, r1, r1, ALU.mult))
                step(pool.tensor_tensor(t2, t1, var, ALU.mult))
                step(pool.tensor_tensor(a, t2, consts["eps"], ALU.add))
                step(pool.tensor_tensor(r2, a, consts["mhalf"], ALU.pow))
                step(pool.tensor_tensor(res[par][:, :], a, r2, ALU.mult))
                pool.tensor_tensor(front.rs[par][:, :], r1, r2, ALU.mult).then_inc(front.rs_done, 1)

            def keep(p, par):
                i = 2 * p + par
                pool.wait_ge(front.xn_done, i + 1)
                wait(pool, z_done, i - 1)
                pool.tensor_tensor(n_res[par][:, :, :], front.xn[par][:, :, :],
                                   res[par][:, :].unsqueeze(2).broadcast_to([P, TT, D]), ALU.mult).then_inc(n_done, 1)

            rstd(0, 0)
            rstd(0, 1)
            keep(0, 0)

            def body(p, par, first, last):
                if not last:
                    keep(*after(p, par))
                if not (isinstance(p, int) and p == END - 1):
                    rstd(p + 1, par)

            rounds(pool, NBLK, body)

        @block.scalar
        def _(act):
            def take(p, par):
                i = 2 * p + par
                act.wait_ge(front.turned, i + 1)
                wait(act, hlo_done, i)
                for h in range(DH):
                    last_ = act.activation(hf[:, h, :], pA[h][:, :], ACT.Identity, bias=gb[:, 1, h:h + 1],
                                           scale=gb[:, 0, h:h + 1])
                last_.then_inc(hf_done, 1)
                act.wait_ge(hf_done, i + 1)
                wait(act, kv_mm, TT * i)
                act.activation(hp[0][:, :, :], hf[:, :, :], ACT.Identity).then_inc(hhi_done, 1)

            def queries(p, par):
                i = 2 * p + par
                act.wait_ge(q_mm, i + 1)
                wait(act, y_mm, TT * (i - 1))
                for h in range(DH):
                    last_ = act.activation(qT[par][:, h, :], pA[h][:, :], ACT.Identity)
                last_.then_inc(q_ev, 1)

            def keys(p, par):
                i = 2 * p + par
                act.wait_ge(k_mm, i + 1)
                wait(act, s_mm, 4 * TT * (i - 1))
                for h in range(DH):
                    for o in range(QUAD):
                        last_ = act.activation(kE[par][o][:, h, :], pA[h][:, :], ACT.Identity,
                                               scale=quarter[:, o:o + 1])
                last_.then_inc(k_ev, 1)

            def output(p, par, t):
                i = 2 * p + par
                act.wait_ge(y_mm, TT * i + t + 1)
                if t == 0:
                    wait(act, yT_mm, i)
                act.activation(ys[:, t, :], pY[:, 0:D], ACT.Identity).then_inc(y_ev, 1)

            def high(p, par):
                i = 2 * p + par
                act.wait_ge(yT_mm, i + 1)
                wait(act, o_mm, i)
                for h in range(DH):
                    last_ = act.activation(yp[0][:, h, :], pA[h][:, :], ACT.Identity)
                last_.then_inc(yhi_done, 1)

            take(0, 0)
            queries(0, 0)
            keys(0, 0)

            def body(p, par, first, last):
                if not last:
                    take(*after(p, par))
                if not first:
                    output(*before(p, par), TT - 1)
                    high(*before(p, par))
                output(p, par, 0)
                if not last:
                    queries(*after(p, par))
                output(p, par, 1)
                if not last:
                    keys(*after(p, par))
                output(p, par, 2)

            rounds(act, NBLK, body)
            output(END - 1, 1, TT - 1)
            high(END - 1, 1)

        @block.vector
        def _(dve):
            def low(p, par):
                i = 2 * p + par
                dve.wait_ge(hf_done, i + 1)
                dve.wait_ge(hhi_done, i + 1)
                wait(dve, kv_mm, TT * i)
                dve.tensor_tensor(hp[1][:, :, :], hf[:, :, :], hp[0][:, :, :].bitcast(F32),
                                  ALU.subtract).then_inc(hlo_done, 1)

            def keep_kv(p, par, t):
                i = 2 * p + par
                dve.wait_ge(kv_mm, TT * i + t + 1)
                if t == 0:
                    wait(dve, y_mm, TT * (i - 1))
                dve.tensor_copy(kv[par][:, t, :], pA[t % 2][:, :]).then_inc(kv_ev, 1)

            def scores(p, par, t):
                c = TT * (2 * p + par) + t
                wait(dve, y_mm, c - 1)
                for j in range(4):
                    dve.wait_ge(s_mm, 4 * c + j + 1)
                    mask = causal[:, :].unsqueeze(1).broadcast_to([P, QUAD, P])
                    dve.tensor_tensor(sT[t % 2][:, j, :, :], pS[j][:, :, :], mask, ALU.mult).then_inc(s_ev, 1)

            def keep_state(p, par, t):
                if par == 1 and t == TT - 1:
                    return
                dve.wait_ge(m_mm, states(p, par, t) + 1)
                dve.tensor_tensor(state[t % 2][:, :, :],
                                  pM[:, 0:DH * P].rearrange("p (a b) -> p a b", a=DH),
                                  same[:, :, :], ALU.mult).then_inc(m_ev, 1)

            def y_low(p, par):
                i = 2 * p + par
                dve.wait_ge(yhi_done, i + 1)
                wait(dve, o_mm, i)
                for h in range(DH):
                    last_ = dve.tensor_tensor(yp[1][:, h, :], pA[h][:, :], yp[0][:, h, :].bitcast(F32), ALU.subtract)
                last_.then_inc(ylo_done, 1)

            def total(p, par):
                i = 2 * p + par
                dve.wait_ge(o_mm, i + 1)
                dve.wait_ge(n_done, i + 1)
                wait(dve, stored[par], 16 * p)
                for h in range(2):
                    last_ = dve.tensor_tensor(z[par][:, 2 * h:2 * h + 2, :],
                                              pA[h][:, :].rearrange("p (t d) -> p t d", t=2),
                                              n_res[par][:, 2 * h:2 * h + 2, :], ALU.add)
                last_.then_inc(z_done, 1)

            for b in range(2):
                front.stats(dve, 0, b)
                front.norm(dve, 0, b)
            low(0, 0)
            for t in range(TT):
                keep_kv(0, 0, t)

            def body(p, par, first, last):
                ahead = not (isinstance(p, int) and p == END - 1)
                scores(p, par, 0)
                keep_state(p, par, 0)
                if ahead:
                    front.stats(dve, p + 1, par)
                if not last:
                    low(*after(p, par))
                scores(p, par, 1)
                if not first:
                    y_low(*before(p, par))
                keep_state(p, par, 1)
                scores(p, par, 2)
                if not first:
                    total(*before(p, par))
                keep_state(p, par, 2)
                if ahead:
                    front.norm(dve, p + 1, par)
                scores(p, par, 3)
                if not last:
                    keep_kv(*after(p, par), 0)
                    keep_kv(*after(p, par), 1)
                keep_state(p, par, 3)
                if not last:
                    keep_kv(*after(p, par), 2)
                    keep_kv(*after(p, par), 3)

            rounds(dve, NBLK, body)
            y_low(END - 1, 1)
            total(END - 1, 1)

        @block.tensor
        def _(pe):
            def turn(p, par):
                wait(pe, kv_ev, TT * (2 * p + par))
                front.turn(pe, pA, p, par)

            def feature_major(p, par, name, done, emptied):
                i = 2 * p + par
                for sem, value in emptied:
                    wait(pe, sem, value)
                pe.wait_ge(hf_done, i + 1)
                pe.wait_ge(hlo_done, i + 1)
                for m in range(DH):
                    for k in range(DH):
                        mm = three_pass(pe, pA[m][:, :], tuple(x[:, k, m * P:(m + 1) * P] for x in w[name]),
                                        tuple(x[:, k, :] for x in hp), k == 0, k == DH - 1)
                mm.then_inc(done, 1)

            def token_major(p, par, t):
                i = 2 * p + par
                if t < 2:
                    pe.wait_ge(k_ev, i + 1)
                else:
                    pe.wait_ge(kv_ev, TT * i + t - 1)
                ts = slice(t * P, (t + 1) * P)
                for k in range(DH):
                    mm = three_pass(pe, pA[t % 2][:, :], tuple(x[:, k, ts] for x in hp),
                                    tuple(x[:, k, :] for x in wkv), k == 0, k == DH - 1)
                mm.then_inc(kv_mm, 1)

            def scores(p, par, t):
                i = 2 * p + par
                c = TT * i + t
                ts = slice(t * P, (t + 1) * P)
                if t == 0:
                    pe.wait_ge(q_ev, i + 1)
                    pe.wait_ge(k_ev, i + 1)
                for h in range(DH):
                    for g in range(2):
                        j = 2 * h + g
                        js = slice(64 * g, 64 * (g + 1))
                        wait(pe, s_ev, 4 * (c - 1) + j + 1)
                        for o in range(QUAD):
                            mm = pe.matmul(pS[j][:, o, :], kE[par][o][js, h, ts], qT[par][js, h, ts],
                                           start=True, stop=True)
                        mm.then_inc(s_mm, 1)

            def add_state(p, par, t):
                if par == 1 and t == TT - 1:
                    return
                wait(pe, m_ev, states(p, par, t))
                if t == 0:
                    pe.wait_ge(kv_ev, TT * (2 * p + par + 1))
                for h in range(DH):
                    hs = slice(h * P, (h + 1) * P)
                    mm = pe.matmul(pM[:, hs], kv[par][:, t, hs], kv[par][:, t, D + h * P:D + (h + 1) * P],
                                   start=(par == 0 and t == 0 and h == 0), stop=True, skip_group_check=True)
                mm.then_inc(m_mm, 1)

            def output(p, par, t):
                c = TT * (2 * p + par) + t
                ts = slice(t * P, (t + 1) * P)
                wait(pe, y_ev, c)
                begun = False
                if not (par == 0 and t == 0):
                    pe.wait_ge(m_ev, states(p, par, t))
                    for h in range(DH):
                        pe.matmul(pY[:, h * P:(h + 1) * P], qT[par][:, h, ts], state[(t - 1) % 2][:, h, :],
                                  start=not begun, stop=False, skip_group_check=True)
                        begun = True
                for j in range(4):
                    pe.wait_ge(s_ev, 4 * c + j + 1)
                    for o in range(QUAD):
                        head = QUAD * j + o
                        vs = slice(head * HD, (head + 1) * HD)
                        mm = pe.matmul(pY[:, vs], sT[t % 2][:, j, o, :],
                                       kv[par][:, t, D + head * HD:D + (head + 1) * HD],
                                       start=not begun, stop=True, skip_group_check=True)
                        begun = True
                mm.then_inc(y_mm, 1)

            def turn_y(p, par):
                i = 2 * p + par
                wait(pe, hf_done, min(i + 3, NBLK) if isinstance(i, int) else i + 3)
                pe.wait_ge(y_ev, TT * (i + 1))
                for h in range(DH):
                    for t in range(TT):
                        mm = pe.transpose(pA[h][:, t * P:(t + 1) * P], ys[:, t, h * P:(h + 1) * P],
                                          consts["ident"][:, :])
                mm.then_inc(yT_mm, 1)

            def project_out(p, par):
                i = 2 * p + par
                pe.wait_ge(ylo_done, i + 1)
                wait(pe, q_ev, min(i + 3, NBLK) if isinstance(i, int) else i + 3)
                for t in range(TT):
                    po = pA[t // 2][:, (t % 2) * D:(t % 2 + 1) * D]
                    ts = slice(t * P, (t + 1) * P)
                    for k in range(DH):
                        mm = three_pass(pe, po, tuple(x[:, k, ts] for x in yp),
                                        tuple(x[:, k, :] for x in w["o"]), k == 0, k == DH - 1)
                mm.then_inc(o_mm, 1)

            turn(0, 0)
            feature_major(0, 0, "q", q_mm, [])
            feature_major(0, 0, "k", k_mm, [(q_ev, 1)])
            for t in range(TT):
                token_major(0, 0, t)

            def body(p, par, first, last):
                i = 2 * p + par
                nxt = after(p, par)
                prv = None if first else before(p, par)
                scores(p, par, 0)
                if not last:
                    turn(*nxt)
                if prv:
                    output(*prv, TT - 1)
                add_state(p, par, 0)
                scores(p, par, 1)
                if prv:
                    turn_y(*prv)
                output(p, par, 0)
                add_state(p, par, 1)
                if not last:
                    feature_major(*nxt, "q", q_mm, [(ylo_done, i)])
                scores(p, par, 2)
                if prv:
                    project_out(*prv)
                output(p, par, 1)
                add_state(p, par, 2)
                if not last:
                    feature_major(*nxt, "k", k_mm, [(z_done, i), (q_ev, i + 2)])
                scores(p, par, 3)
                if not last:
                    token_major(*nxt, 0)
                    token_major(*nxt, 1)
                output(p, par, 2)
                add_state(p, par, 3)
                if not last:
                    token_major(*nxt, 2)
                    token_major(*nxt, 3)

            rounds(pe, NBLK, body)
            output(END - 1, 1, TT - 1)
            turn_y(END - 1, 1)
            project_out(END - 1, 1)


HID = 1024
FT = HID // P
RING = 4


class Hidden:

    def __init__(self, ph):
        self.g = [ph.sb(f"g{n}", [P, BLK]) for n in range(RING)]
        self.gp = [ph.pair(f"gp{n}", [P, BLK]) for n in range(RING)]
        self.pg = [ph.ps(f"pg{n}", [P, BLK]) for n in range(RING)]
        self.mm = ph.sem("hid_mm")
        self.g_done = ph.sem("hid_gelu")
        self.hi_done = ph.sem("hid_hi")
        self.lo_done = ph.sem("hid_lo")
        self.used = ph.sem("hid_used")

    def up(self, pe, n, f, w, h, waits):
        s = f % RING
        for sem, value in waits:
            wait(pe, sem, value)
        wait(pe, self.g_done, n - RING + 1)
        for k in range(DH):
            mm = three_pass(pe, self.pg[s][:, :], tuple(x[:, k, f * P:(f + 1) * P] for x in w),
                            tuple(x[:, k, :] for x in h), k == 0, k == DH - 1)
        mm.then_inc(self.mm, 1)

    def gelu(self, act, n, f, bias):
        s = f % RING
        act.wait_ge(self.mm, n + 1)
        wait(act, self.lo_done, n - RING + 1)
        act.activation(self.g[s][:, :], self.pg[s][:, :], ACT.Gelu_apprx_tanh, bias=bias).then_inc(self.g_done, 1)

    def high(self, act, n, f):
        s = f % RING
        act.wait_ge(self.g_done, n + 1)
        wait(act, self.used, n - RING + 1)
        act.activation(self.gp[s][0][:, :], self.g[s][:, :], ACT.Identity).then_inc(self.hi_done, 1)

    def low(self, dve, n, f):
        s = f % RING
        dve.wait_ge(self.hi_done, n + 1)
        wait(dve, self.used, n - RING + 1)
        dve.tensor_tensor(self.gp[s][1][:, :], self.g[s][:, :], self.gp[s][0][:, :].bitcast(F32),
                          ALU.subtract).then_inc(self.lo_done, 1)

    def down(self, pe, n, f, w, banks):
        s = f % RING
        pe.wait_ge(self.lo_done, n + 1)
        for m in range(DH):
            mm = three_pass(pe, banks[m][:, :], tuple(x[:, f, m * P:(m + 1) * P] for x in w),
                            tuple(x[:, :] for x in self.gp[s]), f == 0, f == FT - 1)
        mm.then_inc(self.used, 1)
        return mm

    def down_tokens(self, pe, n, f, w, banks):
        s = f % RING
        pe.wait_ge(self.lo_done, n + 1)
        for t in range(TT):
            out = banks[t // 2][:, (t % 2) * D:(t % 2 + 1) * D]
            ts = slice(t * P, (t + 1) * P)
            (xh, xl), (wh, wl) = (x[:, ts] for x in self.gp[s]), (x[:, f, :] for x in w)
            first = f == 0 and t % 2 == 0
            pe.matmul(out, xl, wh, start=first, stop=False, skip_group_check=True)
            pe.matmul(out, xh, wl, start=False, stop=False, skip_group_check=True)
            mm = pe.matmul(out, xh, wh, start=False, stop=f == FT - 1, skip_group_check=True)
        mm.then_inc(self.used, 1)
        return mm


LEVELS = 3


def gelu_levels(nc, x_dram, n_dram, y_dram, consts, ln_g, ln_b, w1_d, b1_d, w2_d, b2_d, b2row_d):
    with ExitStack() as ctx:
        ph = Phase(nc, ctx, "gl")
        w1 = [ph.pair(f"w1_{l}", [P, DH, HID]) for l in range(LEVELS)]
        w2 = [ph.pair(f"w2_{l}", [P, FT, D]) for l in range(LEVELS)]
        gb = ph.sb("gb", [P, 2, DH])
        b1 = ph.sb("b1", [P, LEVELS, FT])
        b2 = ph.sb("b2", [P, LEVELS, DH])
        b2row = ph.sb("b2row", [P, D])
        flat = lambda t: tuple(x[:, :, :].rearrange("p a b -> p (a b)") for x in t)
        split = []
        for l in range(LEVELS):
            split += [(flat(w1[l]), w1_d[l]), (flat(w2[l]), w2_d[l])]
        load_weights(nc, "gll",
                     [(gb[:, 0, :], ln_g), (gb[:, 1, :], ln_b),
                      (b1[:, :, :].rearrange("p a b -> p (a b)"), b1_d),
                      (b2[:, :, :].rearrange("p a b -> p (a b)"), b2_d),
                      (b2row[:, :], b2row_d.unsqueeze(0).broadcast_to([P, D]))], split)
        front = Front(ph, n_dram, consts["ident"])
        back = Back(ph, front, y_dram)
        back.front = None
        xres = [ph.sb(f"xres{b}", [P, TT, D]) for b in range(2)]
        hf = [ph.sb(f"hf{b}", [P, DH, BLK]) for b in range(2)]
        hp = [ph.pair(f"hp{b}", [P, DH, BLK]) for b in range(2)]
        hid = Hidden(ph)
        pT = [ph.ps(f"pT{h}", [P, BLK]) for h in range(DH)]
        pH = [ph.ps(f"pH{h}", [P, BLK]) for h in range(DH)]
        xres_loaded = [ph.sem(f"xres_loaded{b}") for b in range(2)]
        moved = ph.sem("moved")
        hf_done = [ph.sem(f"hf{b}") for b in range(2)]
        hhi_done = [ph.sem(f"hhi{b}") for b in range(2)]
        hlo_done = [ph.sem(f"hlo{b}") for b in range(2)]
        z_done = ph.sem("z")
        block = ctx.enter_context(nc.Block())
        PAIRSOF = NBLK // 2

        def passes(eng, body):
            body(0, True, False)
            with eng.Fori(1, PAIRSOF - 1) as p:
                body(p, False, False)
            body(PAIRSOF - 1, False, True)

        def order(p):
            for l in range(LEVELS):
                for b in range(2):
                    yield 2 * LEVELS * p + 2 * l + b, l, b

        @block.sync
        def _(sp):
            def load_res(p, b):
                src = x_dram[bass.ds((2 * p + b) * BLK, BLK), :].rearrange("(t p) d -> p t d", p=P)
                sp.dma_start(xres[b][:, :, :], src).then_inc(xres_loaded[b], 16)

            for b in range(2):
                front.load(sp, 0, b)
            for b in range(2):
                load_res(0, b)

            def body(p, first, last):
                if not first:
                    back.store(sp, p - 1, 1)
                    load_res(p, 1)
                if not last:
                    for b in range(2):
                        sp.wait_ge(moved, 2 * p + b + 1)
                        front.load(sp, p + 1, b)
                back.store(sp, p, 0)
                if not last:
                    load_res(p + 1, 0)

            passes(sp, body)
            back.store(sp, PAIRSOF - 1, 1)
            back.all_stored(sp)

        @block.gpsimd
        def _(pool):
            def finish(p, b):
                back.rstd(pool, consts, p, b)
                pool.wait_ge(back.zn_done, 2 * p + b + 1)
                pool.wait_ge(xres_loaded[b], 16 * (p + 1))
                pool.tensor_tensor(back.z[b][:, :, :], back.z[b][:, :, :], xres[b][:, :, :],
                                   ALU.add).then_inc(back.added, 1)

            for b in range(2):
                front.rstd(pool, consts, 0, b)

            def body(p, first, last):
                if not first:
                    finish(p - 1, 1)
                for b in range(2):
                    pool.wait_ge(front.loaded[b], 16 * (p + 1))
                    back.z_free(pool, p, b)
                    pool.wait_ge(front.xn_done, 2 * p + b + 1)
                    pool.tensor_tensor(back.z[b][:, :, :], front.x[b][:, :, :],
                                       b2row[:, :].unsqueeze(1).broadcast_to([P, TT, D]), ALU.add).then_inc(moved, 1)
                if not last:
                    for b in range(2):
                        front.rstd(pool, consts, p + 1, b)
                finish(p, 0)

            passes(pool, body)
            finish(PAIRSOF - 1, 1)

        @block.scalar
        def _(act):
            def take(p, l, b):
                n = 3 * p + l
                if l == 0:
                    act.wait_ge(front.turned, 2 * p + b + 1)
                    banks = pT
                else:
                    act.wait_ge(hid.used, FT * (6 * p + 2 * (l - 1) + b + 1))
                    banks = pH
                wait(act, hlo_done[b], n)
                for h in range(DH):
                    if l == 0:
                        last_ = act.activation(hf[b][:, h, :], banks[h][:, :], ACT.Identity,
                                               bias=gb[:, 1, h:h + 1], scale=gb[:, 0, h:h + 1])
                    else:
                        last_ = act.activation(hf[b][:, h, :], banks[h][:, :], ACT.Identity,
                                               bias=b2[:, l - 1, h:h + 1])
                last_.then_inc(hf_done[b], 1)

            def high(p, l, b):
                n = 3 * p + l
                act.wait_ge(hf_done[b], n + 1)
                wait(act, hid.mm, FT * (2 * (3 * p + l - 1) + b + 1))
                act.activation(hp[b][0][:, :, :], hf[b][:, :, :], ACT.Identity).then_inc(hhi_done[b], 1)

            def body(p, first, last):
                if first:
                    take(0, 0, 0)
                    high(0, 0, 0)
                for o, l, b in order(p):
                    prev = (l, 0) if b else (l - 1, 1)
                    moves = prev[0] in range(LEVELS - 1)
                    if moves:
                        take(p, prev[0] + 1, prev[1])
                    for f in range(FT):
                        hid.gelu(act, FT * o + f, f, b1[:, l, f:f + 1])
                        hid.high(act, FT * o + f, f)
                        if f == 0 and moves:
                            high(p, prev[0] + 1, prev[1])
                        if f == 1 and (l, b) == (0, 0):
                            take(p, 0, 1)
                            high(p, 0, 1)
                        if f == 1 and (l, b) == (LEVELS - 1, 1) and not last:
                            take(p + 1, 0, 0)
                            high(p + 1, 0, 0)

            passes(act, body)

        @block.vector
        def _(dve):
            def halves(p, l, b):
                n = 3 * p + l
                dve.wait_ge(hf_done[b], n + 1)
                dve.wait_ge(hhi_done[b], n + 1)
                wait(dve, hid.mm, FT * (2 * (3 * p + l - 1) + b + 1))
                dve.tensor_tensor(hp[b][1][:, :, :], hf[b][:, :, :], hp[b][0][:, :, :].bitcast(F32),
                                  ALU.subtract).then_inc(hlo_done[b], 1)

            def out(p, b):
                dve.wait_ge(hid.used, FT * (6 * p + 4 + b + 1))
                dve.wait_ge(moved, 2 * p + b + 1)
                for h in range(2):
                    zz = back.z[b][:, 2 * h:2 * h + 2, :]
                    last_ = dve.tensor_tensor(zz, pH[h][:, :].rearrange("p (a b) -> p a b", a=2), zz, ALU.add)
                last_.then_inc(z_done, 1)

            def body(p, first, last):
                if first:
                    for b in range(2):
                        front.stats(dve, 0, b)
                        front.norm(dve, 0, b)
                    halves(0, 0, 0)
                for o, l, b in order(p):
                    prev = (l, 0) if b else (l - 1, 1)
                    ends = None
                    if (l, b) == (0, 0) and not first:
                        ends = (p - 1, 1)
                    if (l, b) == (LEVELS - 1, 1):
                        ends = (p, 0)
                    if ends:
                        out(*ends)
                    for f in range(FT):
                        hid.low(dve, FT * o + f, f)
                        if f == 0 and prev[0] in range(LEVELS - 1):
                            halves(p, prev[0] + 1, prev[1])
                        if f == 1 and ends:
                            back.stats(dve, z_done, 2 * ends[0] + ends[1] + 1, *ends)
                        if f == 2 and (l, b) == (0, 0):
                            halves(p, 0, 1)
                        if f == 2 and (l, b) == (LEVELS - 1, 1) and not last:
                            halves(p + 1, 0, 0)
                        if f == 4 and ends:
                            back.norm(dve, *ends)
                        if l == 1 and f == 2 and not last:
                            front.stats(dve, p + 1, b)
                        if l == 1 and f == 5 and not last:
                            front.norm(dve, p + 1, b)

            passes(dve, body)
            out(PAIRSOF - 1, 1)
            back.stats(dve, z_done, 2 * PAIRSOF, PAIRSOF - 1, 1)
            back.norm(dve, PAIRSOF - 1, 1)

        @block.tensor
        def _(pe):
            LAG = 3

            def body(p, first, last):
                if first:
                    front.turn(pe, pT, 0, 0)
                    pe.wait_ge(hf_done[0], 1)
                    front.turn(pe, pT, 0, 1)
                for o, l, b in order(p):
                    for f in range(FT + LAG):
                        if f == 4 and l == LEVELS - 1 and not last:
                            if b == 0:
                                pe.wait_ge(hf_done[1], 3 * p + 1)
                            else:
                                pe.wait_ge(hf_done[0], 3 * (p + 1) + 1)
                            front.turn(pe, pT, p + 1, b)
                        if f < FT:
                            waits = [(hf_done[b], 3 * p + l + 1), (hlo_done[b], 3 * p + l + 1)] if f == 0 else []
                            hid.up(pe, FT * o + f, f, w1[l], hp[b], waits)
                        g = f - LAG
                        if g == 0:
                            if (l, b) == (0, 0):
                                wait(pe, z_done, 2 * p)
                            elif (l, b) == (LEVELS - 1, 1):
                                pe.wait_ge(z_done, 2 * p + 1)
                            elif b == 1:
                                pe.wait_ge(hf_done[0], 3 * p + l + 2)
                            else:
                                pe.wait_ge(hf_done[1], 3 * p + l + 1)
                        if g >= 0:
                            if l < LEVELS - 1:
                                hid.down(pe, FT * o + g, g, w2[l], pH)
                            else:
                                hid.down_tokens(pe, FT * o + g, g, w2[l], pH)

            passes(pe, body)


EXPERTS = 8
GROUP = P // EXPERTS
GROUPS = 2 * D * HID // (GROUP * HID)


def expert_weights(nc, x_dram, consts, shared, mw_dram, tw_d, base_d, gw1_d, gb1_d, gw2_d, gb2_d, esel_d,
                   delta_d, spread_d, tb1_d, b1_d, tb2_d, b2_d):
    mb1, mb2 = shared
    with ExitStack() as ctx:
        ph = Phase(nc, ctx, "eg")
        gw1 = ph.sb("gw1", [P, DH, D])
        gb1 = ph.sb("gb1", [P, DH])
        gw2 = ph.sb("gw2", [P, DH, EXPERTS])
        gb2 = ph.sb("gb2", [EXPERTS, 1])
        esel = ph.sb("esel", [EXPERTS, P])
        delta = ph.sb("delta", [P, GROUP])
        spread = ph.sb("spread", [GROUP, P])
        tb1 = ph.sb("tb1", [EXPERTS, HID])
        b1 = ph.sb("b1", [P, FT])
        tb2 = ph.sb("tb2", [EXPERTS, D])
        b2 = ph.sb("b2", [1, D])
        hsum = ph.sb("hsum", [P, NBLK, DH])
        mix = ph.sb("mix", [P, BATCH, GROUP])
        load_weights(nc, "egl", [
            (gw1[:, :, :].rearrange("p a b -> p (a b)"), gw1_d), (gb1[:, :], gb1_d),
            (gw2[:, :, :].rearrange("p a b -> p (a b)"), gw2_d), (gb2[:, :], gb2_d), (esel[:, :], esel_d),
            (delta[:, :], delta_d), (spread[:, :], spread_d), (tb1[:, :], tb1_d), (b1[:, :], b1_d),
            (tb2[:, :], tb2_d), (b2[:, :], b2_d)], [])

        with ExitStack() as inner:
            gp = Phase(nc, inner, "g1")
            front = Front(gp, x_dram, consts["ident"])
            xT = [gp.sb(f"xT{b}", [P, DH, BLK]) for b in range(2)]
            junk = [gp.sb(f"junk{n}", [P, BLK]) for n in range(2 * DH)]
            accs = [gp.sb(f"acc{b}", [P, DH]) for b in range(2)]
            pT = [gp.ps(f"pT{h}", [P, BLK]) for h in range(DH)]
            pG = [gp.ps(f"pG{h}", [P, BLK]) for h in range(2 * DH)]
            xT_done, g_mm, summed, kept = gp.sem("xT"), gp.sem("g_mm"), gp.sem("summed"), gp.sem("kept")
            block = inner.enter_context(nc.Block())

            @block.sync
            def _(sp):
                front.load(sp, 0, 0)
                front.load(sp, 0, 1)

                def body(p, par, first, last):
                    if not (isinstance(p, int) and p == NBLK // 2 - 1):
                        sp.wait_ge(front.xn_done, 2 * p + par + 1)
                        front.load(sp, p + 1, par)

                rounds(sp, NBLK, body)

            @block.gpsimd
            def _(pool):
                rounds(pool, NBLK, lambda p, par, first, last: front.rstd(pool, consts, p, par))

            @block.scalar
            def _(act):
                def take(p, par):
                    i = 2 * p + par
                    act.wait_ge(front.turned, i + 1)
                    wait(act, g_mm, i - 1)
                    for h in range(DH):
                        last_ = act.activation(xT[par][:, h, :], pT[h][:, :], ACT.Identity)
                    last_.then_inc(xT_done, 1)

                take(0, 0)

                def body(p, par, first, last):
                    i = 2 * p + par
                    if not last:
                        take(*after(p, par))
                    act.wait_ge(g_mm, i + 1)
                    wait(act, kept, i - 1)
                    for h in range(DH):
                        last_ = act.activation(junk[DH * par + h][:, :], pG[DH * par + h][:, :], ACT.Relu, bias=gb1[:, h:h + 1],
                                               accum_out=accs[par][:, h:h + 1])
                    last_.then_inc(summed, 1)

                rounds(act, NBLK, body)

            @block.vector
            def _(dve):
                front.stats(dve, 0, 0)
                front.norm(dve, 0, 0)

                def body(p, par, first, last):
                    i = 2 * p + par
                    if not last:
                        front.stats(dve, *after(p, par))
                        front.norm(dve, *after(p, par))
                    dve.wait_ge(summed, i + 1)
                    dve.tensor_copy(hsum[:, bass.ds(i, 1), :], accs[par][:, :].unsqueeze(1)).then_inc(kept, 1)

                rounds(dve, NBLK, body)

            @block.tensor
            def _(pe):
                front.turn(pe, pT, 0, 0)

                def body(p, par, first, last):
                    i = 2 * p + par
                    pe.wait_ge(xT_done, i + 1)
                    if not last:
                        front.turn(pe, pT, *after(p, par))
                    wait(pe, summed, i - 1)
                    for m in range(DH):
                        for k in range(DH):
                            mm = pe.matmul(pG[DH * par + m][:, :], gw1[:, k, m * P:(m + 1) * P], xT[par][:, k, :],
                                           start=k == 0, stop=k == DH - 1)
                    mm.then_inc(g_mm, 1)

                rounds(pe, NBLK, body)

        with ExitStack() as inner:
            gp = Phase(nc, inner, "g2")
            hm = gp.sb("hm", [P, DH, BATCH])
            gT = gp.sb("gT", [EXPERTS, BATCH])
            gP = gp.sb("gP", [P, BATCH])
            gB = gp.sb("gB", [EXPERTS, BATCH, P])
            ones = gp.sb("ones", [EXPERTS, P])
            pg = gp.ps("pg", [P, BATCH])
            pe_ = gp.ps("pe", [P, BATCH])
            pb = gp.ps("pb", [P, FT, BATCH])
            pc = [gp.ps(f"pc{n}", [P, 2, D]) for n in range(BATCH // 2)]
            v, t = gp.sem("v"), gp.sem("t")
            block = inner.enter_context(nc.Block())

            @block.vector
            def _(dve):
                dve.memset(ones[:, :], 1.0).then_inc(v, 1)
                pairs = hsum[:, :, :].rearrange("p (b two) h -> p h b two", two=SEQ // BLK)
                dve.tensor_tensor(hm[:, :, :], pairs[:, :, :, 0], pairs[:, :, :, 1], ALU.add).then_inc(v, 1)
                dve.wait_ge(t, 1)
                dve.tensor_scalar(gT[:, :], pg[0:EXPERTS, :], 1.0 / SEQ, gb2[:, 0:1], ALU.mult,
                                  ALU.add).then_inc(v, 1)
                dve.wait_ge(v, 3)
                for b in range(BATCH):
                    last = dve.tensor_scalar(gB[:, b, :], ones[:, :], gT[:, b:b + 1], None, ALU.mult)
                last.then_inc(v, 1)
                dve.wait_ge(t, 2)
                dve.tensor_copy(gP[:, :], pe_[:, :]).then_inc(v, 1)
                dve.wait_ge(v, 5)
                for b in range(BATCH):
                    last = dve.tensor_scalar(mix[:, b, :], delta[:, :], gP[:, b:b + 1], None, ALU.mult)
                last.then_inc(v, 1)
                dve.wait_ge(t, 3)
                dve.tensor_tensor(mb1[:, :, :], pb[:, :, :].rearrange("p f b -> p b f"),
                                  b1[:, :].unsqueeze(1).broadcast_to([P, BATCH, FT]), ALU.add).then_inc(v, 1)
                dve.wait_ge(t, 4)
                for n in range(BATCH // 2):
                    last = dve.tensor_copy(mb2[:, 2 * n:2 * n + 2, :], pc[n][:, :, :])
                last.then_inc(v, 1)

            @block.tensor
            def _(pe):
                pe.wait_ge(v, 2)
                for h in range(DH):
                    mm = pe.matmul(pg[0:EXPERTS, :], gw2[:, h, :], hm[:, h, :], start=h == 0, stop=h == DH - 1)
                mm.then_inc(t, 1)
                pe.wait_ge(v, 3)
                pe.matmul(pe_[:, :], esel[:, :], gT[:, :], start=True, stop=True).then_inc(t, 1)
                for f in range(FT):
                    mm = pe.matmul(pb[:, f, :], tb1[:, f * P:(f + 1) * P], gT[:, :], start=True, stop=True)
                mm.then_inc(t, 1)
                pe.wait_ge(v, 4)
                for b in range(BATCH):
                    out = pc[b // 2][:, b % 2, :]
                    pe.matmul(out, gB[:, b, :], tb2[:, :], start=True, stop=False)
                    mm = pe.matmul(out, ones[0:1, :], b2[:, :], start=False, stop=True)
                mm.then_inc(t, 1)

        with ExitStack() as inner:
            gp = Phase(nc, inner, "g3")
            tw = [gp.sb(f"tw{b}", [P, HID]) for b in range(2)]
            base = [gp.sb(f"base{b}", [GROUP, HID]) for b in range(2)]
            mw = [gp.sb(f"mw{b}", [P, HID]) for b in range(2)]
            pw = [gp.ps(f"pw{n}", [P, BLK]) for n in range(4)]
            loaded = [gp.sem(f"loaded{b}") for b in range(2)]
            stored = [gp.sem(f"stored{b}") for b in range(2)]
            mm_done, ev_act, ev_dve = gp.sem("mm"), gp.sem("ev_act"), gp.sem("ev_dve")
            block = inner.enter_context(nc.Block())

            @block.sync
            def _(sp):
                def body(p, par, first, last):
                    i = 2 * p + par
                    wait(sp, mm_done, i - 1)
                    sp.dma_start(tw[par][:, :], tw_d[bass.ds(i * P, P), :]).then_inc(loaded[par], 16)
                    sp.dma_start(base[par][:, :], base_d[bass.ds(i * GROUP, GROUP), :]).then_inc(loaded[par], 16)

                rounds(sp, GROUPS, body)

            @block.gpsimd
            def _(pool):
                def body(p, par, first, last):
                    i = 2 * p + par
                    pool.wait_ge(ev_act, i + 1)
                    pool.wait_ge(ev_dve, i + 1)
                    dst = mw_dram[:, bass.ds(i * GROUP, GROUP), :]
                    pool.dma_start(dst, mw[par][:, :]).then_inc(stored[par], 16)

                rounds(pool, GROUPS, body)
                for s in stored:
                    pool.wait_ge(s, 16 * GROUPS // 2)

            @block.scalar
            def _(act):
                def body(p, par, first, last):
                    i = 2 * p + par
                    act.wait_ge(mm_done, i + 1)
                    wait(act, stored[par], 16 * p)
                    act.activation(mw[par][:, 0:BLK], pw[2 * par][:, :], ACT.Identity).then_inc(ev_act, 1)

                rounds(act, GROUPS, body)

            @block.vector
            def _(dve):
                def body(p, par, first, last):
                    i = 2 * p + par
                    dve.wait_ge(mm_done, i + 1)
                    wait(dve, stored[par], 16 * p)
                    dve.tensor_copy(mw[par][:, BLK:HID], pw[2 * par + 1][:, :]).then_inc(ev_dve, 1)

                rounds(dve, GROUPS, body)

            @block.tensor
            def _(pe):
                def body(p, par, first, last):
                    i = 2 * p + par
                    pe.wait_ge(loaded[par], 32 * (p + 1))
                    wait(pe, ev_act, i - 1)
                    wait(pe, ev_dve, i - 1)
                    for n in range(2):
                        ns = slice(n * BLK, (n + 1) * BLK)
                        pe.matmul(pw[2 * par + n][:, :], mix[:, :, :].rearrange("p b h -> p (b h)"),
                                  tw[par][:, ns], start=True, stop=False)
                        mm = pe.matmul(pw[2 * par + n][:, :], spread[:, :], base[par][:, ns], start=False, stop=True)
                    mm.then_inc(mm_done, 1)

                rounds(pe, GROUPS, body)


def batch_mlp(nc, x_dram, y_dram, consts, shared, mw_dram):
    mb1, mb2 = shared
    with ExitStack() as ctx:
        ph = Phase(nc, ctx, "bm")
        front = Front(ph, x_dram, consts["ident"])
        back = Back(ph, front, y_dram)
        xres = [ph.sb(f"xres{b}", [P, TT, D]) for b in range(2)]
        hf = [ph.sb(f"hf{b}", [P, DH, BLK]) for b in range(2)]
        hp = [ph.pair(f"hp{b}", [P, DH, BLK]) for b in range(2)]
        raw = ph.sb("raw", [P, 4, HID])
        w1 = [ph.pair(f"w1{b}", [P, DH, HID]) for b in range(2)]
        w2 = [ph.pair(f"w2{b}", [P, FT, D]) for b in range(2)]
        hid = Hidden(ph)
        pT = [ph.ps(f"pT{h}", [P, BLK]) for h in range(DH)]
        pH = [ph.ps(f"pH{h}", [P, BLK]) for h in range(DH)]
        raw_loaded = ph.sem("raw_loaded")
        whi_done, wlo_done = ph.sem("whi"), ph.sem("wlo")
        kept = ph.sem("kept")
        bias = [ph.sb(f"bias{b}", [P, FT]) for b in range(2)]
        bias_done = ph.sem("bias")
        hf_done, hhi_done, hlo_done = ph.sem("hf"), ph.sem("hhi"), ph.sem("hlo")
        z_done = ph.sem("z")
        block = ctx.enter_context(nc.Block())
        PER = SEQ // BLK
        Q = 2 * PER
        PASSES = NBLK // Q

        def passes(eng, body):
            body(0, True, False)
            with eng.Fori(1, PASSES - 1) as p:
                body(p, False, False)
            body(PASSES - 1, False, True)

        def at(p, q):
            return 2 * p + q // 2, q % 2

        def pieces(b):
            out = []
            for h in range(DH):
                out.append(tuple(x[:, h, :] for x in w1[b]))
            for h in range(2):
                out.append(tuple(x[:, h * 4:(h + 1) * 4, :].rearrange("p a b -> p (a b)") for x in w2[b]))
            return out

        @block.sync
        def _(sp):
            def load_w(b):
                src = mw_dram[b, 0:D, :].rearrange("(k p) n -> p k n", p=P)
                sp.dma_start(raw[:, 0:2, :], src).then_inc(raw_loaded, 16)
                src = mw_dram[b, D:2 * D, :].rearrange("r (q d) -> (r q) d", d=D)
                src = src.rearrange("(f p) d -> p f d", p=P)
                dst = raw[:, 2:4, :].rearrange("p a (f d) -> p (a f) d", d=D)
                sp.dma_start(dst, src).then_inc(raw_loaded, 16)

            load_w(0)
            front.load(sp, 0, 0)
            front.load(sp, 0, 1)

            def body(p, first, last):
                for q in range(Q):
                    i = Q * p + q
                    if q % PER == 0 and not (last and q == PER):
                        sp.wait_ge(wlo_done, 4 * (2 * p + q // PER + 1))
                        load_w(2 * p + q // PER + 1)
                    if not (last and q >= Q - 2):
                        sp.wait_ge(kept, i + 1)
                        sp.wait_ge(front.xn_done, i + 1)
                        front.load(sp, at(p, q)[0] + 1, q % 2)
                    if not (first and q == 0):
                        back.store(sp, *before(*at(p, q)))

            passes(sp, body)
            back.store(sp, NBLK // 2 - 1, 1)
            back.all_stored(sp)

        @block.gpsimd
        def _(pool):
            front.rstd(pool, consts, 0, 0)
            front.rstd(pool, consts, 0, 1)

            def finish(pp, par):
                back.rstd(pool, consts, pp, par)
                pool.wait_ge(back.zn_done, 2 * pp + par + 1)
                pool.tensor_tensor(back.z[par][:, :, :], back.z[par][:, :, :], xres[par][:, :, :],
                                   ALU.add).then_inc(back.added, 1)

            def body(p, first, last):
                for q in range(Q):
                    i = Q * p + q
                    pp, par = at(p, q)
                    pool.wait_ge(front.loaded[par], 16 * (pp + 1))
                    wait(pool, back.added, i - 1)
                    pool.tensor_tensor(xres[par][:, :, :], front.x[par][:, :, :],
                                       consts["one"].unsqueeze(2).broadcast_to([P, TT, D]), ALU.mult).then_inc(kept, 1)
                    if not (first and q == 0):
                        finish(*before(pp, par))
                    if not (last and q >= Q - 2):
                        front.rstd(pool, consts, pp + 1, par)

            passes(pool, body)
            finish(NBLK // 2 - 1, 1)

        @block.scalar
        def _(act):
            def take(i, par):
                act.wait_ge(front.turned, i + 1)
                wait(act, hlo_done, i - 1)
                for h in range(DH):
                    last_ = act.activation(hf[par][:, h, :], pT[h][:, :], ACT.Identity)
                last_.then_inc(hf_done, 1)
                act.wait_ge(hf_done, i + 1)
                wait(act, hid.mm, FT * (i - 1))
                act.activation(hp[par][0][:, :, :], hf[par][:, :, :], ACT.Identity).then_inc(hhi_done, 1)

            def piece(batch, b, k):
                if k == 0:
                    act.wait_ge(raw_loaded, 32 * (batch + 1))
                    wait(act, hid.used, FT * PER * (batch - 1))
                act.activation(pieces(b)[k][0], raw[:, k, :], ACT.Identity).then_inc(whi_done, 1)

            for k in range(4):
                piece(0, 0, k)
            take(0, 0)

            def body(p, first, last):
                for q in range(Q):
                    i = Q * p + q
                    batch = 2 * p + q // PER
                    for f in range(FT):
                        if f == 0 and q % PER == 0:
                            act.wait_ge(bias_done, batch + 1)
                        hid.gelu(act, FT * i + f, f, bias[q // PER][:, f:f + 1])
                        hid.high(act, FT * i + f, f)
                        if f < 4 and q % PER == PER - 1 and not (last and q == Q - 1):
                            piece(batch + 1, (q // PER + 1) % 2, f)
                        if f == 5 and not (last and q == Q - 1):
                            take(i + 1, (q + 1) % 2)

            passes(act, body)

        @block.vector
        def _(dve):
            def halves(i, par):
                dve.wait_ge(hf_done, i + 1)
                dve.wait_ge(hhi_done, i + 1)
                wait(dve, hid.mm, FT * (i - 1))
                dve.tensor_tensor(hp[par][1][:, :, :], hf[par][:, :, :], hp[par][0][:, :, :].bitcast(F32),
                                  ALU.subtract).then_inc(hlo_done, 1)

            def piece(batch, b, k):
                dve.wait_ge(whi_done, 4 * batch + k + 1)
                if k == 0:
                    wait(dve, hid.used, FT * PER * (batch - 1))
                hi, lo = pieces(b)[k]
                dve.tensor_tensor(lo, raw[:, k, :], hi.bitcast(F32), ALU.subtract).then_inc(wlo_done, 1)

            def hidden_bias(batch, b):
                wait(dve, hid.g_done, FT * PER * (batch - 1))
                src = mb1[:, bass.ds(batch, 1), :].rearrange("p a f -> p (a f)")
                dve.tensor_tensor(bias[b][:, :], src, src, ALU.max).then_inc(bias_done, 1)

            def out(i, pp, par, batch):
                dve.wait_ge(hid.used, FT * (i + 1))
                back.z_free(dve, pp, par)
                for h in range(2):
                    bias = mb2[:, bass.ds(batch, 1), :] if not isinstance(batch, int) else mb2[:, batch:batch + 1, :]
                    last_ = dve.tensor_tensor(back.z[par][:, 2 * h:2 * h + 2, :],
                                              pH[h][:, :].rearrange("p (a b) -> p a b", a=2),
                                              bias.broadcast_to([P, 2, D]), ALU.add)
                last_.then_inc(z_done, 1)

            hidden_bias(0, 0)
            for k in range(4):
                piece(0, 0, k)
            for b in range(2):
                front.stats(dve, 0, b)
                front.norm(dve, 0, b)
            halves(0, 0)

            def body(p, first, last):
                for q in range(Q):
                    i = Q * p + q
                    pp, par = at(p, q)
                    ends = None if first and q == 0 else before(pp, par)
                    if q % PER == PER - 1 and not (last and q == Q - 1):
                        hidden_bias(2 * p + q // PER + 1, (q // PER + 1) % 2)
                    if ends:
                        out(i - 1, *ends, 2 * p + (q - 1) // PER)
                    for f in range(FT):
                        hid.low(dve, FT * i + f, f)
                        if f < 4 and q % PER == PER - 1 and not (last and q == Q - 1):
                            piece(2 * p + q // PER + 1, (q // PER + 1) % 2, f)
                        if f == 1 and ends:
                            back.stats(dve, z_done, i, *ends)
                        if f == 4 and ends:
                            back.norm(dve, *ends)
                        if f == 5 and not (last and q == Q - 1):
                            halves(i + 1, (q + 1) % 2)
                        if not (last and q >= Q - 2):
                            if f == 3:
                                front.stats(dve, pp + 1, par)
                            if f == 6:
                                front.norm(dve, pp + 1, par)

            passes(dve, body)
            out(NBLK - 1, NBLK // 2 - 1, 1, BATCH - 1)
            back.stats(dve, z_done, NBLK, NBLK // 2 - 1, 1)
            back.norm(dve, NBLK // 2 - 1, 1)

        @block.tensor
        def _(pe):
            LAG = 3

            front.turn(pe, pT, 0, 0)

            def body(p, first, last):
                for q in range(Q):
                    i = Q * p + q
                    b = q // PER
                    for f in range(FT + LAG):
                        if f == 3 and not (last and q == Q - 1):
                            pe.wait_ge(hf_done, i + 1)
                            front.turn(pe, pT, *after(*at(p, q)))
                        if f < FT:
                            waits = [(hlo_done, i + 1), (wlo_done, 4 * (2 * p + b + 1))] if f == 0 else []
                            hid.up(pe, FT * i + f, f, w1[b], hp[q % 2], waits)
                        g = f - LAG
                        if g == 0:
                            wait(pe, z_done, i)
                        if g >= 0:
                            hid.down_tokens(pe, FT * i + g, g, w2[b], pH)

            passes(pe, body)


FILT = 64
EMB = 3
INNER = 3 * D
HALF = SEQ // 2
KT = HALF // P
IT = INNER // P
TWO_PI = 2 * np.pi
ROUND = 1.5 * 2.0 ** 23


def two_pi_parts():
    a = np.float32(6.28125)
    b = np.float32(round((TWO_PI - float(a)) * 2 ** 20) / 2 ** 20)
    return float(a), float(b), float(np.float32(TWO_PI - float(a) - float(b)))


def long_filter(nc, consts, shared, z_d, t_d, decay_d, w1_d, w2_d, w3_d, wo_d, b_d, freq_d, fb_d, half_d):
    cos_m, sin_m, ks = shared
    with ExitStack() as ctx:
        ph = Phase(nc, ctx, "lf")
        z = ph.sb("z", [EMB, SEQ])
        tcol = ph.sb("tcol", [P, KT, 2])
        dec = ph.sb("dec", [P, D])
        ws = [ph.sb("w1", [EMB, FILT]), ph.sb("w2", [FILT, FILT]), ph.sb("w3", [FILT, FILT])]
        wo = ph.sb("wo", [FILT, D])
        bs = ph.sb("bs", [FILT, 3])
        freq = ph.sb("freq", [FILT, 1])
        fb = ph.sb("fb", [1, D])
        hc = ph.sb("hc", [P, 3, KT])
        load_weights(nc, "lfl", [
            (z[:, :], z_d), (tcol[:, :, :].rearrange("p a b -> p (a b)"), t_d),
            (dec[:, :], decay_d.unsqueeze(0).broadcast_to([P, D])), (ws[0][:, :], w1_d), (ws[1][:, :], w2_d),
            (ws[2][:, :], w3_d), (wo[:, :], wo_d), (bs[:, :], b_d), (freq[:, :], freq_d), (fb[:, :], fb_d),
            (hc[:, :, :].rearrange("p a b -> p (a b)"), half_d)], [])
        h = [ph.sb(f"h{n}", [FILT, SEQ]) for n in range(3)]
        a, n, r = (ph.sb(x, [FILT, SEQ]) for x in "anr")
        env = ph.sb("env", [P, KT, 2, D])
        kf = ph.sb("kf", [P, KT, 2, D])
        kp = ph.pair("kp", [P, KT, 2, D])
        t1 = ph.sb("t1", [P, KT, 5, D])
        ph_ = [ph.ps(f"ph{x}", [P, HALF]) for x in range(2)]
        pk = [ph.ps(f"pk{x}", [P, 2, D]) for x in range(2)]
        pf = [ph.ps(f"pf{x}", [P, 2, D]) for x in range(4)]
        v, v3, s, t = ph.sem("v"), ph.sem("v3"), ph.sem("s"), ph.sem("t")
        block = ctx.enter_context(nc.Block())
        LAYER = 8

        @block.tensor
        def _(pe):
            for l in range(3):
                src = z if l == 0 else h[l - 1]
                if l:
                    pe.wait_ge(s, l)
                for c in range(2):
                    mm = pe.matmul(ph_[c][0:FILT, :], ws[l][:, :], src[:, c * HALF:(c + 1) * HALF],
                                   start=True, stop=True)
                mm.then_inc(t, 1)
            pe.wait_ge(s, 3)
            samples = h[2][:, :].rearrange("p (k s r) -> p k r s", k=KT, r=2)
            for k in range(KT):
                if k >= 2:
                    pe.wait_ge(v, 3 * LAYER + k - 1)
                for q in range(2):
                    mm = pe.matmul(pk[k % 2][:, q, :], samples[:, k, q, :], wo[:, :], start=True, stop=True)
                mm.then_inc(t, 1)
            pe.wait_ge(v, 3 * LAYER + KT + 2)
            for k in range(KT):
                if k >= 2:
                    pe.wait_ge(v, 3 * LAYER + KT + 2 + 3 * (k - 1))
                for x, m in enumerate((cos_m, sin_m)):
                    for q in range(KT):
                        out = pf[2 * (k % 2) + x][:, :, :].rearrange("p a b -> p (a b)")
                        mm = three_pass(pe, out, tuple(w[:, q, k * P:(k + 1) * P] for w in m),
                                        tuple(w[:, q, :, :].rearrange("p a b -> p (a b)") for w in kp),
                                        q == 0, q == KT - 1)
                mm.then_inc(t, 1)

        @block.scalar
        def _(act):
            for l in range(3):
                act.wait_ge(v, LAYER * (l + 1))
                act.activation(h[l][:, :], r[:, :], ACT.Sin).then_inc(s, 1)
            for k in range(KT):
                for q in range(2):
                    last = act.activation(env[:, k, q, :], dec[:, :], ACT.Exp, scale=tcol[:, k, q:q + 1])
            last.then_inc(s, 1)
            act.wait_ge(v, 3 * LAYER + KT + 1)
            act.activation(kp[0][:, :, :, :], kf[:, :, :, :], ACT.Identity).then_inc(s, 1)

        @block.vector
        def _(dve):
            p1, p2, p3 = two_pi_parts()
            count = [0]

            def step(ins):
                count[0] += 1
                ins.then_inc(v, 1)
                dve.wait_ge(v, count[0])

            for l in range(3):
                dve.wait_ge(t, l + 1)
                if l:
                    dve.wait_ge(s, l)
                for c in range(2):
                    cs = slice(c * HALF, (c + 1) * HALF)
                    step(dve.tensor_scalar(a[:, cs], ph_[c][0:FILT, :], bs[:, l:l + 1], freq[:, 0:1], ALU.add, ALU.mult))
                step(dve.tensor_scalar(n[:, :], a[:, :], 1 / TWO_PI, ROUND, ALU.mult, ALU.add))
                step(dve.tensor_scalar(n[:, :], n[:, :], ROUND, None, ALU.subtract))
                step(dve.scalar_tensor_tensor(a[:, :], n[:, :], -p1, a[:, :], ALU.mult, ALU.add))
                step(dve.scalar_tensor_tensor(a[:, :], n[:, :], -p2, a[:, :], ALU.mult, ALU.add))
                step(dve.scalar_tensor_tensor(r[:, :], n[:, :], -p3, a[:, :], ALU.mult, ALU.add))
                step(dve.tensor_scalar(r[:, :], r[:, :], 3.1415925, -3.1415925, ALU.min, ALU.max))
            dve.wait_ge(s, 4)
            for k in range(KT):
                dve.wait_ge(t, 3 + k + 1)
                step(dve.tensor_tensor(kf[:, k, :, :], pk[k % 2][:, :, :], env[:, k, :, :], ALU.mult))
            step(dve.tensor_tensor(kf[0:1, 0, 0, :], kf[0:1, 0, 0, :], fb[:, :], ALU.add))
            dve.wait_ge(s, 5)
            step(dve.tensor_tensor(kp[1][:, :, :, :], kf[:, :, :, :], kp[0][:, :, :, :].bitcast(F32), ALU.subtract))
            for k in range(KT):
                dve.wait_ge(t, 3 + KT + k + 1)
                re, im = pf[2 * (k % 2)], pf[2 * (k % 2) + 1]
                c_, s_, ms = (hc[:, x, k:k + 1] for x in range(3))
                dve.tensor_scalar(t1[:, k, 0, :], re[:, 0, :], ms, None, ALU.mult)
                dve.tensor_scalar(t1[:, k, 1, :], im[:, 0, :], s_, None, ALU.mult)
                dve.tensor_scalar(t1[:, k, 2, :], re[:, 1, :], s_, None, ALU.mult)
                dve.tensor_scalar(t1[:, k, 3, :], im[:, 1, :], s_, None, ALU.mult)
                step(dve.tensor_scalar(t1[:, k, 4, :], im[:, 1, :], ms, None, ALU.mult))
                stt = dve.scalar_tensor_tensor
                stt(ks[:, k, 0, 1, :], re[:, 0, :], c_, t1[:, k, 1, :], ALU.mult, ALU.add)
                stt(ks[:, k, 1, 1, :], im[:, 0, :], c_, t1[:, k, 0, :], ALU.mult, ALU.add)
                stt(ks[:, k, 0, 2, :], re[:, 1, :], c_, t1[:, k, 4, :], ALU.mult, ALU.add)
                stt(ks[:, k, 1, 2, :], im[:, 1, :], c_, t1[:, k, 2, :], ALU.mult, ALU.add)
                step(stt(ks[:, k, 0, 0, :], re[:, 1, :], c_, t1[:, k, 3, :], ALU.mult, ALU.add))
                dve.tensor_scalar(t1[:, k, 2, :], re[:, 1, :], ms, None, ALU.mult).then_inc(v3, 1)
                dve.wait_ge(v3, k + 1)
                step(stt(ks[:, k, 1, 0, :], im[:, 1, :], c_, t1[:, k, 2, :], ALU.mult, ALU.add))


def hyena(nc, x_dram, y_dram, consts, cos_d, sin_d, filter_args, in_w, in_b, sw_d, sb_d, out_w, outb_d):
    with ExitStack() as ctx:
        ph = Phase(nc, ctx, "hy")
        cos_m = ph.pair("cos", [P, KT, HALF])
        sin_m = ph.pair("sin", [P, KT, HALF])
        ks = ph.sb("ks", [P, KT, 2, 3, D])
        flat = lambda t: tuple(x[:, :, :].rearrange("p a b -> p (a b)") for x in t)
        load_weights(nc, "hym", [], [(flat(cos_m), cos_d), (flat(sin_m), sin_d)])
        long_filter(nc, consts, (cos_m, sin_m, ks), *filter_args)
        wi = ph.pair("wi", [P, DH, INNER])
        wo = ph.pair("wo", [P, DH, D])
        inb = ph.sb("inb", [P, IT])
        sw = ph.sb("sw", [P, 3, IT])
        sbias = ph.sb("sbias", [P, IT])
        outb = ph.sb("outb", [P, D])
        load_weights(nc, "hyl",
                     [(inb[:, :], in_b), (sw[:, :, :].rearrange("p a b -> p (a b)"), sw_d), (sbias[:, :], sb_d),
                      (outb[:, :], outb_d.unsqueeze(0).broadcast_to([P, D]))],
                     [(flat(wi), in_w), (flat(wo), out_w)], chunk=1536)
        front = Front(ph, x_dram, consts["ident"], in_place=True)
        xres = ph.sb("xres", [P, 2 * TT, D])
        hp = [ph.pair(f"hp{b}", [P, DH, BLK]) for b in range(2)]
        up = [ph.sb(f"up{b}", [P, SEQ + 2]) for b in range(2)]
        acc = ph.sb("acc", [P, SEQ])
        x1 = ph.sb("x1", [P, SEQ])
        x0 = ph.sb("x0", [P, DH, SEQ])
        vx = ph.sb("vx", [P, DH, SEQ])
        both = ph.pair("both", [P, 2 * SEQ])
        vT = [x[:, :].rearrange("p (k r c) -> p k r c", k=KT, r=2) for x in both]
        yp = [x[:, :].rearrange("p (h t) -> p h t", h=DH) for x in both]
        NPM = 3
        pm = [ph.sb(f"pm{n}", [P, 2, 2, D]) for n in range(NPM)]
        yf = ph.sb("yf", [P, 4, D])
        yk = [ph.pair(f"yk{b}", [P, 4, D]) for b in range(2)]
        zy = ph.sb("zy", [P, 2 * SEQ])
        yv = zy[:, :].rearrange("p (h t r) -> p h r t", h=DH, r=2)
        z = zy[:, :].rearrange("p (t d) -> p t d", d=D)
        st = ph.sb("st", [P, 2 * TT, 6])
        mv = ph.sb("mv", [P, 2 * TT, 2])
        rs = ph.sb("rs", [P, 2 * TT])
        ve = ph.sb("ve", [P, 2 * TT])
        tick = ph.sb("tick", [P, 1])
        pF = [ph.ps(f"pF{n}", [P, BLK]) for n in range(4)]
        pG = [ph.ps(f"pG{n}", [P, BLK]) for n in range(4)]
        padded = ph.sem("padded")
        hhi, hlo = ph.sem("hhi"), ph.sem("hlo")
        in_mm, up_done, t0_done = ph.sem("in_mm"), ph.sem("up"), ph.sem("t0")
        cv = ph.sem("cv")
        vT_mm, vT_hi, vT_lo = ph.sem("vT_mm"), ph.sem("vT_hi"), ph.sem("vT_lo")
        f_mm, i_mm = ph.sem("f_mm"), ph.sem("i_mm")
        mul = ph.sem("mul")
        comb = ph.sem("comb")
        half = ph.sem("half")
        y_hi, y_lo = ph.sem("y_hi"), ph.sem("y_lo")
        yv_done, yv_hi, yv_lo = ph.sem("yv"), ph.sem("yv_hi"), ph.sem("yv_lo")
        e_mm = ph.sem("e_mm")
        z_done, st_done, mv_done, ve_done, rs_done = (ph.sem(x) for x in ("z", "st", "mv", "ve", "rs"))
        zn_done, added = ph.sem("zn"), ph.sem("added")
        stored, res_loaded = ph.sem("stored"), ph.sem("res_loaded")
        block = ctx.enter_context(nc.Block())

        ORDER = [(DH, "x1", 0), (2 * DH, "v", 0), (DH + 1, "x1", 1), (2 * DH + 1, "v", 1), (0, "x0", 0), (1, "x0", 1)]
        STEPS = [2, 3, 2, 3, 2, 2]
        CV = sum(STEPS)

        def cv_at(i, n):
            return CV * i + sum(STEPS[:n + 1])

        def batches(eng, body):
            rounds(eng, BATCH, lambda p, par, first, last: body(2 * p + par, first, last))

        def tokens(dram, i):
            return dram[bass.ds(i * SEQ, SEQ), :].rearrange("(t p) d -> p t d", p=P)

        @block.sync
        def _(sp):
            front.load(sp, 0, 0)
            front.load(sp, 0, 1)

            def body(i, first, last):
                wait(sp, added, i)
                sp.dma_start(xres[:, :, :], tokens(x_dram, i)).then_inc(res_loaded, 16)
                if not last:
                    for b in range(2):
                        sp.wait_ge(front.turned, 2 * i + b + 1)
                        front.load(sp, i + 1, b)
                sp.wait_ge(added, i + 1)
                sp.dma_start(tokens(y_dram, i), z).then_inc(stored, 16)

            batches(sp, body)
            sp.wait_ge(stored, 16 * BATCH)

        @block.gpsimd
        def _(pool):
            front.rstd(pool, consts, 0, 0)
            front.rstd(pool, consts, 0, 1)

            def body(i, first, last):
                for k in range(KT):
                    for o in range(4):
                        n = 16 * i + 4 * k + o
                        pool.wait_ge(comb, n + 1)
                        if o == 0:
                            wait(pool, y_lo, 4 * i + k)
                        m = pm[(4 * k + o) % NPM]
                        pool.tensor_tensor(yf[:, o, :], m[:, 0, 0, :], m[:, 0, 1, :], ALU.add).then_inc(half, 1)
                    if k == 1 and not last:
                        front.rstd(pool, consts, i + 1, 0)
                        front.rstd(pool, consts, i + 1, 1)
                pool.wait_ge(mv_done, i + 1)
                wait(pool, zn_done, i)
                pool.tensor_tensor(ve[:, :], mv[:, :, 1], consts["eps"][:, 0:1].broadcast_to([P, 2 * TT]),
                                   ALU.add).then_inc(ve_done, 1)
                pool.wait_ge(ve_done, i + 1)
                pool.tensor_tensor(rs[:, :], ve[:, :], consts["mhalf"][:, 0:1].broadcast_to([P, 2 * TT]),
                                   ALU.pow).then_inc(rs_done, 1)
                pool.wait_ge(zn_done, i + 1)
                pool.wait_ge(res_loaded, 16 * (i + 1))
                pool.tensor_tensor(z, z, xres[:, :, :], ALU.add).then_inc(added, 1)

            batches(pool, body)

        @block.scalar
        def _(act):
            def high(i, b):
                act.wait_ge(front.turned, 2 * i + b + 1)
                wait(act, in_mm, 12 * i)
                for h in range(DH):
                    last_ = act.activation(hp[b][0][:, h, :], pF[h][:, :], ACT.Identity)
                last_.then_inc(hhi, 1)

            def project(i):
                for n, (m, _, _) in enumerate(ORDER):
                    u = up[n % 2]
                    if n >= 2:
                        act.wait_ge(cv, cv_at(i, n - 2))
                    elif not (isinstance(i, int) and i == 0):
                        act.wait_ge(cv, cv_at(i - 1, n + len(ORDER) - 2))
                    for b in range(2):
                        act.wait_ge(in_mm, 12 * i + 2 * n + b + 1)
                        act.activation(u[:, 2 + b * BLK:2 + (b + 1) * BLK], pF[2 + b][:, :], ACT.Identity,
                                       bias=inb[:, m:m + 1]).then_inc(up_done, 1)
                    act.wait_ge(up_done, 12 * i + 2 * n + 2)
                    wait(act, cv, cv_at(i, n - 1) if n else CV * i)
                    act.activation(acc[:, :], u[:, 2:SEQ + 2], ACT.Identity, bias=sbias[:, m:m + 1],
                                   scale=sw[:, 2, m:m + 1]).then_inc(t0_done, 1)

            def vt_high(i):
                for q in range(KT):
                    act.wait_ge(vT_mm, 4 * i + q + 1)
                    if q == 0:
                        wait(act, e_mm, i)
                    act.activation(vT[0][:, q, :, :], pG[q][:, :].rearrange("p (r c) -> p r c", r=2),
                                   ACT.Identity).then_inc(vT_hi, 1)

            high(0, 0)
            high(0, 1)
            act.wait_ge(padded, 1)
            project(0)
            vt_high(0)

            def body(i, first, last):
                for k in range(KT):
                    act.wait_ge(half, 16 * i + 4 * (k + 1))
                    wait(act, i_mm, 4 * i + k - 1)
                    act.activation(yk[k % 2][0][:, :, :], yf[:, :, :], ACT.Identity).then_inc(y_hi, 1)
                if not last:
                    high(i + 1, 0)
                act.wait_ge(yv_done, 4 * (i + 1))
                act.activation(yp[0], zy[:, :].rearrange("p (h t) -> p h t", h=DH), ACT.Identity).then_inc(yv_hi, 1)
                if not last:
                    high(i + 1, 1)
                    project(i + 1)
                    vt_high(i + 1)

            batches(act, body)

        @block.vector
        def _(dve):
            def low(i, b):
                dve.wait_ge(hhi, 2 * i + b + 1)
                wait(dve, in_mm, 12 * i)
                for h in range(DH):
                    last_ = dve.tensor_tensor(hp[b][1][:, h, :], pF[h][:, :], hp[b][0][:, h, :].bitcast(F32),
                                              ALU.subtract)
                last_.then_inc(hlo, 1)

            def short_conv(i):
                for n, (m, kind, h) in enumerate(ORDER):
                    u = up[n % 2]
                    base = CV * i + sum(STEPS[:n])
                    dve.wait_ge(t0_done, 6 * i + n + 1)
                    dve.scalar_tensor_tensor(acc[:, :], u[:, 1:SEQ + 1], sw[:, 1, m:m + 1], acc[:, :],
                                             ALU.mult, ALU.add).then_inc(cv, 1)
                    dve.wait_ge(cv, base + 1)
                    dst = {"x1": x1[:, :], "v": acc[:, :], "x0": x0[:, h, :]}[kind]
                    dve.scalar_tensor_tensor(dst, u[:, 0:SEQ], sw[:, 0, m:m + 1], acc[:, :],
                                             ALU.mult, ALU.add).then_inc(cv, 1)
                    if kind == "v":
                        dve.wait_ge(cv, base + 2)
                        dve.tensor_tensor(vx[:, h, :], acc[:, :], x1[:, :], ALU.mult).then_inc(cv, 1)

            def vt_low(i):
                for q in range(KT):
                    dve.wait_ge(vT_hi, 4 * i + q + 1)
                    dve.tensor_tensor(vT[1][:, q, :, :], pG[q][:, :].rearrange("p (r c) -> p r c", r=2),
                                      vT[0][:, q, :, :].bitcast(F32), ALU.subtract).then_inc(vT_lo, 1)

            def y_low(i, k):
                dve.wait_ge(y_hi, 4 * i + k + 1)
                dve.tensor_tensor(yk[k % 2][1][:, :, :], yf[:, :, :], yk[k % 2][0][:, :, :].bitcast(F32),
                                  ALU.subtract).then_inc(y_lo, 1)

            def products(i, k):
                re, im = (pF[2 * (k % 2) + x][:, :].rearrange("p (r c) -> p r c", r=2) for x in range(2))

                def combine(o):
                    n = 16 * i + 4 * k + o
                    m = pm[(4 * k + o) % NPM]
                    dve.wait_ge(mul, n + 1)
                    dve.tensor_tensor(m[:, 0, :, :], m[:, 0, :, :], m[:, 1, :, :],
                                      ALU.subtract if o % 2 == 0 else ALU.add).then_inc(comb, 1)

                dve.wait_ge(f_mm, 4 * i + k + 1)
                for o in range(4):
                    n = 16 * i + 4 * k + o
                    m = pm[(4 * k + o) % NPM]
                    slot = slice(1, 3) if o < 2 else slice(0, 2)
                    a, b = (re, im) if o % 2 == 0 else (im, re)
                    wait(dve, half, n - NPM + 1)
                    dve.tensor_tensor(m[:, 0, :, :], a, ks[:, k, 0, slot, :], ALU.mult)
                    dve.tensor_tensor(m[:, 1, :, :], b, ks[:, k, 1, slot, :], ALU.mult).then_inc(mul, 1)
                    if o:
                        combine(o - 1)
                    if o == 1 and k:
                        y_low(i, k - 1)
                combine(3)

            dve.memset(up[0][:, 0:2], 0.0)
            dve.memset(up[1][:, 0:2], 0.0).then_inc(padded, 1)
            for b in range(2):
                front.stats(dve, 0, b)
                front.norm(dve, 0, b)
            low(0, 0)
            low(0, 1)
            short_conv(0)
            vt_low(0)

            def body(i, first, last):
                for k in range(KT):
                    products(i, k)
                    for b in range(2):
                        if k == 0 and not last:
                            front.stats(dve, i + 1, b)
                        if k == 2 and not last:
                            front.norm(dve, i + 1, b)
                y_low(i, KT - 1)
                dve.wait_ge(i_mm, 4 * (i + 1))
                wait(dve, stored, 16 * i)
                for h in range(DH):
                    for r in range(2):
                        dve.tensor_tensor(yv[:, h, r, :], pG[2 * h + r][:, :],
                                          x0[:, h, :].rearrange("p (t r) -> p r t", r=2)[:, r, :],
                                          ALU.mult).then_inc(yv_done, 1)
                if not last:
                    low(i + 1, 0)
                dve.wait_ge(yv_hi, i + 1)
                dve.wait_ge(yv_done, 4 * (i + 1))
                dve.tensor_tensor(yp[1], zy[:, :].rearrange("p (h t) -> p h t", h=DH), yp[0].bitcast(F32),
                                  ALU.subtract).then_inc(yv_lo, 1)
                if not last:
                    low(i + 1, 1)
                    short_conv(i + 1)
                dve.wait_ge(e_mm, i + 1)
                dve.wait_ge(yv_lo, i + 1)
                for n in range(4):
                    last_ = dve.tensor_tensor(z[:, 2 * n:2 * n + 2, :],
                                              pF[n][:, :].rearrange("p (t d) -> p t d", t=2),
                                              outb[:, :].unsqueeze(1).broadcast_to([P, 2, D]), ALU.add)
                last_.then_inc(z_done, 1)
                dve.wait_ge(z_done, i + 1)
                for t in range(2 * TT):
                    last_ = dve.bn_stats(st[:, t, :], z[:, t, :])
                last_.then_inc(st_done, 1)
                dve.wait_ge(st_done, i + 1)
                wait(dve, rs_done, i)
                dve.memset(tick[:, :], 0.0)
                for t in range(2 * TT):
                    last_ = dve.bn_aggr(mv[:, t, :], st[:, t, :])
                last_.then_inc(mv_done, 1)
                if not last:
                    vt_low(i + 1)
                dve.wait_ge(rs_done, i + 1)
                for t in range(2 * TT):
                    last_ = dve.tensor_scalar(z[:, t, :], z[:, t, :], mv[:, t, 0:1], rs[:, t:t + 1],
                                              ALU.subtract, ALU.mult)
                last_.then_inc(zn_done, 1)

            batches(dve, body)

        @block.tensor
        def _(pe):
            def project(i):
                wait(pe, mul, 16 * i)
                front.turn(pe, pF, i, 0)
                pe.wait_ge(hlo, 2 * i + 1)
                front.turn(pe, pF, i, 1)
                pe.wait_ge(hlo, 2 * i + 2)
                for n, (m, _, _) in enumerate(ORDER):
                    for b in range(2):
                        wait(pe, up_done, 12 * i + 2 * n + b - 1)
                        for k in range(DH):
                            mm = three_pass(pe, pF[2 + b][:, :], tuple(w[:, k, m * P:(m + 1) * P] for w in wi),
                                            tuple(x[:, k, :] for x in hp[b]), k == 0, k == DH - 1)
                        mm.then_inc(in_mm, 1)

            def turn_vx(i):
                pe.wait_ge(cv, cv_at(i, 3))
                wait(pe, yv_done, 4 * i)
                for q in range(KT):
                    for r in range(2):
                        for h in range(DH):
                            src = vx[:, h, :].rearrange("p (q s r) -> p q r s", q=KT, r=2)[:, q, r, :]
                            mm = pe.transpose(pG[q][:, r * D + h * P:r * D + (h + 1) * P], src, consts["ident"][:, :])
                    mm.then_inc(vT_mm, 1)

            def forward(i, k):
                if k == 0:
                    pe.wait_ge(vT_lo, 4 * (i + 1))
                    wait(pe, z_done, i)
                    pe.wait_ge(up_done, 12 * (i + 1))
                if k >= 2:
                    pe.wait_ge(mul, 16 * i + 4 * (k - 1))
                for x, m in enumerate((cos_m, sin_m)):
                    for q in range(KT):
                        mm = three_pass(pe, pF[2 * (k % 2) + x][:, :], tuple(w[:, q, k * P:(k + 1) * P] for w in m),
                                        tuple(v[:, q, :, :].rearrange("p r c -> p (r c)") for v in vT),
                                        q == 0, q == KT - 1)
                mm.then_inc(f_mm, 1)

            def inverse(i, k):
                pe.wait_ge(y_lo, 4 * i + k + 1)
                for h in range(DH):
                    for r in range(2):
                        for x, m in enumerate((cos_m, sin_m)):
                            mm = three_pass(pe, pG[2 * h + r][:, :],
                                            tuple(y[:, 2 * r + x, h * P:(h + 1) * P] for y in yk[k % 2]),
                                            tuple(w[:, k, :] for w in m), k == 0 and x == 0,
                                            k == KT - 1 and x == 1)
                mm.then_inc(i_mm, 1)

            def project_out(i, last):
                pe.wait_ge(yv_lo, i + 1)
                if last:
                    pe.wait_ge(mul, 16 * (i + 1))
                else:
                    pe.wait_ge(up_done, 12 * (i + 2))
                for t in range(2 * TT):
                    for h in range(DH):
                        mm = three_pass(pe, pF[t // 2][:, (t % 2) * D:(t % 2 + 1) * D],
                                        tuple(y[:, h, t * P:(t + 1) * P] for y in yp),
                                        tuple(w[:, h, :] for w in wo), h == 0, h == DH - 1)
                mm.then_inc(e_mm, 1)

            project(0)
            turn_vx(0)

            def body(i, first, last):
                for k in range(KT + 1):
                    if k < KT:
                        forward(i, k)
                    if k:
                        inverse(i, k - 1)
                if not last:
                    project(i + 1)
                project_out(i, last)
                if not last:
                    turn_vx(i + 1)

            batches(pe, body)


def program(nc, t, out):
    def scratch(name, shape):
        return nc.dram_tensor(name, shape, F32, kind="Internal").ap()

    xs = [scratch(f"x_after_{n}", (TOKENS, D)) for n in range(3)]
    mid = scratch("x_mid", (TOKENS, D))
    mw = scratch("batch_weights", (BATCH, 2 * D, HID))
    with ExitStack() as ctx:
        consts = make_consts(nc, ctx, t["identity"])
        hyena(nc, t["u"], xs[0], consts, t["cos"], t["sin"],
              tuple(t[n] for n in ("pos", "times", "decay", "mlp_w1", "mlp_w2", "mlp_w3", "mlp_wo", "mlp_b", "freq",
                                   "filt_bias", "half_angle")),
              t["in_w"], t["in_b"], t["short_w"], t["short_b"], t["out_w"], t["out_b"])
        channel_mix(nc, xs[0], xs[1], consts, t["W_r"], t["W_k"], t["W_v"], t["mu_r"], t["mu_k"])
        linear_attention(nc, xs[1], mid, consts, t["wq"], t["wk"], t["wv"], t["wo"], t["ln1_g"], t["ln1_b"],
                         t["head_of_four"], t["causal"], t["same_head"])
        gelu_levels(nc, xs[1], mid, xs[2], consts, t["ln2_g"], t["ln2_b"], t["cms_w1"], t["cms_b1"], t["cms_w2"],
                    t["cms_b2"], t["cms_b2_last"])
        ph = Phase(nc, ctx, "shared")
        shared = ph.sb("mb1", [P, BATCH, FT]), ph.sb("mb2", [P, BATCH, D])
        expert_weights(nc, xs[2], consts, shared, mw, t["expert_rows"], t["base_rows"], t["gate_w1"], t["gate_b1"],
                       t["gate_w2"], t["gate_b2"], t["expert_select"], t["row_select"], t["row_spread"],
                       t["Tb1"], t["b1"], t["Tb2"], t["b2"])
        batch_mlp(nc, xs[2], out, consts, shared, mw)


def tables():
    f = np.float32

    def columns(v):
        return v.reshape(-1, P).T

    def rows(w):
        return w.reshape(w.shape[0] // P, P, -1).transpose(1, 0, 2).reshape(P, -1)

    time = np.linspace(0.0, 1.0, SEQ).astype(f)
    angle = (f(1e-4) * (f(TWO_PI) * np.linspace(0.0, SEQ - 1.0, SEQ).astype(f) / f(SEQ))).astype(f)
    deltas = np.linspace(np.log(0.01) / 1.5, np.log(0.01) / 0.3, D).astype(f)
    k = np.arange(HALF) + 0.5
    grid = TWO_PI / SEQ * np.outer(k, k)
    half = np.pi * k / SEQ
    head = np.arange(P) // HD
    got = {
        "identity": np.eye(P), "cos": rows(np.cos(grid)), "sin": rows(np.sin(grid)),
        "pos": np.stack([time, np.cos(angle), -np.sin(angle)]),
        "times": time.reshape(KT, P, 2).transpose(1, 0, 2).reshape(P, 2 * KT), "decay": -np.abs(deltas),
        "half_angle": np.concatenate([columns(g / HALF) for g in (np.cos(half), np.sin(half), -np.sin(half))], 1),
        "head_of_four": np.stack([head % QUAD == o for o in range(QUAD)], 1), "causal": np.triu(np.ones((P, P))),
        "same_head": head[:, None] == head[None, :], "expert_select": np.repeat(np.eye(EXPERTS), GROUP, 1),
        "row_select": np.tile(np.eye(GROUP), (EXPERTS, 1)), "row_spread": np.tile(np.eye(GROUP), (1, BATCH)),
    }
    return {n: np.ascontiguousarray(a, dtype=f) for n, a in got.items()}


def kernel(**inputs):
    import concourse.bacc as bacc
    from concourse.bass_utils import run_bass_kernel_spmd

    def columns(v):
        return v.reshape(-1, P).T

    def rows(w):
        return w.reshape(w.shape[0] // P, P, -1).transpose(1, 0, 2).reshape(P, -1)

    def part(prefix):
        return lambda name: np.asarray(inputs[f"{prefix}_{name}"])

    a, c, l, g = part("L0_attn"), part("L0_ffn"), part("L1_attn"), part("L1_ffn")
    sw = a("short_w")
    w2_rows = g("TW2").transpose(0, 2, 1).reshape(EXPERTS, D, HID)
    experts = np.concatenate([g("TW1").transpose(0, 2, 1), w2_rows], 1)
    given = {
        "u": a("u").reshape(TOKENS, D), "in_w": rows(a("in_w")), "in_b": columns(a("in_b")),
        "short_w": np.concatenate([columns(sw[:, j]) for j in range(3)], 1), "short_b": columns(a("short_b")),
        "mlp_w1": a("mlp_w1"), "mlp_w2": a("mlp_w2"), "mlp_w3": a("mlp_w3"), "mlp_wo": a("mlp_wo"),
        "mlp_b": np.stack([a("mlp_b1"), a("mlp_b2"), a("mlp_b3")], 1), "freq": a("freq").T,
        "filt_bias": a("filt_bias").reshape(1, D), "out_w": rows(a("out_w")), "out_b": a("out_b"),
        "W_r": rows(c("W_r").T), "W_k": rows(c("W_k").T), "W_v": rows(c("W_v").T),
        "mu_r": columns(c("mu_r")), "mu_k": columns(c("mu_k")),
        "wq": rows(l("wq")), "wk": rows(l("wk")), "wv": rows(l("wv")), "wo": rows(l("wo")),
        "ln1_g": columns(l("ln1_g")), "ln1_b": columns(l("ln1_b")),
        "ln2_g": columns(l("ln2_g")), "ln2_b": columns(l("ln2_b")),
        "cms_w1": np.stack([rows(w) for w in l("cms_w1")]), "cms_w2": np.stack([rows(w) for w in l("cms_w2")]),
        "cms_b1": columns(l("cms_b1")), "cms_b2": columns(l("cms_b2")), "cms_b2_last": l("cms_b2")[-1],
        "gate_w1": rows(g("gate_w1").T), "gate_b1": columns(g("gate_b1")), "gate_w2": rows(g("gate_w2").T),
        "gate_b2": g("gate_b2").reshape(EXPERTS, 1),
        "expert_rows": experts.reshape(EXPERTS, GROUPS, GROUP, HID).transpose(1, 0, 2, 3).reshape(GROUPS * P, HID),
        "base_rows": np.concatenate([g("W1").T, g("W2").T.reshape(D, HID)], 0),
        "b1": columns(g("b1")), "b2": g("b2").reshape(1, D), "Tb1": g("Tb1"), "Tb2": g("Tb2"),
    }
    nc = bacc.Bacc("TRN2", target_bir_lowering=False, num_devices=1)
    arrays, views = {}, {}
    for name, value in {**given, **tables()}.items():
        arrays[f"{name}_dram"] = np.ascontiguousarray(value)
        views[name] = nc.dram_tensor(f"{name}_dram", value.shape, F32, kind="ExternalInput").ap()
    out = nc.dram_tensor("out_dram", (TOKENS, D), F32, kind="ExternalOutput").ap()
    program(nc, views, out)
    result = run_bass_kernel_spmd(nc, [arrays], core_ids=[0])
    return result.results[0]["out_dram"].reshape(BATCH, SEQ, D)
```

```python
from contextlib import ExitStack

import numpy as np

import concourse.bass as bass
from concourse import mybir

P = 128
EPS = 1e-5
F32 = mybir.dt.float32
F32R = mybir.dt.float32r
ALU = mybir.AluOpType
ACT = mybir.ActivationFunctionType

BATCH, SEQ, D = 8, 1024, 256
TOKENS = BATCH * SEQ
DH = D // P
BLK = 512
NBLK = TOKENS // BLK
TT = BLK // P


def wait(eng, sem, value):
    if isinstance(value, int) and value <= 0:
        return
    eng.wait_ge(sem, value)


def rounds(eng, n, body):
    body(0, 0, True, False)
    body(0, 1, False, False)
    if n > 4:
        with eng.Fori(1, n // 2 - 1) as p:
            body(p, 0, False, False)
            body(p, 1, False, False)
    body(n // 2 - 1, 0, False, False)
    body(n // 2 - 1, 1, False, True)


def after(p, par):
    return (p, 1) if par == 0 else (p + 1, 0)


def before(p, par):
    return (p, 0) if par == 1 else (p - 1, 1)


def skewed(eng, n, ahead, behind, body):
    def run(p, par):
        def do(d, stage):
            q, b = p + (par + d) // 2, (par + d) % 2
            if not isinstance(p, int) or 0 <= 2 * q + b < n:
                stage(q, b)
        body(do)

    first, lo, hi, end = -((ahead + 1) // 2), behind // 2 + 1, (n - ahead) // 2, (n + behind + 1) // 2
    for p in range(first, lo):
        run(p, 0)
        run(p, 1)
    with eng.Fori(lo, hi) as p:
        run(p, 0)
        run(p, 1)
    for p in range(hi, end):
        run(p, 0)
        run(p, 1)


def three_pass(pe, out, w, x, start, stop):
    (w_hi, w_lo), (x_hi, x_lo) = w, x
    pe.matmul(out, w_lo, x_hi, start=start, stop=False)
    pe.matmul(out, w_hi, x_lo, start=False, stop=False)
    return pe.matmul(out, w_hi, x_hi, start=False, stop=stop)


class Phase:

    def __init__(self, nc, ctx, name):
        self.nc, self.ctx, self.name, self.sems = nc, ctx, name, []
        ctx.callback(self.close)

    def close(self):
        if self.sems:
            self.nc.clear_and_free_semaphores(self.sems)
            self.nc.all_engine_barrier()

    def sb(self, name, shape, dt=F32):
        return self.ctx.enter_context(self.nc.sbuf_tensor(f"{self.name}_{name}", shape, dt))

    def ps(self, name, shape, dt=F32):
        return self.ctx.enter_context(self.nc.psum_tensor(f"{self.name}_{name}", shape, dt))

    def sem(self, name):
        self.sems.append(self.nc.alloc_semaphore(name=f"{self.name}_{name}"))
        return self.sems[-1]

    def pair(self, name, shape):
        return self.sb(name + "_hi", shape, F32R), self.sb(name + "_lo", shape, F32R)


def load_weights(nc, name, plain, split, chunk=2048):
    with ExitStack() as ctx:
        ph = Phase(nc, ctx, name)
        n_bufs = 3
        raw = [ph.sb(f"raw{b}", [P, chunk]) for b in range(n_bufs)] if split else []
        loaded_plain = ph.sem("loaded_plain")
        loaded = [ph.sem(f"loaded{b}") for b in range(n_bufs)]
        hi_done = ph.sem("hi_done")
        lo_done = ph.sem("lo_done")
        pieces = []
        for (hi, lo), src in split:
            rows, n = src.shape
            for c in range(0, n, chunk):
                m = min(chunk, n - c)
                pieces.append((rows, m, hi[:, c:c + m], lo[:, c:c + m], src[:, c:c + m]))
        block = ctx.enter_context(nc.Block())

        @block.sync
        def _(sp):
            def load(n, rows, m, src):
                wait(sp, lo_done, n - n_bufs + 1)
                sp.dma_start(raw[n % n_bufs][0:rows, 0:m], src).then_inc(loaded[n % n_bufs], 16)

            for n, (rows, m, _, _, src) in enumerate(pieces[:n_bufs]):
                load(n, rows, m, src)
            for dst, src in plain:
                sp.dma_start(dst, src).then_inc(loaded_plain, 16)
            for n, (rows, m, _, _, src) in enumerate(pieces[n_bufs:]):
                load(n + n_bufs, rows, m, src)
            if plain:
                sp.wait_ge(loaded_plain, 16 * len(plain))

        @block.scalar
        def _(act):
            for n, (rows, m, hi, _, _) in enumerate(pieces):
                act.wait_ge(loaded[n % n_bufs], 16 * (n // n_bufs + 1))
                act.activation(hi, raw[n % n_bufs][0:rows, 0:m], ACT.Identity).then_inc(hi_done, 1)

        @block.vector
        def _(dve):
            for n, (rows, m, hi, lo, _) in enumerate(pieces):
                dve.wait_ge(hi_done, n + 1)
                dve.tensor_tensor(lo, raw[n % n_bufs][0:rows, 0:m], hi.bitcast(F32),
                                  ALU.subtract).then_inc(lo_done, 1)


class Front:

    def __init__(self, ph, x_dram, ident, in_place=False):
        self.ph, self.x_dram, self.ident = ph, x_dram, ident
        self.x = [ph.sb(f"f_x{b}", [P, TT, D]) for b in range(2)]
        self.xn = self.x if in_place else [ph.sb(f"f_xn{b}", [P, TT, D]) for b in range(2)]
        self.st = [ph.sb(f"f_st{b}", [P, TT, 6]) for b in range(2)]
        self.mv = [ph.sb(f"f_mv{b}", [P, TT, 2]) for b in range(2)]
        self.rs = [ph.sb(f"f_rs{b}", [P, TT]) for b in range(2)]
        self.ve = [ph.sb(f"f_ve{b}", [P, TT]) for b in range(2)]
        self.tick = ph.sb("f_tick", [P, 1])
        self.loaded = [ph.sem(f"x_loaded{b}") for b in range(2)]
        self.st_done = ph.sem("f_stats")
        self.mv_done = ph.sem("f_mv")
        self.ve_done = ph.sem("f_ve")
        self.rs_done = ph.sem("f_rstd")
        self.xn_done = ph.sem("f_xn")
        self.turned = ph.sem("f_turned")

    def load(self, sp, p, par):
        i = 2 * p + par
        src = self.x_dram[bass.ds(i * BLK, BLK), :].rearrange("(t p) d -> p t d", p=P)
        sp.dma_start(self.x[par][:, :, :], src).then_inc(self.loaded[par], 16)

    def stats(self, dve, p, par):
        i = 2 * p + par
        dve.wait_ge(self.loaded[par], 16 * (p + 1))
        for t in range(TT):
            last = dve.bn_stats(self.st[par][:, t, :], self.x[par][:, t, :])
        last.then_inc(self.st_done, 1)
        dve.wait_ge(self.st_done, i + 1)
        wait(dve, self.rs_done, i - 1)
        dve.memset(self.tick[:, :], 0.0)
        for t in range(TT):
            last = dve.bn_aggr(self.mv[par][:, t, :], self.st[par][:, t, :])
        last.then_inc(self.mv_done, 1)

    def rstd(self, pool, consts, p, par):
        i = 2 * p + par
        pool.wait_ge(self.mv_done, i + 1)
        wait(pool, self.xn_done, i - 1)
        pool.tensor_tensor(self.ve[par][:, :], self.mv[par][:, :, 1], consts["eps"], ALU.add).then_inc(self.ve_done, 1)
        pool.wait_ge(self.ve_done, i + 1)
        pool.tensor_tensor(self.rs[par][:, :], self.ve[par][:, :], consts["mhalf"], ALU.pow).then_inc(self.rs_done, 1)

    def norm(self, dve, p, par):
        i = 2 * p + par
        dve.wait_ge(self.rs_done, i + 1)
        wait(dve, self.turned, i - 1)
        for t in range(TT):
            last = dve.tensor_scalar(self.xn[par][:, t, :], self.x[par][:, t, :], self.mv[par][:, t, 0:1],
                                     self.rs[par][:, t:t + 1], ALU.subtract, ALU.mult)
        last.then_inc(self.xn_done, 1)

    def turn(self, pe, banks, p, par):
        pe.wait_ge(self.xn_done, 2 * p + par + 1)
        for h in range(DH):
            for t in range(TT):
                last = pe.transpose(banks[h][:, t * P:(t + 1) * P], self.xn[par][:, t, h * P:(h + 1) * P],
                                    self.ident[:, :])
        last.then_inc(self.turned, 1)


class TokenNorm:

    def __init__(self, ph, name, tiles=TT):
        self.tiles = tiles
        self.st = [ph.sb(f"{name}_st{b}", [P, tiles, 6]) for b in range(2)]
        self.mv = [ph.sb(f"{name}_mv{b}", [P, tiles, 2]) for b in range(2)]
        self.tmp = [ph.sb(f"{name}_tmp{b}", [P, 2, tiles]) for b in range(2)]
        self.scale = [ph.sb(f"{name}_scale{b}", [P, tiles]) for b in range(2)]
        self.shift = [ph.sb(f"{name}_shift{b}", [P, tiles]) for b in range(2)]
        self.tick = ph.sb(f"{name}_tick", [P, 1])
        self.st_done = ph.sem(f"{name}_stats")
        self.mv_done = ph.sem(f"{name}_mv")
        self.step = ph.sem(f"{name}_step")
        self.factors_done = ph.sem(f"{name}_factors")
        self.done = ph.sem(f"{name}_normed")

    def stats(self, dve, x, p, par):
        i = 2 * p + par
        for t in range(self.tiles):
            last = dve.bn_stats(self.st[par][:, t, :], x[:, t, :])
        last.then_inc(self.st_done, 1)
        dve.wait_ge(self.st_done, i + 1)
        wait(dve, self.factors_done, i - 1)
        dve.memset(self.tick[:, :], 0.0)
        for t in range(self.tiles):
            last = dve.bn_aggr(self.mv[par][:, t, :], self.st[par][:, t, :])
        last.then_inc(self.mv_done, 1)

    def factors(self, pool, consts, p, par):
        i = 2 * p + par
        mean, var = self.mv[par][:, :, 0], self.mv[par][:, :, 1]
        t0, t1, scale = self.tmp[par][:, 0, :], self.tmp[par][:, 1, :], self.scale[par][:, :]
        const = lambda name: consts[name][:, 0:1].broadcast_to([P, self.tiles])
        pool.wait_ge(self.mv_done, i + 1)
        wait(pool, self.done, i - 1)
        pool.tensor_tensor(t0, var, const("eps"), ALU.add).then_inc(self.step, 1)
        pool.wait_ge(self.step, 3 * i + 1)
        pool.tensor_tensor(scale, t0, const("mhalf"), ALU.pow).then_inc(self.step, 1)
        pool.wait_ge(self.step, 3 * i + 2)
        pool.tensor_tensor(t1, mean, scale, ALU.mult).then_inc(self.step, 1)
        pool.wait_ge(self.step, 3 * i + 3)
        pool.tensor_tensor(self.shift[par][:, :], t1, const("mone"), ALU.mult).then_inc(self.factors_done, 1)

    def apply(self, act, out, x, p, par):
        act.wait_ge(self.factors_done, 2 * p + par + 1)
        for t in range(self.tiles):
            last = act.activation(out[:, t, :], x[:, t, :], ACT.Identity, bias=self.shift[par][:, t:t + 1],
                                  scale=self.scale[par][:, t:t + 1])
        last.then_inc(self.done, 1)


class Back:

    def __init__(self, ph, front, y_dram):
        self.ph, self.front, self.y_dram = ph, front, y_dram
        self.z = [ph.sb(f"z{b}", [P, TT, D]) for b in range(2)]
        self.st = [ph.sb(f"b_st{b}", [P, TT, 6]) for b in range(2)]
        self.mv = [ph.sb(f"b_mv{b}", [P, TT, 2]) for b in range(2)]
        self.rs = [ph.sb(f"b_rs{b}", [P, TT]) for b in range(2)]
        self.ve = [ph.sb(f"b_ve{b}", [P, TT]) for b in range(2)]
        self.tick = ph.sb("b_tick", [P, 1])
        self.st_done = ph.sem("b_stats")
        self.mv_done = ph.sem("b_mv")
        self.ve_done = ph.sem("b_ve")
        self.rs_done = ph.sem("b_rstd")
        self.zn_done = ph.sem("b_zn")
        self.added = ph.sem("b_added")
        self.stored = [ph.sem(f"b_stored{b}") for b in range(2)]

    def z_free(self, eng, p, par):
        wait(eng, self.stored[par], 16 * p)

    def stats(self, dve, z_sem, z_count, p, par):
        i = 2 * p + par
        dve.wait_ge(z_sem, z_count)
        for t in range(TT):
            last = dve.bn_stats(self.st[par][:, t, :], self.z[par][:, t, :])
        last.then_inc(self.st_done, 1)
        dve.wait_ge(self.st_done, i + 1)
        wait(dve, self.rs_done, i - 1)
        dve.memset(self.tick[:, :], 0.0)
        for t in range(TT):
            last = dve.bn_aggr(self.mv[par][:, t, :], self.st[par][:, t, :])
        last.then_inc(self.mv_done, 1)

    def rstd(self, pool, consts, p, par):
        i = 2 * p + par
        pool.wait_ge(self.mv_done, i + 1)
        wait(pool, self.zn_done, i - 1)
        pool.tensor_tensor(self.ve[par][:, :], self.mv[par][:, :, 1], consts["eps"], ALU.add).then_inc(self.ve_done, 1)
        pool.wait_ge(self.ve_done, i + 1)
        pool.tensor_tensor(self.rs[par][:, :], self.ve[par][:, :], consts["mhalf"], ALU.pow).then_inc(self.rs_done, 1)

    def norm(self, dve, p, par):
        i = 2 * p + par
        dve.wait_ge(self.rs_done, i + 1)
        z = self.z[par]
        for t in range(TT):
            last = dve.tensor_scalar(z[:, t, :], z[:, t, :], self.mv[par][:, t, 0:1],
                                     self.rs[par][:, t:t + 1], ALU.subtract, ALU.mult)
        last.then_inc(self.zn_done, 1)

    def add(self, pool, p, par):
        pool.wait_ge(self.zn_done, 2 * p + par + 1)
        z = self.z[par]
        pool.tensor_tensor(z[:, :, :], z[:, :, :], self.front.x[par][:, :, :], ALU.add).then_inc(self.added, 1)

    def store(self, eng, p, par):
        i = 2 * p + par
        eng.wait_ge(self.added, i + 1)
        dst = self.y_dram[bass.ds(i * BLK, BLK), :].rearrange("(t p) d -> p t d", p=P)
        eng.dma_start(dst, self.z[par][:, :, :]).then_inc(self.stored[par], 16)

    def all_stored(self, eng):
        for s in self.stored:
            eng.wait_ge(s, 16 * NBLK // 2)


def channel_mix(nc, x_dram, y_dram, consts, W_r, W_k, W_v, mu_r, mu_k):
    with ExitStack() as ctx:
        ph = Phase(nc, ctx, "cm")
        wr = ph.pair("wr", [P, DH, D])
        wk = ph.pair("wk", [P, DH, D])
        wv = ph.pair("wv", [P, DH, D])
        mu = ph.sb("mu", [P, 2, DH])
        flat = lambda w: tuple(t[:, :, :].rearrange("p a b -> p (a b)") for t in w)
        load_weights(nc, "cml",
                     [(mu[:, 0, :], mu_r), (mu[:, 1, :], mu_k)],
                     [(flat(wr), W_r), (flat(wk), W_k), (flat(wv), W_v)])
        x, x_res, z, r = ([ph.sb(f"{n}{b}", [P, TT, D]) for b in range(2)] for n in ("x", "x_res", "z", "r"))
        xT = [ph.sb(f"xT{b}", [P, DH, BLK + 1]) for b in range(2)]
        dx, kr, ka = ([ph.sb(f"{n}{b}", [P, DH, BLK]) for b in range(2)] for n in ("dx", "kr", "ka"))
        mixed = {m: [ph.sb(f"mix_{m}{b}", [P, DH, BLK]) for b in range(2)] for m in "rk"}
        mixp = {m: [ph.pair(f"mixp_{m}{b}", [P, DH, BLK]) for b in range(2)] for m in "rk"}
        kap = [ph.pair(f"kap{b}", [P, DH, BLK]) for b in range(2)]
        front = TokenNorm(ph, "front")
        back = TokenNorm(ph, "back")
        pT = [ph.ps(f"pT{h}", [P, BLK]) for h in range(DH)]
        pK = [ph.ps(f"pK{h}", [P, BLK]) for h in range(DH)]
        pR = [ph.ps(f"pR{h}", [P, 2, D]) for h in range(2)]
        pV = [ph.ps(f"pV{h}", [P, 2, D]) for h in range(2)]
        x_loaded = [ph.sem(f"x_loaded{b}") for b in range(2)]
        res_loaded = [ph.sem(f"res_loaded{b}") for b in range(2)]
        stored = [ph.sem(f"stored{b}") for b in range(2)]
        zeroed = ph.sem("zeroed")
        turned = ph.sem("turned")
        xT_done = ph.sem("xT")
        dx_done = ph.sem("dx")
        mix_done = ph.sem("mix")
        hi_done = ph.sem("mix_hi")
        lo_done = ph.sem("mix_lo")
        k_done = ph.sem("k")
        kr_done = ph.sem("kr")
        ka_done = ph.sem("ka")
        kahi_done = ph.sem("kahi")
        kalo_done = ph.sem("kalo")
        r_done = ph.sem("r_mm")
        sig_done = ph.sem("r_sig")
        v_done = ph.sem("v_mm")
        z_done = ph.sem("z")
        added = ph.sem("added")
        block = ctx.enter_context(nc.Block())
        AHEAD, BEHIND = 4, 2

        def tokens(dram, i):
            return dram[bass.ds(i * BLK, BLK), :].rearrange("(t p) d -> p t d", p=P)

        @block.sync
        def _(sp):
            def load(p, par):
                wait(sp, turned, 2 * p + par - 1)
                sp.dma_start(x[par][:, :, :], tokens(x_dram, 2 * p + par)).then_inc(x_loaded[par], 16)

            def load_res(p, par):
                wait(sp, added, 2 * p + par - 1)
                sp.dma_start(x_res[par][:, :, :], tokens(x_dram, 2 * p + par)).then_inc(res_loaded[par], 16)

            def store(p, par):
                sp.wait_ge(added, 2 * p + par + 1)
                sp.dma_start(tokens(y_dram, 2 * p + par), z[par][:, :, :]).then_inc(stored[par], 16)

            def body(do):
                do(-1, load_res)
                do(4, load)
                do(-2, store)

            skewed(sp, NBLK, AHEAD, BEHIND, body)
            for s in stored:
                sp.wait_ge(s, 16 * NBLK // 2)

        @block.gpsimd
        def _(pool):
            pool.memset(xT[0][:, :, 0:1], 0.0).then_inc(zeroed, 1)
            pool.wait_ge(zeroed, 1)

            def difference(p, par):
                i = 2 * p + par
                pool.wait_ge(xT_done, i + 1)
                wait(pool, mix_done, 2 * (i - 1))
                pool.tensor_tensor(dx[par][:, :, :], xT[par][:, :, 1:BLK + 1], xT[par][:, :, 0:BLK],
                                   ALU.subtract).then_inc(dx_done, 1)

            def square(p, par):
                i = 2 * p + par
                pool.wait_ge(kr_done, i + 1)
                wait(pool, kalo_done, i - 1)
                pool.tensor_tensor(ka[par][:, :, :], kr[par][:, :, :], kr[par][:, :, :], ALU.mult).then_inc(ka_done, 1)

            def add(p, par):
                pool.wait_ge(back.done, 2 * p + par + 1)
                pool.wait_ge(res_loaded[par], 16 * (p + 1))
                pool.tensor_tensor(z[par][:, :, :], z[par][:, :, :], x_res[par][:, :, :], ALU.add).then_inc(added, 1)

            def body(do):
                do(1, difference)
                do(-2, lambda p, par: back.factors(pool, consts, p, par))
                do(0, square)
                do(3, lambda p, par: front.factors(pool, consts, p, par))
                do(-2, add)

            skewed(pool, NBLK, AHEAD, BEHIND, body)

        @block.scalar
        def _(act):
            def take(p, par):
                i = 2 * p + par
                act.wait_ge(turned, i + 1)
                wait(act, mix_done, 2 * (i - 1))
                for h in range(DH):
                    last = act.activation(xT[par][:, h, 1:BLK + 1], pT[h][:, :], ACT.Identity)
                if par:
                    act.wait_ge(xT_done, i)
                    last = act.activation(xT[1][:, :, 0:1], xT[0][:, :, BLK:BLK + 1], ACT.Identity)
                last.then_inc(xT_done, 1)

            def mix_high(m, n):
                def stage(p, par):
                    i = 2 * p + par
                    act.wait_ge(mix_done, 2 * i + n + 1)
                    wait(act, r_done if m == "r" else k_done, i - 1)
                    act.activation(mixp[m][par][0][:, :, :], mixed[m][par][:, :, :],
                                   ACT.Identity).then_inc(hi_done, 1)
                return stage

            def relu(p, par):
                i = 2 * p + par
                act.wait_ge(k_done, i + 1)
                wait(act, ka_done, i - 1)
                for h in range(DH):
                    last = act.activation(kr[par][:, h, :], pK[h][:, :], ACT.Relu)
                last.then_inc(kr_done, 1)

            def sigmoid(p, par):
                i = 2 * p + par
                act.wait_ge(r_done, i + 1)
                wait(act, z_done, i - 1)
                for h in range(2):
                    last = act.activation(r[par][:, 2 * h:2 * h + 2, :], pR[h][:, :, :], ACT.Sigmoid)
                last.then_inc(sig_done, 1)

            def squares_high(p, par):
                i = 2 * p + par
                act.wait_ge(ka_done, i + 1)
                wait(act, v_done, i - 1)
                act.activation(kap[par][0][:, :, :], ka[par][:, :, :], ACT.Identity).then_inc(kahi_done, 1)

            def body(do):
                do(1, take)
                do(2, lambda p, par: front.apply(act, x[par], x[par], p, par))
                do(0, relu)
                do(-2, lambda p, par: back.apply(act, z[par], z[par], p, par))
                do(1, mix_high("k", 0))
                do(1, mix_high("r", 1))
                do(0, sigmoid)
                do(0, squares_high)

            skewed(act, NBLK, AHEAD, BEHIND, body)

        @block.vector
        def _(dve):
            def mix(p, par):
                i = 2 * p + par
                dve.wait_ge(dx_done, i + 1)
                wait(dve, lo_done, 2 * (i - 1))
                for m in "kr":
                    for h in range(DH):
                        s = mu[:, 0 if m == "r" else 1, h:h + 1]
                        last = dve.scalar_tensor_tensor(mixed[m][par][:, h, :], dx[par][:, h, :], s,
                                                        xT[par][:, h, 0:BLK], ALU.mult, ALU.add)
                    last.then_inc(mix_done, 1)

            def mix_low(p, par):
                i = 2 * p + par
                for n, m in enumerate("kr"):
                    dve.wait_ge(hi_done, 2 * i + n + 1)
                    dve.wait_ge(mix_done, 2 * i + n + 1)
                    hi, lo = mixp[m][par]
                    dve.tensor_tensor(lo[:, :, :], mixed[m][par][:, :, :], hi[:, :, :].bitcast(F32),
                                      ALU.subtract).then_inc(lo_done, 1)

            def squares_low(p, par):
                dve.wait_ge(kahi_done, 2 * p + par + 1)
                hi, lo = kap[par]
                dve.tensor_tensor(lo[:, :, :], ka[par][:, :, :], hi[:, :, :].bitcast(F32),
                                  ALU.subtract).then_inc(kalo_done, 1)

            def front_stats(p, par):
                dve.wait_ge(x_loaded[par], 16 * (p + 1))
                front.stats(dve, x[par], p, par)

            def gate(p, par):
                i = 2 * p + par
                dve.wait_ge(v_done, i + 1)
                dve.wait_ge(sig_done, i + 1)
                wait(dve, stored[par], 16 * p)
                for h in range(2):
                    last = dve.tensor_tensor(z[par][:, 2 * h:2 * h + 2, :], pV[h][:, :, :],
                                             r[par][:, 2 * h:2 * h + 2, :], ALU.mult)
                last.then_inc(z_done, 1)
                dve.wait_ge(z_done, i + 1)
                back.stats(dve, z[par], p, par)

            def body(do):
                do(-1, squares_low)
                do(1, mix)
                do(3, front_stats)
                do(1, mix_low)
                do(-1, gate)

            skewed(dve, NBLK, AHEAD, BEHIND, body)

        @block.tensor
        def _(pe):
            def turn(p, par):
                i = 2 * p + par
                pe.wait_ge(front.done, i + 1)
                wait(pe, xT_done, i)
                for h in range(DH):
                    for t in range(TT):
                        last = pe.transpose(pT[h][:, t * P:(t + 1) * P], x[par][:, t, h * P:(h + 1) * P],
                                            consts["ident"][:, :])
                last.then_inc(turned, 1)

            def keys(p, par):
                i = 2 * p + par
                pe.wait_ge(lo_done, 2 * i + 1)
                wait(pe, kr_done, i)
                for m in range(DH):
                    for k in range(DH):
                        mm = three_pass(pe, pK[m][:, :], tuple(w[:, k, m * P:(m + 1) * P] for w in wk),
                                        tuple(h[:, k, :] for h in mixp["k"][par]), k == 0, k == DH - 1)
                mm.then_inc(k_done, 1)

            def token_major(banks, halves, weights, done):
                for t in range(TT):
                    ts = slice(t * P, (t + 1) * P)
                    for k in range(DH):
                        mm = three_pass(pe, banks[t // 2][:, t % 2, :], tuple(h[:, k, ts] for h in halves),
                                        tuple(w[:, k, :] for w in weights), k == 0, k == DH - 1)
                mm.then_inc(done, 1)

            def gates(p, par):
                i = 2 * p + par
                pe.wait_ge(lo_done, 2 * i + 2)
                wait(pe, sig_done, i)
                token_major(pR, mixp["r"][par], wr, r_done)

            def values(p, par):
                i = 2 * p + par
                pe.wait_ge(kalo_done, i + 1)
                wait(pe, z_done, i)
                token_major(pV, kap[par], wv, v_done)

            def body(do):
                do(0, keys)
                do(0, gates)
                do(-1, values)
                do(2, turn)

            skewed(pe, NBLK, AHEAD, BEHIND, body)


def make_consts(nc, ctx, ident_d):
    ph = Phase(nc, ctx, "c")
    ident = ph.sb("ident", [P, P])
    mhalf = ph.sb("mhalf", [P, TT])
    eps = ph.sb("eps", [P, TT])
    one = ph.sb("one", [P, TT])
    mone = ph.sb("mone", [P, TT])
    loaded = ph.sem("loaded")
    made = ph.sem("made")
    with nc.Block() as block:
        @block.sync
        def _(sp):
            sp.dma_start(ident[:, :], ident_d).then_inc(loaded, 16)
            sp.wait_ge(loaded, 16)

        @block.gpsimd
        def _(pool):
            pool.memset(mhalf[:, :], -0.5).then_inc(made, 1)
            pool.memset(eps[:, :], EPS).then_inc(made, 1)
            pool.memset(one[:, :], 1.0).then_inc(made, 1)
            pool.memset(mone[:, :], -1.0).then_inc(made, 1)
            pool.wait_ge(made, 4)
    return {"ident": ident, "mhalf": mhalf[:, :], "eps": eps[:, :], "one": one[:, :], "mone": mone[:, :]}


HEADS = 16
HD = D // HEADS
HH = HEADS // DH
QUAD = HH // 2


def linear_attention(nc, x_dram, y_dram, consts, wq, wk, wv, wo, ln_g, ln_b, own_d, causal_d, same_d):
    with ExitStack() as ctx:
        ph = Phase(nc, ctx, "la")
        w = {n: ph.pair(f"w{n}", [P, DH, D]) for n in ("q", "k", "o")}
        wkv = ph.pair("wkv", [P, DH, 2 * D])
        gb = ph.sb("gb", [P, 2, DH])
        own = ph.sb("own", [P, HH])
        causal = ph.sb("causal", [P, P])
        same = ph.sb("same", [P, DH, P])
        flat = lambda t: tuple(x[:, :, :].rearrange("p a b -> p (a b)") for x in t)
        kvd = []
        for h in range(DH):
            for n, src in enumerate((wk, wv)):
                kvd.append((tuple(t[:, h, n * D:(n + 1) * D] for t in wkv), src[:, h * D:(h + 1) * D]))
        load_weights(nc, "lal",
                     [(gb[:, 0, :], ln_g), (gb[:, 1, :], ln_b), (own[:, :], own_d), (causal[:, :], causal_d),
                      (same[:, 0, :], same_d), (same[:, 1, :], same_d)],
                     [(flat(w["q"]), wq), (flat(w["k"]), wk), (flat(w["o"]), wo)] + kvd)
        front = Front(ph, x_dram, consts["ident"], in_place=True)
        tmp = [ph.sb(f"tmp{b}", [P, 5, TT]) for b in range(2)]
        res = [ph.sb(f"res{b}", [P, TT]) for b in range(2)]
        n_res = [ph.sb(f"n_res{b}", [P, TT, D]) for b in range(2)]
        hf = ph.sb("hf", [P, DH, BLK])
        hp = ph.pair("hp", [P, DH, BLK])
        qT = [ph.sb(f"qT{b}", [P, DH, BLK]) for b in range(2)]
        qp = [ph.pair(f"qp{b}", [P, DH, BLK]) for b in range(2)]
        kp = [ph.pair(f"kp{b}", [P, DH, BLK]) for b in range(2)]
        qE = [ph.pair(f"qE{b}", [P, DH, HH, P]) for b in range(2)]
        kv = [ph.sb(f"kv{b}", [P, TT, 2 * D]) for b in range(2)]
        sT = [ph.sb(f"sT{b}", [P, 4, QUAD, P]) for b in range(2)]
        state = [ph.sb(f"state{b}", [P, DH, P]) for b in range(2)]
        vE = [ph.sb(f"vE{b}", [P, DH, HH * (P + HD)]) for b in range(2)]
        yp = [ph.pair(f"yp{b}", [P, DH, BLK]) for b in range(2)]
        z = [ph.sb(f"z{b}", [P, TT, D]) for b in range(2)]
        pA = [ph.ps(f"pA{h}", [P, BLK]) for h in range(2)]
        pS = [ph.ps(f"pS{j}", [P, QUAD, P]) for j in range(4)]
        pY = ph.ps("pY", [P, BLK])
        pM = ph.ps("pM", [P, DH * P * 2])
        small = ph.sem("small")
        n_done = ph.sem("n_res")
        hf_done = ph.sem("hf")
        hhi_done = ph.sem("hhi")
        hlo_done = ph.sem("hlo")
        q_mm, k_mm, kv_mm = ph.sem("q_mm"), ph.sem("k_mm"), ph.sem("kv_mm")
        q_ev, k_ev, kv_ev = ph.sem("q_ev"), ph.sem("k_ev"), ph.sem("kv_ev")
        qhi_done, qlo_done = ph.sem("qhi"), ph.sem("qlo")
        klo_done = ph.sem("klo")
        qEhi_done, qElo_done = ph.sem("qEhi"), ph.sem("qElo")
        s_mm = ph.sem("s_mm")
        s_ev = ph.sem("s_ev")
        m_mm = ph.sem("m_mm")
        m_ev = ph.sem("m_ev")
        zeroed = ph.sem("zeroed")
        vE_done = ph.sem("vE")
        y_mm = ph.sem("y_mm")
        yhi_done = ph.sem("yhi")
        ylo_done = ph.sem("ylo")
        o_mm = ph.sem("o_mm")
        z_done = ph.sem("z")
        stored = [ph.sem(f"stored{b}") for b in range(2)]
        block = ctx.enter_context(nc.Block())
        STATES = 2 * TT - 1
        END = NBLK // 2

        def states(p, par, t):
            return STATES * p + TT * par + t

        @block.sync
        def _(sp):
            front.load(sp, 0, 0)
            front.load(sp, 0, 1)

            def store(p, par):
                i = 2 * p + par
                sp.wait_ge(z_done, i + 1)
                dst = y_dram[bass.ds(i * BLK, BLK), :].rearrange("(t p) d -> p t d", p=P)
                sp.dma_start(dst, z[par][:, :, :]).then_inc(stored[par], 16)

            def body(p, par, first, last):
                if not (isinstance(p, int) and p == END - 1):
                    sp.wait_ge(front.turned, 2 * p + par + 1)
                    sp.wait_ge(n_done, 2 * p + par + 1)
                    front.load(sp, p + 1, par)
                if not first:
                    store(*before(p, par))

            rounds(sp, NBLK, body)
            store(END - 1, 1)
            for s in stored:
                sp.wait_ge(s, 16 * NBLK // 2)

        @block.gpsimd
        def _(pool):
            def rstd(p, par):
                i = 2 * p + par
                var = front.mv[par][:, :, 1]
                a, r1, r2, t1, t2 = (tmp[par][:, n, :] for n in range(5))
                count = [0]

                def step(ins):
                    count[0] += 1
                    ins.then_inc(small, 1)
                    pool.wait_ge(small, 7 * i + count[0])

                pool.wait_ge(front.mv_done, i + 1)
                wait(pool, front.xn_done, i - 1)
                wait(pool, n_done, i - 1)
                step(pool.tensor_tensor(a, var, consts["eps"], ALU.add))
                step(pool.tensor_tensor(r1, a, consts["mhalf"], ALU.pow))
                step(pool.tensor_tensor(t1, r1, r1, ALU.mult))
                step(pool.tensor_tensor(t2, t1, var, ALU.mult))
                step(pool.tensor_tensor(a, t2, consts["eps"], ALU.add))
                step(pool.tensor_tensor(r2, a, consts["mhalf"], ALU.pow))
                step(pool.tensor_tensor(res[par][:, :], a, r2, ALU.mult))
                pool.tensor_tensor(front.rs[par][:, :], r1, r2, ALU.mult).then_inc(front.rs_done, 1)

            def keep(p, par):
                i = 2 * p + par
                pool.wait_ge(front.xn_done, i + 1)
                wait(pool, z_done, i - 1)
                pool.tensor_tensor(n_res[par][:, :, :], front.xn[par][:, :, :],
                                   res[par][:, :].unsqueeze(2).broadcast_to([P, TT, D]), ALU.mult).then_inc(n_done, 1)

            def expand(p, par, t):
                i = 2 * p + par
                pool.wait_ge(qlo_done, i + 1)
                wait(pool, s_mm, 4 * (TT * i + t - 1))
                q = qp[par][1][:, :, t * P:(t + 1) * P].bitcast(F32).unsqueeze(2).broadcast_to([P, DH, HH, P])
                mask = own[:, :].unsqueeze(1).unsqueeze(3).broadcast_to([P, DH, HH, P])
                pool.tensor_tensor(qE[t % 2][1][:, :, :, :], q, mask, ALU.mult).then_inc(qElo_done, 1)

            def values(p, par, t):
                c = TT * (2 * p + par) + t
                pool.wait_ge(kv_ev, c + 1)
                wait(pool, y_mm, c - 1)
                own_columns = vE[t % 2][:, :, :].rearrange("p h (o s) -> p h o s", o=HH)[:, :, :, 0:HD]
                v = kv[par][:, t, D:2 * D].rearrange("p (h o s) -> p h o s", h=DH, o=HH)
                one = consts["one"][:, 0:1].unsqueeze(2).unsqueeze(3).broadcast_to([P, DH, HH, HD])
                pool.tensor_tensor(own_columns, v, one, ALU.mult).then_inc(vE_done, 1)

            for b in range(2):
                pool.memset(vE[b][:, :, :], 0.0).then_inc(zeroed, 1)
            rstd(0, 0)
            rstd(0, 1)
            keep(0, 0)
            expand(0, 0, 0)
            expand(0, 0, 1)
            pool.wait_ge(zeroed, 2)

            def body(p, par, first, last):
                values(p, par, 0)
                values(p, par, 1)
                expand(p, par, 2)
                expand(p, par, 3)
                values(p, par, 2)
                if not (isinstance(p, int) and p == END - 1):
                    rstd(p + 1, par)
                if not last:
                    keep(*after(p, par))
                values(p, par, 3)
                if not last:
                    expand(*after(p, par), 0)
                    expand(*after(p, par), 1)

            rounds(pool, NBLK, body)

        @block.scalar
        def _(act):
            def take(p, par):
                i = 2 * p + par
                act.wait_ge(front.turned, i + 1)
                wait(act, hlo_done, i)
                for h in range(DH):
                    last_ = act.activation(hf[:, h, :], pA[h][:, :], ACT.Identity, bias=gb[:, 1, h:h + 1],
                                           scale=gb[:, 0, h:h + 1])
                last_.then_inc(hf_done, 1)
                act.wait_ge(hf_done, i + 1)
                wait(act, kv_mm, TT * i)
                act.activation(hp[0][:, :, :], hf[:, :, :], ACT.Identity).then_inc(hhi_done, 1)

            def queries(p, par):
                i = 2 * p + par
                act.wait_ge(q_mm, i + 1)
                wait(act, y_mm, TT * (i - 1))
                wait(act, qlo_done, i - 1)
                for h in range(DH):
                    last_ = act.activation(qT[par][:, h, :], pA[h][:, :], ACT.Identity)
                last_.then_inc(q_ev, 1)
                act.wait_ge(q_ev, i + 1)
                act.activation(qp[par][0][:, :, :], qT[par][:, :, :], ACT.Identity).then_inc(qhi_done, 1)

            def expand(p, par, t):
                i = 2 * p + par
                act.wait_ge(qhi_done, i + 1)
                wait(act, s_mm, 4 * (TT * i + t - 1))
                for o in range(HH):
                    last_ = act.activation(qE[t % 2][0][:, :, o, :], qp[par][0][:, :, t * P:(t + 1) * P].bitcast(F32),
                                           ACT.Identity, scale=own[:, o:o + 1])
                last_.then_inc(qEhi_done, 1)

            def keys(p, par):
                i = 2 * p + par
                act.wait_ge(k_mm, i + 1)
                wait(act, s_mm, 4 * TT * (i - 1))
                for h in range(DH):
                    last_ = act.activation(kp[par][0][:, h, :], pA[h][:, :], ACT.Identity)
                last_.then_inc(k_ev, 1)

            def high(p, par, t):
                i = 2 * p + par
                act.wait_ge(y_mm, TT * i + t + 1)
                if t == 0:
                    wait(act, o_mm, i - 1)
                ts = slice(t * P, (t + 1) * P)
                act.activation(yp[par][0][:, :, ts], pY[:, 0:DH * P].rearrange("p (h t) -> p h t", h=DH),
                               ACT.Identity).then_inc(yhi_done, 1)

            take(0, 0)
            queries(0, 0)
            keys(0, 0)
            expand(0, 0, 0)
            expand(0, 0, 1)

            def body(p, par, first, last):
                if not last:
                    take(*after(p, par))
                if not first:
                    high(*before(p, par), TT - 1)
                high(p, par, 0)
                expand(p, par, 2)
                if not last:
                    queries(*after(p, par))
                high(p, par, 1)
                expand(p, par, 3)
                if not last:
                    keys(*after(p, par))
                    expand(*after(p, par), 0)
                high(p, par, 2)
                if not last:
                    expand(*after(p, par), 1)

            rounds(act, NBLK, body)
            high(END - 1, 1, TT - 1)

        @block.vector
        def _(dve):
            def low(p, par):
                i = 2 * p + par
                dve.wait_ge(hf_done, i + 1)
                dve.wait_ge(hhi_done, i + 1)
                wait(dve, kv_mm, TT * i)
                dve.tensor_tensor(hp[1][:, :, :], hf[:, :, :], hp[0][:, :, :].bitcast(F32),
                                  ALU.subtract).then_inc(hlo_done, 1)

            def queries_low(p, par):
                i = 2 * p + par
                dve.wait_ge(qhi_done, i + 1)
                wait(dve, qElo_done, TT * (i - 1))
                dve.tensor_tensor(qp[par][1][:, :, :], qT[par][:, :, :], qp[par][0][:, :, :].bitcast(F32),
                                  ALU.subtract).then_inc(qlo_done, 1)

            def keys_low(p, par):
                dve.wait_ge(k_ev, 2 * p + par + 1)
                for h in range(DH):
                    last_ = dve.tensor_tensor(kp[par][1][:, h, :], pA[h][:, :], kp[par][0][:, h, :].bitcast(F32),
                                              ALU.subtract)
                last_.then_inc(klo_done, 1)

            def keep_kv(p, par, t):
                i = 2 * p + par
                dve.wait_ge(kv_mm, TT * i + t + 1)
                if t == 0:
                    wait(dve, y_mm, TT * (i - 1))
                dve.tensor_copy(kv[par][:, t, :], pA[t % 2][:, :]).then_inc(kv_ev, 1)

            def scores(p, par, t):
                c = TT * (2 * p + par) + t
                wait(dve, y_mm, c - 1)
                for j in range(4):
                    dve.wait_ge(s_mm, 4 * c + j + 1)
                    mask = causal[:, :].unsqueeze(1).broadcast_to([P, QUAD, P])
                    dve.tensor_tensor(sT[t % 2][:, j, :, :], pS[j][:, :, :], mask, ALU.mult).then_inc(s_ev, 1)

            def keep_state(p, par, t):
                if par == 1 and t == TT - 1:
                    return
                dve.wait_ge(m_mm, states(p, par, t) + 1)
                dve.tensor_tensor(state[t % 2][:, :, :],
                                  pM[:, 0:DH * P].rearrange("p (a b) -> p a b", a=DH),
                                  same[:, :, :], ALU.mult).then_inc(m_ev, 1)

            def y_low(p, par, t):
                dve.wait_ge(yhi_done, TT * (2 * p + par) + t + 1)
                hi, lo = (x[:, :, t * P:(t + 1) * P] for x in yp[par])
                dve.tensor_tensor(lo, pY[:, 0:DH * P].rearrange("p (h t) -> p h t", h=DH), hi.bitcast(F32),
                                  ALU.subtract).then_inc(ylo_done, 1)

            def total(p, par):
                i = 2 * p + par
                dve.wait_ge(o_mm, i + 1)
                dve.wait_ge(n_done, i + 1)
                wait(dve, stored[par], 16 * p)
                for h in range(2):
                    last_ = dve.tensor_tensor(z[par][:, 2 * h:2 * h + 2, :],
                                              pA[h][:, :].rearrange("p (t d) -> p t d", t=2),
                                              n_res[par][:, 2 * h:2 * h + 2, :], ALU.add)
                last_.then_inc(z_done, 1)

            for b in range(2):
                front.stats(dve, 0, b)
                front.norm(dve, 0, b)
            low(0, 0)
            queries_low(0, 0)
            keys_low(0, 0)
            for t in range(TT):
                keep_kv(0, 0, t)

            def body(p, par, first, last):
                ahead = not (isinstance(p, int) and p == END - 1)
                scores(p, par, 0)
                if not last:
                    low(*after(p, par))
                if not first:
                    y_low(*before(p, par), TT - 1)
                keep_state(p, par, 0)
                if ahead:
                    front.stats(dve, p + 1, par)
                scores(p, par, 1)
                y_low(p, par, 0)
                keep_state(p, par, 1)
                scores(p, par, 2)
                if not first:
                    total(*before(p, par))
                if not last:
                    queries_low(*after(p, par))
                y_low(p, par, 1)
                keep_state(p, par, 2)
                if ahead:
                    front.norm(dve, p + 1, par)
                if not last:
                    keys_low(*after(p, par))
                scores(p, par, 3)
                if not last:
                    keep_kv(*after(p, par), 0)
                    keep_kv(*after(p, par), 1)
                y_low(p, par, 2)
                keep_state(p, par, 3)
                if not last:
                    keep_kv(*after(p, par), 2)
                    keep_kv(*after(p, par), 3)

            rounds(dve, NBLK, body)
            y_low(END - 1, 1, TT - 1)
            total(END - 1, 1)

        @block.tensor
        def _(pe):
            def turn(p, par):
                wait(pe, kv_ev, TT * (2 * p + par))
                front.turn(pe, pA, p, par)

            def feature_major(p, par, name, done, emptied):
                i = 2 * p + par
                for sem, value in emptied:
                    wait(pe, sem, value)
                pe.wait_ge(hf_done, i + 1)
                pe.wait_ge(hlo_done, i + 1)
                for m in range(DH):
                    for k in range(DH):
                        mm = three_pass(pe, pA[m][:, :], tuple(x[:, k, m * P:(m + 1) * P] for x in w[name]),
                                        tuple(x[:, k, :] for x in hp), k == 0, k == DH - 1)
                mm.then_inc(done, 1)

            def token_major(p, par, t):
                i = 2 * p + par
                if t < 2:
                    pe.wait_ge(klo_done, i + 1)
                else:
                    pe.wait_ge(kv_ev, TT * i + t - 1)
                ts = slice(t * P, (t + 1) * P)
                for k in range(DH):
                    mm = three_pass(pe, pA[t % 2][:, :], tuple(x[:, k, ts] for x in hp),
                                    tuple(x[:, k, :] for x in wkv), k == 0, k == DH - 1)
                mm.then_inc(kv_mm, 1)

            def scores(p, par, t):
                i = 2 * p + par
                c = TT * i + t
                ts = slice(t * P, (t + 1) * P)
                if t == 0:
                    pe.wait_ge(klo_done, i + 1)
                pe.wait_ge(qEhi_done, c + 1)
                pe.wait_ge(qElo_done, c + 1)
                for h in range(DH):
                    for g in range(2):
                        j = 2 * h + g
                        wait(pe, s_ev, 4 * (c - 1) + j + 1)
                        heads = slice(QUAD * g, QUAD * (g + 1))
                        three_pass(pe, pS[j][:, :, :].rearrange("p o t -> p (o t)"), tuple(x[:, h, ts] for x in kp[par]),
                                   tuple(x[:, h, heads, :].rearrange("p o t -> p (o t)") for x in qE[t % 2]),
                                   True, True).then_inc(s_mm, 1)

            def add_state(p, par, t):
                if par == 1 and t == TT - 1:
                    return
                wait(pe, m_ev, states(p, par, t))
                if t == 0:
                    pe.wait_ge(kv_ev, TT * (2 * p + par + 1))
                for h in range(DH):
                    hs = slice(h * P, (h + 1) * P)
                    mm = pe.matmul(pM[:, hs], kv[par][:, t, hs], kv[par][:, t, D + h * P:D + (h + 1) * P],
                                   start=(par == 0 and t == 0 and h == 0), stop=True, skip_group_check=True)
                mm.then_inc(m_mm, 1)

            def output(p, par, t):
                c = TT * (2 * p + par) + t
                ts = slice(t * P, (t + 1) * P)
                wait(pe, ylo_done, c)
                pe.wait_ge(vE_done, c + 1)
                carried = not (par == 0 and t == 0)
                if carried:
                    pe.wait_ge(m_ev, states(p, par, t))
                for h in range(DH):
                    out = pY[:, h * P:(h + 1) * P]
                    if carried:
                        pe.matmul(out, state[(t - 1) % 2][:, h, :], qT[par][:, h, ts], start=True, stop=False)
                    for o in range(HH):
                        j = 2 * h + o // QUAD
                        if o % QUAD == 0:
                            pe.wait_ge(s_ev, 4 * c + j + 1)
                        mm = pe.matmul(out, vE[t % 2][:, h, o * P:(o + 1) * P], sT[t % 2][:, j, o % QUAD, :],
                                       start=o == 0 and not carried, stop=o == HH - 1)
                mm.then_inc(y_mm, 1)

            def project_out(p, par):
                i = 2 * p + par
                pe.wait_ge(ylo_done, TT * (i + 1))
                wait(pe, q_ev, min(i + 3, NBLK) if isinstance(i, int) else i + 3)
                for t in range(TT):
                    po = pA[t // 2][:, (t % 2) * D:(t % 2 + 1) * D]
                    ts = slice(t * P, (t + 1) * P)
                    for k in range(DH):
                        mm = three_pass(pe, po, tuple(x[:, k, ts] for x in yp[par]),
                                        tuple(x[:, k, :] for x in w["o"]), k == 0, k == DH - 1)
                mm.then_inc(o_mm, 1)

            turn(0, 0)
            feature_major(0, 0, "q", q_mm, [])
            feature_major(0, 0, "k", k_mm, [(q_ev, 1)])
            for t in range(TT):
                token_major(0, 0, t)

            def body(p, par, first, last):
                i = 2 * p + par
                nxt = after(p, par)
                prv = None if first else before(p, par)
                scores(p, par, 0)
                if not last:
                    turn(*nxt)
                if prv:
                    output(*prv, TT - 1)
                add_state(p, par, 0)
                scores(p, par, 1)
                output(p, par, 0)
                add_state(p, par, 1)
                if not last:
                    feature_major(*nxt, "q", q_mm, [])
                scores(p, par, 2)
                if prv:
                    project_out(*prv)
                output(p, par, 1)
                add_state(p, par, 2)
                if not last:
                    feature_major(*nxt, "k", k_mm, [(z_done, i), (q_ev, i + 2)])
                scores(p, par, 3)
                if not last:
                    token_major(*nxt, 0)
                    token_major(*nxt, 1)
                output(p, par, 2)
                add_state(p, par, 3)
                if not last:
                    token_major(*nxt, 2)
                    token_major(*nxt, 3)

            rounds(pe, NBLK, body)
            output(END - 1, 1, TT - 1)
            project_out(END - 1, 1)


HID = 1024
FT = HID // P
RING = 4


class Hidden:

    def __init__(self, ph):
        self.g = [ph.sb(f"g{n}", [P, BLK]) for n in range(RING)]
        self.gp = [ph.pair(f"gp{n}", [P, BLK]) for n in range(RING)]
        self.pg = [ph.ps(f"pg{n}", [P, BLK]) for n in range(RING)]
        self.mm = ph.sem("hid_mm")
        self.g_done = ph.sem("hid_gelu")
        self.hi_done = ph.sem("hid_hi")
        self.lo_done = ph.sem("hid_lo")
        self.used = ph.sem("hid_used")

    def up(self, pe, n, f, w, h, waits):
        s = f % RING
        for sem, value in waits:
            wait(pe, sem, value)
        wait(pe, self.g_done, n - RING + 1)
        for k in range(DH):
            mm = three_pass(pe, self.pg[s][:, :], tuple(x[:, k, f * P:(f + 1) * P] for x in w),
                            tuple(x[:, k, :] for x in h), k == 0, k == DH - 1)
        mm.then_inc(self.mm, 1)

    def gelu(self, act, n, f, bias):
        s = f % RING
        act.wait_ge(self.mm, n + 1)
        wait(act, self.lo_done, n - RING + 1)
        act.activation(self.g[s][:, :], self.pg[s][:, :], ACT.Gelu_apprx_tanh, bias=bias).then_inc(self.g_done, 1)

    def high(self, act, n, f):
        s = f % RING
        act.wait_ge(self.g_done, n + 1)
        wait(act, self.used, n - RING + 1)
        act.activation(self.gp[s][0][:, :], self.g[s][:, :], ACT.Identity).then_inc(self.hi_done, 1)

    def low(self, dve, n, f):
        s = f % RING
        dve.wait_ge(self.hi_done, n + 1)
        wait(dve, self.used, n - RING + 1)
        dve.tensor_tensor(self.gp[s][1][:, :], self.g[s][:, :], self.gp[s][0][:, :].bitcast(F32),
                          ALU.subtract).then_inc(self.lo_done, 1)

    def down(self, pe, n, f, w, banks):
        s = f % RING
        pe.wait_ge(self.lo_done, n + 1)
        for m in range(DH):
            mm = three_pass(pe, banks[m][:, :], tuple(x[:, f, m * P:(m + 1) * P] for x in w),
                            tuple(x[:, :] for x in self.gp[s]), f == 0, f == FT - 1)
        mm.then_inc(self.used, 1)
        return mm

    def down_tokens(self, pe, n, f, w, banks):
        s = f % RING
        pe.wait_ge(self.lo_done, n + 1)
        for t in range(TT):
            out = banks[t // 2][:, (t % 2) * D:(t % 2 + 1) * D]
            ts = slice(t * P, (t + 1) * P)
            (xh, xl), (wh, wl) = (x[:, ts] for x in self.gp[s]), (x[:, f, :] for x in w)
            first = f == 0 and t % 2 == 0
            pe.matmul(out, xl, wh, start=first, stop=False, skip_group_check=True)
            pe.matmul(out, xh, wl, start=False, stop=False, skip_group_check=True)
            mm = pe.matmul(out, xh, wh, start=False, stop=f == FT - 1, skip_group_check=True)
        mm.then_inc(self.used, 1)
        return mm


LEVELS = 3


def gelu_levels(nc, x_dram, n_dram, y_dram, consts, ln_g, ln_b, w1_d, b1_d, w2_d, b2_d, b2row_d):
    with ExitStack() as ctx:
        ph = Phase(nc, ctx, "gl")
        w1 = [ph.pair(f"w1_{l}", [P, DH, HID]) for l in range(LEVELS)]
        w2 = [ph.pair(f"w2_{l}", [P, FT, D]) for l in range(LEVELS)]
        gb = ph.sb("gb", [P, 2, DH])
        b1 = ph.sb("b1", [P, LEVELS, FT])
        b2 = ph.sb("b2", [P, LEVELS, DH])
        b2row = ph.sb("b2row", [P, D])
        flat = lambda t: tuple(x[:, :, :].rearrange("p a b -> p (a b)") for x in t)
        split = []
        for l in range(LEVELS):
            split += [(flat(w1[l]), w1_d[l]), (flat(w2[l]), w2_d[l])]
        load_weights(nc, "gll",
                     [(gb[:, 0, :], ln_g), (gb[:, 1, :], ln_b),
                      (b1[:, :, :].rearrange("p a b -> p (a b)"), b1_d),
                      (b2[:, :, :].rearrange("p a b -> p (a b)"), b2_d),
                      (b2row[:, :], b2row_d.unsqueeze(0).broadcast_to([P, D]))], split)
        front = Front(ph, n_dram, consts["ident"])
        back = Back(ph, front, y_dram)
        back.front = None
        xres = [ph.sb(f"xres{b}", [P, TT, D]) for b in range(2)]
        hf = [ph.sb(f"hf{b}", [P, DH, BLK]) for b in range(2)]
        hp = [ph.pair(f"hp{b}", [P, DH, BLK]) for b in range(2)]
        hid = Hidden(ph)
        pT = [ph.ps(f"pT{h}", [P, BLK]) for h in range(DH)]
        pH = [ph.ps(f"pH{h}", [P, BLK]) for h in range(DH)]
        xres_loaded = [ph.sem(f"xres_loaded{b}") for b in range(2)]
        moved = ph.sem("moved")
        hf_done = [ph.sem(f"hf{b}") for b in range(2)]
        hhi_done = [ph.sem(f"hhi{b}") for b in range(2)]
        hlo_done = [ph.sem(f"hlo{b}") for b in range(2)]
        z_done = ph.sem("z")
        block = ctx.enter_context(nc.Block())
        PAIRSOF = NBLK // 2

        def passes(eng, body):
            body(0, True, False)
            with eng.Fori(1, PAIRSOF - 1) as p:
                body(p, False, False)
            body(PAIRSOF - 1, False, True)

        def order(p):
            for l in range(LEVELS):
                for b in range(2):
                    yield 2 * LEVELS * p + 2 * l + b, l, b

        @block.sync
        def _(sp):
            def load_res(p, b):
                src = x_dram[bass.ds((2 * p + b) * BLK, BLK), :].rearrange("(t p) d -> p t d", p=P)
                sp.dma_start(xres[b][:, :, :], src).then_inc(xres_loaded[b], 16)

            for b in range(2):
                front.load(sp, 0, b)
            for b in range(2):
                load_res(0, b)

            def body(p, first, last):
                if not first:
                    back.store(sp, p - 1, 1)
                    load_res(p, 1)
                if not last:
                    for b in range(2):
                        sp.wait_ge(moved, 2 * p + b + 1)
                        front.load(sp, p + 1, b)
                back.store(sp, p, 0)
                if not last:
                    load_res(p + 1, 0)

            passes(sp, body)
            back.store(sp, PAIRSOF - 1, 1)
            back.all_stored(sp)

        @block.gpsimd
        def _(pool):
            def finish(p, b):
                back.rstd(pool, consts, p, b)
                pool.wait_ge(back.zn_done, 2 * p + b + 1)
                pool.wait_ge(xres_loaded[b], 16 * (p + 1))
                pool.tensor_tensor(back.z[b][:, :, :], back.z[b][:, :, :], xres[b][:, :, :],
                                   ALU.add).then_inc(back.added, 1)

            for b in range(2):
                front.rstd(pool, consts, 0, b)

            def body(p, first, last):
                if not first:
                    finish(p - 1, 1)
                for b in range(2):
                    pool.wait_ge(front.loaded[b], 16 * (p + 1))
                    back.z_free(pool, p, b)
                    pool.wait_ge(front.xn_done, 2 * p + b + 1)
                    pool.tensor_tensor(back.z[b][:, :, :], front.x[b][:, :, :],
                                       b2row[:, :].unsqueeze(1).broadcast_to([P, TT, D]), ALU.add).then_inc(moved, 1)
                if not last:
                    for b in range(2):
                        front.rstd(pool, consts, p + 1, b)
                finish(p, 0)

            passes(pool, body)
            finish(PAIRSOF - 1, 1)

        @block.scalar
        def _(act):
            def take(p, l, b):
                n = 3 * p + l
                if l == 0:
                    act.wait_ge(front.turned, 2 * p + b + 1)
                    banks = pT
                else:
                    act.wait_ge(hid.used, FT * (6 * p + 2 * (l - 1) + b + 1))
                    banks = pH
                wait(act, hlo_done[b], n)
                for h in range(DH):
                    if l == 0:
                        last_ = act.activation(hf[b][:, h, :], banks[h][:, :], ACT.Identity,
                                               bias=gb[:, 1, h:h + 1], scale=gb[:, 0, h:h + 1])
                    else:
                        last_ = act.activation(hf[b][:, h, :], banks[h][:, :], ACT.Identity,
                                               bias=b2[:, l - 1, h:h + 1])
                last_.then_inc(hf_done[b], 1)

            def high(p, l, b):
                n = 3 * p + l
                act.wait_ge(hf_done[b], n + 1)
                wait(act, hid.mm, FT * (2 * (3 * p + l - 1) + b + 1))
                act.activation(hp[b][0][:, :, :], hf[b][:, :, :], ACT.Identity).then_inc(hhi_done[b], 1)

            def body(p, first, last):
                if first:
                    take(0, 0, 0)
                    high(0, 0, 0)
                for o, l, b in order(p):
                    prev = (l, 0) if b else (l - 1, 1)
                    moves = prev[0] in range(LEVELS - 1)
                    if moves:
                        take(p, prev[0] + 1, prev[1])
                    for f in range(FT):
                        hid.gelu(act, FT * o + f, f, b1[:, l, f:f + 1])
                        hid.high(act, FT * o + f, f)
                        if f == 0 and moves:
                            high(p, prev[0] + 1, prev[1])
                        if f == 1 and (l, b) == (0, 0):
                            take(p, 0, 1)
                            high(p, 0, 1)
                        if f == 1 and (l, b) == (LEVELS - 1, 1) and not last:
                            take(p + 1, 0, 0)
                            high(p + 1, 0, 0)

            passes(act, body)

        @block.vector
        def _(dve):
            def halves(p, l, b):
                n = 3 * p + l
                dve.wait_ge(hf_done[b], n + 1)
                dve.wait_ge(hhi_done[b], n + 1)
                wait(dve, hid.mm, FT * (2 * (3 * p + l - 1) + b + 1))
                dve.tensor_tensor(hp[b][1][:, :, :], hf[b][:, :, :], hp[b][0][:, :, :].bitcast(F32),
                                  ALU.subtract).then_inc(hlo_done[b], 1)

            def out(p, b):
                dve.wait_ge(hid.used, FT * (6 * p + 4 + b + 1))
                dve.wait_ge(moved, 2 * p + b + 1)
                for h in range(2):
                    zz = back.z[b][:, 2 * h:2 * h + 2, :]
                    last_ = dve.tensor_tensor(zz, pH[h][:, :].rearrange("p (a b) -> p a b", a=2), zz, ALU.add)
                last_.then_inc(z_done, 1)

            def body(p, first, last):
                if first:
                    for b in range(2):
                        front.stats(dve, 0, b)
                        front.norm(dve, 0, b)
                    halves(0, 0, 0)
                for o, l, b in order(p):
                    prev = (l, 0) if b else (l - 1, 1)
                    ends = None
                    if (l, b) == (0, 0) and not first:
                        ends = (p - 1, 1)
                    if (l, b) == (LEVELS - 1, 1):
                        ends = (p, 0)
                    if ends:
                        out(*ends)
                    for f in range(FT):
                        hid.low(dve, FT * o + f, f)
                        if f == 0 and prev[0] in range(LEVELS - 1):
                            halves(p, prev[0] + 1, prev[1])
                        if f == 1 and ends:
                            back.stats(dve, z_done, 2 * ends[0] + ends[1] + 1, *ends)
                        if f == 2 and (l, b) == (0, 0):
                            halves(p, 0, 1)
                        if f == 2 and (l, b) == (LEVELS - 1, 1) and not last:
                            halves(p + 1, 0, 0)
                        if f == 4 and ends:
                            back.norm(dve, *ends)
                        if l == 1 and f == 2 and not last:
                            front.stats(dve, p + 1, b)
                        if l == 1 and f == 5 and not last:
                            front.norm(dve, p + 1, b)

            passes(dve, body)
            out(PAIRSOF - 1, 1)
            back.stats(dve, z_done, 2 * PAIRSOF, PAIRSOF - 1, 1)
            back.norm(dve, PAIRSOF - 1, 1)

        @block.tensor
        def _(pe):
            LAG = 3

            def body(p, first, last):
                if first:
                    front.turn(pe, pT, 0, 0)
                    pe.wait_ge(hf_done[0], 1)
                    front.turn(pe, pT, 0, 1)
                for o, l, b in order(p):
                    for f in range(FT + LAG):
                        if f == 4 and l == LEVELS - 1 and not last:
                            if b == 0:
                                pe.wait_ge(hf_done[1], 3 * p + 1)
                            else:
                                pe.wait_ge(hf_done[0], 3 * (p + 1) + 1)
                            front.turn(pe, pT, p + 1, b)
                        if f < FT:
                            waits = [(hf_done[b], 3 * p + l + 1), (hlo_done[b], 3 * p + l + 1)] if f == 0 else []
                            hid.up(pe, FT * o + f, f, w1[l], hp[b], waits)
                        g = f - LAG
                        if g == 0:
                            if (l, b) == (0, 0):
                                wait(pe, z_done, 2 * p)
                            elif (l, b) == (LEVELS - 1, 1):
                                pe.wait_ge(z_done, 2 * p + 1)
                            elif b == 1:
                                pe.wait_ge(hf_done[0], 3 * p + l + 2)
                            else:
                                pe.wait_ge(hf_done[1], 3 * p + l + 1)
                        if g >= 0:
                            if l < LEVELS - 1:
                                hid.down(pe, FT * o + g, g, w2[l], pH)
                            else:
                                hid.down_tokens(pe, FT * o + g, g, w2[l], pH)

            passes(pe, body)


EXPERTS = 8
GROUP = P // EXPERTS
SHARE = P // GROUP
CHUNKS = 2 * D * HID // (P * D)


def expert_weights(nc, x_dram, consts, shared, mw_dram, tw_d, base_d, gw1_d, gb1_d, gw2_d, gb2_d, esel_d,
                   delta_d, spread_d, tb1_d, b1_d, tb2_d, b2_d):
    mb1, mb2 = shared
    with ExitStack() as ctx:
        ph = Phase(nc, ctx, "eg")
        gw1 = ph.sb("gw1", [P, DH, D])
        gb1 = ph.sb("gb1", [P, DH])
        gw2 = ph.sb("gw2", [P, DH, EXPERTS])
        gb2 = ph.sb("gb2", [EXPERTS, 1])
        esel = ph.sb("esel", [EXPERTS, P])
        delta = ph.sb("delta", [P, GROUP])
        spread = ph.sb("spread", [P, SHARE, P])
        tb1 = ph.sb("tb1", [EXPERTS, HID])
        b1 = ph.sb("b1", [P, FT])
        tb2 = ph.sb("tb2", [EXPERTS, D])
        b2 = ph.sb("b2", [1, D])
        hsum = ph.sb("hsum", [P, NBLK, DH])
        mix = ph.sb("mix", [P, BATCH, GROUP])
        load_weights(nc, "egl", [
            (gw1[:, :, :].rearrange("p a b -> p (a b)"), gw1_d), (gb1[:, :], gb1_d),
            (gw2[:, :, :].rearrange("p a b -> p (a b)"), gw2_d), (gb2[:, :], gb2_d), (esel[:, :], esel_d),
            (delta[:, :], delta_d), (spread[:, :, :].rearrange("p a b -> p (a b)"), spread_d), (tb1[:, :], tb1_d), (b1[:, :], b1_d),
            (tb2[:, :], tb2_d), (b2[:, :], b2_d)], [])

        with ExitStack() as inner:
            gp = Phase(nc, inner, "g1")
            x, x_load = [gp.sb(f"x{b}", [P, TT, D]) for b in range(2)], [gp.sem(f"x_load{b}") for b in range(2)]
            front = TokenNorm(gp, "front")
            xT = [gp.sb(f"xT{b}", [P, DH, BLK]) for b in range(2)]
            junk = [gp.sb(f"junk{n}", [P, BLK]) for n in range(2 * DH)]
            accs = [gp.sb(f"acc{b}", [P, DH]) for b in range(2)]
            pT = [gp.ps(f"pT{h}", [P, BLK]) for h in range(DH)]
            pG = [gp.ps(f"pG{h}", [P, BLK]) for h in range(2 * DH)]
            turned, xT_done, g_mm = gp.sem("turned"), gp.sem("xT"), gp.sem("g_mm")
            summed, kept = gp.sem("summed"), gp.sem("kept")
            block = inner.enter_context(nc.Block())
            AHEAD, BEHIND = 4, 1

            @block.sync
            def _(sp):
                def load(p, par):
                    wait(sp, turned, 2 * p + par - 1)
                    src = x_dram[bass.ds((2 * p + par) * BLK, BLK), :].rearrange("(t p) d -> p t d", p=P)
                    sp.dma_start(x[par][:, :, :], src).then_inc(x_load[par], 16)

                skewed(sp, NBLK, AHEAD, BEHIND, lambda do: do(4, load))

            @block.gpsimd
            def _(pool):
                skewed(pool, NBLK, AHEAD, BEHIND,
                       lambda do: do(3, lambda p, par: front.factors(pool, consts, p, par)))

            @block.scalar
            def _(act):
                def take(p, par):
                    i = 2 * p + par
                    act.wait_ge(turned, i + 1)
                    wait(act, g_mm, i - 1)
                    for h in range(DH):
                        last_ = act.activation(xT[par][:, h, :], pT[h][:, :], ACT.Identity)
                    last_.then_inc(xT_done, 1)

                def relu(p, par):
                    i = 2 * p + par
                    act.wait_ge(g_mm, i + 1)
                    wait(act, kept, i - 1)
                    for h in range(DH):
                        last_ = act.activation(junk[DH * par + h][:, :], pG[DH * par + h][:, :], ACT.Relu,
                                               bias=gb1[:, h:h + 1], accum_out=accs[par][:, h:h + 1])
                    last_.then_inc(summed, 1)

                def body(do):
                    do(1, take)
                    do(2, lambda p, par: front.apply(act, x[par], x[par], p, par))
                    do(0, relu)

                skewed(act, NBLK, AHEAD, BEHIND, body)

            @block.vector
            def _(dve):
                def stats(p, par):
                    dve.wait_ge(x_load[par], 16 * (p + 1))
                    front.stats(dve, x[par], p, par)

                def keep(p, par):
                    i = 2 * p + par
                    dve.wait_ge(summed, i + 1)
                    dve.tensor_copy(hsum[:, bass.ds(i, 1), :], accs[par][:, :].unsqueeze(1)).then_inc(kept, 1)

                def body(do):
                    do(3, stats)
                    do(-1, keep)

                skewed(dve, NBLK, AHEAD, BEHIND, body)

            @block.tensor
            def _(pe):
                def gate(p, par):
                    i = 2 * p + par
                    pe.wait_ge(xT_done, i + 1)
                    wait(pe, summed, i - 1)
                    for m in range(DH):
                        for k in range(DH):
                            mm = pe.matmul(pG[DH * par + m][:, :], gw1[:, k, m * P:(m + 1) * P], xT[par][:, k, :],
                                           start=k == 0, stop=k == DH - 1)
                    mm.then_inc(g_mm, 1)

                def turn(p, par):
                    i = 2 * p + par
                    pe.wait_ge(front.done, i + 1)
                    wait(pe, xT_done, i)
                    for h in range(DH):
                        for t in range(TT):
                            last = pe.transpose(pT[h][:, t * P:(t + 1) * P], x[par][:, t, h * P:(h + 1) * P],
                                                consts["ident"][:, :])
                    last.then_inc(turned, 1)

                def body(do):
                    do(0, gate)
                    do(2, turn)

                skewed(pe, NBLK, AHEAD, BEHIND, body)

        with ExitStack() as inner:
            gp = Phase(nc, inner, "g2")
            hm = gp.sb("hm", [P, DH, BATCH])
            gT = gp.sb("gT", [EXPERTS, BATCH])
            gP = gp.sb("gP", [P, BATCH])
            gB = gp.sb("gB", [EXPERTS, BATCH, P])
            ones = gp.sb("ones", [EXPERTS, P])
            pg = gp.ps("pg", [P, BATCH])
            pe_ = gp.ps("pe", [P, BATCH])
            pb = gp.ps("pb", [P, FT, BATCH])
            pc = [gp.ps(f"pc{n}", [P, 2, D]) for n in range(BATCH // 2)]
            v, t = gp.sem("v"), gp.sem("t")
            block = inner.enter_context(nc.Block())

            @block.vector
            def _(dve):
                dve.memset(ones[:, :], 1.0).then_inc(v, 1)
                pairs = hsum[:, :, :].rearrange("p (b two) h -> p h b two", two=SEQ // BLK)
                dve.tensor_tensor(hm[:, :, :], pairs[:, :, :, 0], pairs[:, :, :, 1], ALU.add).then_inc(v, 1)
                dve.wait_ge(t, 1)
                dve.tensor_scalar(gT[:, :], pg[0:EXPERTS, :], 1.0 / SEQ, gb2[:, 0:1], ALU.mult,
                                  ALU.add).then_inc(v, 1)
                dve.wait_ge(v, 3)
                for b in range(BATCH):
                    last = dve.tensor_scalar(gB[:, b, :], ones[:, :], gT[:, b:b + 1], None, ALU.mult)
                last.then_inc(v, 1)
                dve.wait_ge(t, 2)
                dve.tensor_copy(gP[:, :], pe_[:, :]).then_inc(v, 1)
                dve.wait_ge(v, 5)
                for b in range(BATCH):
                    last = dve.tensor_scalar(mix[:, b, :], delta[:, :], gP[:, b:b + 1], None, ALU.mult)
                last.then_inc(v, 1)
                dve.wait_ge(t, 3)
                dve.tensor_tensor(mb1[:, :, :], pb[:, :, :].rearrange("p f b -> p b f"),
                                  b1[:, :].unsqueeze(1).broadcast_to([P, BATCH, FT]), ALU.add).then_inc(v, 1)
                dve.wait_ge(t, 4)
                for n in range(BATCH // 2):
                    last = dve.tensor_copy(mb2[:, 2 * n:2 * n + 2, :], pc[n][:, :, :])
                last.then_inc(v, 1)

            @block.tensor
            def _(pe):
                pe.wait_ge(v, 2)
                for h in range(DH):
                    mm = pe.matmul(pg[0:EXPERTS, :], gw2[:, h, :], hm[:, h, :], start=h == 0, stop=h == DH - 1)
                mm.then_inc(t, 1)
                pe.wait_ge(v, 3)
                pe.matmul(pe_[:, :], esel[:, :], gT[:, :], start=True, stop=True).then_inc(t, 1)
                for f in range(FT):
                    mm = pe.matmul(pb[:, f, :], tb1[:, f * P:(f + 1) * P], gT[:, :], start=True, stop=True)
                mm.then_inc(t, 1)
                pe.wait_ge(v, 4)
                for b in range(BATCH):
                    out = pc[b // 2][:, b % 2, :]
                    pe.matmul(out, gB[:, b, :], tb2[:, :], start=True, stop=False)
                    mm = pe.matmul(out, ones[0:1, :], b2[:, :], start=False, stop=True)
                mm.then_inc(t, 1)

        with ExitStack() as inner:
            gp = Phase(nc, inner, "g3")
            tw = [gp.sb(f"tw{b}", [P, SHARE, D]) for b in range(2)]
            base = [gp.sb(f"base{b}", [P, D]) for b in range(2)]
            mw = [gp.sb(f"mw{b}", [P, SHARE, D]) for b in range(2)]
            pw = [gp.ps(f"pw{n}", [P, 2, D]) for n in range(SHARE)]
            loaded = [gp.sem(f"loaded{b}") for b in range(2)]
            stored = [gp.sem(f"stored{b}") for b in range(2)]
            mm_done = gp.sem("mm")
            ev_act, ev_dve = gp.sem("ev_act"), gp.sem("ev_dve")
            block = inner.enter_context(nc.Block())

            @block.sync
            def _(sp):
                def load(p, par):
                    i = 2 * p + par
                    wait(sp, mm_done, 2 * (i - 1))
                    src = tw_d[bass.ds(i * P, P), :].rearrange("p (g n) -> p g n", n=D)
                    sp.dma_start(tw[par][:, :, :], src).then_inc(loaded[par], 16)
                    sp.dma_start(base[par][:, :], base_d[bass.ds(i * P, P), :]).then_inc(loaded[par], 16)

                def store(p, par):
                    i = 2 * p + par
                    sp.wait_ge(ev_act, i + 1)
                    sp.wait_ge(ev_dve, i + 1)
                    dst = mw_dram[bass.ds(i, 1), :, :, :].rearrange("i b (r g) n -> (i b r) g n", g=SHARE)
                    sp.dma_start(dst, mw[par][:, :, :]).then_inc(stored[par], 16)

                def body(do):
                    do(1, load)
                    do(-1, store)

                skewed(sp, CHUNKS, 1, 1, body)
                for s in stored:
                    sp.wait_ge(s, 16 * CHUNKS // 2)

            def leave(eng, g, copy, done):
                def stage(p, par):
                    i = 2 * p + par
                    eng.wait_ge(mm_done, 2 * i + g + 1)
                    wait(eng, stored[par], 16 * p)
                    for n in (2 * g, 2 * g + 1):
                        last = copy(mw[par][:, 2 * n:2 * n + 2, :], pw[4 * par + n][:, :, :])
                    last.then_inc(done, 1)
                return stage

            @block.scalar
            def _(act):
                first = leave(act, 0, lambda out, x: act.activation(out, x, ACT.Identity), ev_act)
                skewed(act, CHUNKS, 1, 1, lambda do: do(0, first))

            @block.vector
            def _(dve):
                second = leave(dve, 1, dve.tensor_copy, ev_dve)
                skewed(dve, CHUNKS, 1, 1, lambda do: do(0, second))

            @block.tensor
            def _(pe):
                def product(p, par):
                    i = 2 * p + par
                    pe.wait_ge(loaded[par], 32 * (p + 1))
                    for g in range(SHARE):
                        if g % 4 == 0:
                            wait(pe, (ev_act, ev_dve)[g // 4], i - 1)
                        out = pw[4 * par + g // 2][:, g % 2, :]
                        pe.matmul(out, mix[:, :, :].rearrange("p b h -> p (b h)"), tw[par][:, g, :],
                                  start=True, stop=False)
                        mm = pe.matmul(out, spread[:, g, :], base[par][:, :], start=False, stop=True)
                        if g % 4 == 3:
                            mm.then_inc(mm_done, 1)

                skewed(pe, CHUNKS, 1, 1, lambda do: do(0, product))


def batch_mlp(nc, x_dram, y_dram, consts, shared, mw_dram):
    mb1, mb2 = shared
    with ExitStack() as ctx:
        ph = Phase(nc, ctx, "bm")
        front = Front(ph, x_dram, consts["ident"])
        back = Back(ph, front, y_dram)
        xres = [ph.sb(f"xres{b}", [P, TT, D]) for b in range(2)]
        hf = [ph.sb(f"hf{b}", [P, DH, BLK]) for b in range(2)]
        hp = [ph.pair(f"hp{b}", [P, DH, BLK]) for b in range(2)]
        raw = ph.sb("raw", [P, 4, HID])
        w1 = [ph.pair(f"w1{b}", [P, DH, HID]) for b in range(2)]
        w2 = [ph.pair(f"w2{b}", [P, FT, D]) for b in range(2)]
        hid = Hidden(ph)
        pT = [ph.ps(f"pT{h}", [P, BLK]) for h in range(DH)]
        pH = [ph.ps(f"pH{h}", [P, BLK]) for h in range(DH)]
        raw_loaded = ph.sem("raw_loaded")
        whi_done, wlo_done = ph.sem("whi"), ph.sem("wlo")
        kept = ph.sem("kept")
        bias = [ph.sb(f"bias{b}", [P, FT]) for b in range(2)]
        bias_done = ph.sem("bias")
        hf_done, hhi_done, hlo_done = ph.sem("hf"), ph.sem("hhi"), ph.sem("hlo")
        z_done = ph.sem("z")
        block = ctx.enter_context(nc.Block())
        PER = SEQ // BLK
        Q = 2 * PER
        PASSES = NBLK // Q

        def passes(eng, body):
            body(0, True, False)
            with eng.Fori(1, PASSES - 1) as p:
                body(p, False, False)
            body(PASSES - 1, False, True)

        def at(p, q):
            return 2 * p + q // 2, q % 2

        def pieces(b):
            out = []
            for h in range(DH):
                out.append(tuple(x[:, h, :] for x in w1[b]))
            for h in range(2):
                out.append(tuple(x[:, h * 4:(h + 1) * 4, :].rearrange("p a b -> p (a b)") for x in w2[b]))
            return out

        @block.sync
        def _(sp):
            def load_w(b):
                for h in range(2):
                    half = slice(h * CHUNKS // 2, (h + 1) * CHUNKS // 2)
                    src = mw_dram[half, b, :, :].rearrange("c p n -> p c n")
                    dst = raw[:, 2 * h:2 * h + 2, :].rearrange("p a (c n) -> p (a c) n", n=D)
                    sp.dma_start(dst, src).then_inc(raw_loaded, 16)

            front.load(sp, 0, 0)
            load_w(0)
            front.load(sp, 0, 1)

            def body(p, first, last):
                for q in range(Q):
                    i = Q * p + q
                    if q % PER == 0 and not (last and q == PER):
                        sp.wait_ge(wlo_done, 4 * (2 * p + q // PER + 1))
                        load_w(2 * p + q // PER + 1)
                    if not (last and q >= Q - 2):
                        sp.wait_ge(kept, i + 1)
                        sp.wait_ge(front.xn_done, i + 1)
                        front.load(sp, at(p, q)[0] + 1, q % 2)
                    if not (first and q == 0):
                        back.store(sp, *before(*at(p, q)))

            passes(sp, body)
            back.store(sp, NBLK // 2 - 1, 1)
            back.all_stored(sp)

        @block.gpsimd
        def _(pool):
            front.rstd(pool, consts, 0, 0)
            front.rstd(pool, consts, 0, 1)

            def finish(pp, par):
                back.rstd(pool, consts, pp, par)
                pool.wait_ge(back.zn_done, 2 * pp + par + 1)
                pool.tensor_tensor(back.z[par][:, :, :], back.z[par][:, :, :], xres[par][:, :, :],
                                   ALU.add).then_inc(back.added, 1)

            def body(p, first, last):
                for q in range(Q):
                    i = Q * p + q
                    pp, par = at(p, q)
                    pool.wait_ge(front.loaded[par], 16 * (pp + 1))
                    wait(pool, back.added, i - 1)
                    pool.tensor_tensor(xres[par][:, :, :], front.x[par][:, :, :],
                                       consts["one"].unsqueeze(2).broadcast_to([P, TT, D]), ALU.mult).then_inc(kept, 1)
                    if not (first and q == 0):
                        finish(*before(pp, par))
                    if not (last and q >= Q - 2):
                        front.rstd(pool, consts, pp + 1, par)

            passes(pool, body)
            finish(NBLK // 2 - 1, 1)

        @block.scalar
        def _(act):
            def take(i, par):
                act.wait_ge(front.turned, i + 1)
                wait(act, hlo_done, i - 1)
                for h in range(DH):
                    last_ = act.activation(hf[par][:, h, :], pT[h][:, :], ACT.Identity)
                last_.then_inc(hf_done, 1)
                act.wait_ge(hf_done, i + 1)
                wait(act, hid.mm, FT * (i - 1))
                act.activation(hp[par][0][:, :, :], hf[par][:, :, :], ACT.Identity).then_inc(hhi_done, 1)

            def piece(batch, b, k):
                if k == 0:
                    act.wait_ge(raw_loaded, 32 * (batch + 1))
                    wait(act, hid.used, FT * PER * (batch - 1))
                act.activation(pieces(b)[k][0], raw[:, k, :], ACT.Identity).then_inc(whi_done, 1)

            for k in range(4):
                piece(0, 0, k)
            take(0, 0)

            def body(p, first, last):
                for q in range(Q):
                    i = Q * p + q
                    batch = 2 * p + q // PER
                    for f in range(FT):
                        if f == 0 and q % PER == 0:
                            act.wait_ge(bias_done, batch + 1)
                        hid.gelu(act, FT * i + f, f, bias[q // PER][:, f:f + 1])
                        hid.high(act, FT * i + f, f)
                        if f < 4 and q % PER == PER - 1 and not (last and q == Q - 1):
                            piece(batch + 1, (q // PER + 1) % 2, f)
                        if f == 5 and not (last and q == Q - 1):
                            take(i + 1, (q + 1) % 2)

            passes(act, body)

        @block.vector
        def _(dve):
            def halves(i, par):
                dve.wait_ge(hf_done, i + 1)
                dve.wait_ge(hhi_done, i + 1)
                wait(dve, hid.mm, FT * (i - 1))
                dve.tensor_tensor(hp[par][1][:, :, :], hf[par][:, :, :], hp[par][0][:, :, :].bitcast(F32),
                                  ALU.subtract).then_inc(hlo_done, 1)

            def piece(batch, b, k):
                dve.wait_ge(whi_done, 4 * batch + k + 1)
                if k == 0:
                    wait(dve, hid.used, FT * PER * (batch - 1))
                hi, lo = pieces(b)[k]
                dve.tensor_tensor(lo, raw[:, k, :], hi.bitcast(F32), ALU.subtract).then_inc(wlo_done, 1)

            def hidden_bias(batch, b):
                wait(dve, hid.g_done, FT * PER * (batch - 1))
                src = mb1[:, bass.ds(batch, 1), :].rearrange("p a f -> p (a f)")
                dve.tensor_tensor(bias[b][:, :], src, src, ALU.max).then_inc(bias_done, 1)

            def out(i, pp, par, batch):
                dve.wait_ge(hid.used, FT * (i + 1))
                back.z_free(dve, pp, par)
                for h in range(2):
                    bias = mb2[:, bass.ds(batch, 1), :] if not isinstance(batch, int) else mb2[:, batch:batch + 1, :]
                    last_ = dve.tensor_tensor(back.z[par][:, 2 * h:2 * h + 2, :],
                                              pH[h][:, :].rearrange("p (a b) -> p a b", a=2),
                                              bias.broadcast_to([P, 2, D]), ALU.add)
                last_.then_inc(z_done, 1)

            front.stats(dve, 0, 0)
            hidden_bias(0, 0)
            front.norm(dve, 0, 0)
            for k in range(4):
                piece(0, 0, k)
            halves(0, 0)
            front.stats(dve, 0, 1)
            front.norm(dve, 0, 1)

            def body(p, first, last):
                for q in range(Q):
                    i = Q * p + q
                    pp, par = at(p, q)
                    ends = None if first and q == 0 else before(pp, par)
                    if q % PER == PER - 1 and not (last and q == Q - 1):
                        hidden_bias(2 * p + q // PER + 1, (q // PER + 1) % 2)
                    if ends:
                        out(i - 1, *ends, 2 * p + (q - 1) // PER)
                    for f in range(FT):
                        hid.low(dve, FT * i + f, f)
                        if f < 4 and q % PER == PER - 1 and not (last and q == Q - 1):
                            piece(2 * p + q // PER + 1, (q // PER + 1) % 2, f)
                        if f == 1 and ends:
                            back.stats(dve, z_done, i, *ends)
                        if f == 4 and ends:
                            back.norm(dve, *ends)
                        if f == 5 and not (last and q == Q - 1):
                            halves(i + 1, (q + 1) % 2)
                        if not (last and q >= Q - 2):
                            if f == 3:
                                front.stats(dve, pp + 1, par)
                            if f == 6:
                                front.norm(dve, pp + 1, par)

            passes(dve, body)
            out(NBLK - 1, NBLK // 2 - 1, 1, BATCH - 1)
            back.stats(dve, z_done, NBLK, NBLK // 2 - 1, 1)
            back.norm(dve, NBLK // 2 - 1, 1)

        @block.tensor
        def _(pe):
            LAG = 3

            front.turn(pe, pT, 0, 0)

            def body(p, first, last):
                for q in range(Q):
                    i = Q * p + q
                    b = q // PER
                    for f in range(FT + LAG):
                        if f == 3 and not (last and q == Q - 1):
                            pe.wait_ge(hf_done, i + 1)
                            front.turn(pe, pT, *after(*at(p, q)))
                        if f < FT:
                            waits = [(hlo_done, i + 1), (wlo_done, 4 * (2 * p + b + 1))] if f == 0 else []
                            hid.up(pe, FT * i + f, f, w1[b], hp[q % 2], waits)
                        g = f - LAG
                        if g == 0:
                            wait(pe, z_done, i)
                        if g >= 0:
                            hid.down_tokens(pe, FT * i + g, g, w2[b], pH)

            passes(pe, body)


FILT = 64
EMB = 3
INNER = 3 * D
HALF = SEQ // 2
KT = HALF // P
IT = INNER // P
TWO_PI = 2 * np.pi
ROUND = 1.5 * 2.0 ** 23


def two_pi_parts():
    a = np.float32(6.28125)
    b = np.float32(round((TWO_PI - float(a)) * 2 ** 20) / 2 ** 20)
    return float(a), float(b), float(np.float32(TWO_PI - float(a) - float(b)))


def long_filter(nc, consts, shared, plain, split, z_d, t_d, decay_d, w1_d, w2_d, w3_d, wo_d, b_d, freq_d, fb_d, half_d):
    cos_m, sin_m, ks = shared
    with ExitStack() as ctx:
        ph = Phase(nc, ctx, "lf")
        z = ph.sb("z", [EMB, SEQ])
        tcol = ph.sb("tcol", [P, KT, 2])
        dec = ph.sb("dec", [P, D])
        ws = [ph.sb("w1", [EMB, FILT]), ph.sb("w2", [FILT, FILT]), ph.sb("w3", [FILT, FILT])]
        wo = ph.sb("wo", [FILT, D])
        bs = ph.sb("bs", [FILT, 3])
        freq = ph.sb("freq", [FILT, 1])
        fb = ph.sb("fb", [1, D])
        hc = ph.sb("hc", [P, 3, KT])
        load_weights(nc, "lfl", [
            (z[:, :], z_d), (tcol[:, :, :].rearrange("p a b -> p (a b)"), t_d),
            (dec[:, :], decay_d.unsqueeze(0).broadcast_to([P, D])), (ws[0][:, :], w1_d), (ws[1][:, :], w2_d),
            (ws[2][:, :], w3_d), (wo[:, :], wo_d), (bs[:, :], b_d), (freq[:, :], freq_d), (fb[:, :], fb_d),
            (hc[:, :, :].rearrange("p a b -> p (a b)"), half_d)] + plain, split)
        h = [ph.sb(f"h{n}", [FILT, SEQ]) for n in range(3)]
        a, n, r = (ph.sb(x, [FILT, SEQ]) for x in "anr")
        env = ph.sb("env", [P, KT, 2, D])
        kf = ph.sb("kf", [P, KT, 2, D])
        kp = ph.pair("kp", [P, KT, 2, D])
        t1 = ph.sb("t1", [P, KT, 5, D])
        ph_ = [ph.ps(f"ph{x}", [P, HALF]) for x in range(2)]
        pk = [ph.ps(f"pk{x}", [P, 2, D]) for x in range(2)]
        pf = [ph.ps(f"pf{x}", [P, 2, D]) for x in range(4)]
        v, v3, s, t = ph.sem("v"), ph.sem("v3"), ph.sem("s"), ph.sem("t")
        block = ctx.enter_context(nc.Block())
        LAYER = 8

        @block.tensor
        def _(pe):
            for l in range(3):
                src = z if l == 0 else h[l - 1]
                if l:
                    pe.wait_ge(s, l)
                for c in range(2):
                    mm = pe.matmul(ph_[c][0:FILT, :], ws[l][:, :], src[:, c * HALF:(c + 1) * HALF],
                                   start=True, stop=True)
                mm.then_inc(t, 1)
            pe.wait_ge(s, 3)
            samples = h[2][:, :].rearrange("p (k s r) -> p k r s", k=KT, r=2)
            for k in range(KT):
                if k >= 2:
                    pe.wait_ge(v, 3 * LAYER + k - 1)
                for q in range(2):
                    mm = pe.matmul(pk[k % 2][:, q, :], samples[:, k, q, :], wo[:, :], start=True, stop=True)
                mm.then_inc(t, 1)
            pe.wait_ge(v, 3 * LAYER + KT + 2)
            for k in range(KT):
                if k >= 2:
                    pe.wait_ge(v, 3 * LAYER + KT + 2 + 3 * (k - 1))
                for x, m in enumerate((cos_m, sin_m)):
                    for q in range(KT):
                        out = pf[2 * (k % 2) + x][:, :, :].rearrange("p a b -> p (a b)")
                        mm = three_pass(pe, out, tuple(w[:, q, k * P:(k + 1) * P] for w in m),
                                        tuple(w[:, q, :, :].rearrange("p a b -> p (a b)") for w in kp),
                                        q == 0, q == KT - 1)
                mm.then_inc(t, 1)

        @block.scalar
        def _(act):
            for l in range(3):
                act.wait_ge(v, LAYER * (l + 1))
                act.activation(h[l][:, :], r[:, :], ACT.Sin).then_inc(s, 1)
            for k in range(KT):
                for q in range(2):
                    last = act.activation(env[:, k, q, :], dec[:, :], ACT.Exp, scale=tcol[:, k, q:q + 1])
            last.then_inc(s, 1)
            act.wait_ge(v, 3 * LAYER + KT + 1)
            act.activation(kp[0][:, :, :, :], kf[:, :, :, :], ACT.Identity).then_inc(s, 1)

        @block.vector
        def _(dve):
            p1, p2, p3 = two_pi_parts()
            count = [0]

            def step(ins):
                count[0] += 1
                ins.then_inc(v, 1)
                dve.wait_ge(v, count[0])

            for l in range(3):
                dve.wait_ge(t, l + 1)
                if l:
                    dve.wait_ge(s, l)
                for c in range(2):
                    cs = slice(c * HALF, (c + 1) * HALF)
                    step(dve.tensor_scalar(a[:, cs], ph_[c][0:FILT, :], bs[:, l:l + 1], freq[:, 0:1], ALU.add, ALU.mult))
                step(dve.tensor_scalar(n[:, :], a[:, :], 1 / TWO_PI, ROUND, ALU.mult, ALU.add))
                step(dve.tensor_scalar(n[:, :], n[:, :], ROUND, None, ALU.subtract))
                step(dve.scalar_tensor_tensor(a[:, :], n[:, :], -p1, a[:, :], ALU.mult, ALU.add))
                step(dve.scalar_tensor_tensor(a[:, :], n[:, :], -p2, a[:, :], ALU.mult, ALU.add))
                step(dve.scalar_tensor_tensor(r[:, :], n[:, :], -p3, a[:, :], ALU.mult, ALU.add))
                step(dve.tensor_scalar(r[:, :], r[:, :], 3.1415925, -3.1415925, ALU.min, ALU.max))
            dve.wait_ge(s, 4)
            for k in range(KT):
                dve.wait_ge(t, 3 + k + 1)
                step(dve.tensor_tensor(kf[:, k, :, :], pk[k % 2][:, :, :], env[:, k, :, :], ALU.mult))
            step(dve.tensor_tensor(kf[0:1, 0, 0, :], kf[0:1, 0, 0, :], fb[:, :], ALU.add))
            dve.wait_ge(s, 5)
            step(dve.tensor_tensor(kp[1][:, :, :, :], kf[:, :, :, :], kp[0][:, :, :, :].bitcast(F32), ALU.subtract))
            for k in range(KT):
                dve.wait_ge(t, 3 + KT + k + 1)
                re, im = pf[2 * (k % 2)], pf[2 * (k % 2) + 1]
                c_, s_, ms = (hc[:, x, k:k + 1] for x in range(3))
                dve.tensor_scalar(t1[:, k, 0, :], re[:, 0, :], ms, None, ALU.mult)
                dve.tensor_scalar(t1[:, k, 1, :], im[:, 0, :], s_, None, ALU.mult)
                dve.tensor_scalar(t1[:, k, 2, :], re[:, 1, :], s_, None, ALU.mult)
                dve.tensor_scalar(t1[:, k, 3, :], im[:, 1, :], s_, None, ALU.mult)
                step(dve.tensor_scalar(t1[:, k, 4, :], im[:, 1, :], ms, None, ALU.mult))
                stt = dve.scalar_tensor_tensor
                stt(ks[:, k, 0, 1, :], re[:, 0, :], c_, t1[:, k, 1, :], ALU.mult, ALU.add)
                stt(ks[:, k, 1, 1, :], im[:, 0, :], c_, t1[:, k, 0, :], ALU.mult, ALU.add)
                stt(ks[:, k, 0, 2, :], re[:, 1, :], c_, t1[:, k, 4, :], ALU.mult, ALU.add)
                stt(ks[:, k, 1, 2, :], im[:, 1, :], c_, t1[:, k, 2, :], ALU.mult, ALU.add)
                step(stt(ks[:, k, 0, 0, :], re[:, 1, :], c_, t1[:, k, 3, :], ALU.mult, ALU.add))
                dve.tensor_scalar(t1[:, k, 2, :], re[:, 1, :], ms, None, ALU.mult).then_inc(v3, 1)
                dve.wait_ge(v3, k + 1)
                step(stt(ks[:, k, 1, 0, :], im[:, 1, :], c_, t1[:, k, 2, :], ALU.mult, ALU.add))


def hyena(nc, x_dram, y_dram, consts, cos_d, sin_d, filter_args, in_w, in_b, sw_d, sb_d, out_w, outb_d):
    with ExitStack() as ctx:
        ph = Phase(nc, ctx, "hy")
        cos_m = ph.pair("cos", [P, KT, HALF])
        sin_m = ph.pair("sin", [P, KT, HALF])
        ks = ph.sb("ks", [P, KT, 2, 3, D])
        flat = lambda t: tuple(x[:, :, :].rearrange("p a b -> p (a b)") for x in t)
        wi = ph.pair("wi", [P, DH, INNER])
        wo = ph.pair("wo", [P, DH, D])
        inb = ph.sb("inb", [P, IT])
        sw = ph.sb("sw", [P, 3, IT])
        sbias = ph.sb("sbias", [P, IT])
        outb = ph.sb("outb", [P, D])
        long_filter(nc, consts, (cos_m, sin_m, ks),
                    [(inb[:, :], in_b), (sw[:, :, :].rearrange("p a b -> p (a b)"), sw_d), (sbias[:, :], sb_d),
                     (outb[:, :], outb_d.unsqueeze(0).broadcast_to([P, D]))],
                    [(flat(cos_m), cos_d), (flat(sin_m), sin_d), (flat(wi), in_w), (flat(wo), out_w)], *filter_args)
        x = ph.sb("x", [P, 2 * TT, D])
        hp = [ph.pair(f"hp{b}", [P, DH, BLK]) for b in range(2)]
        up = [ph.sb(f"up{b}", [P, SEQ + 2]) for b in range(2)]
        acc = ph.sb("acc", [P, SEQ])
        x0 = [ph.sb(f"x0{b}", [P, DH, SEQ]) for b in range(2)]
        vx = ph.sb("vx", [P, DH, SEQ])
        yp = ph.pair("yp", [P, DH, SEQ])
        vT = ph.pair("vT", [P, KT, 2, D])
        NPM = 4
        pm = [ph.sb(f"pm{n}", [P, 2, 2, D]) for n in range(NPM)]
        yf = ph.sb("yf", [P, 4, D])
        yk = ph.pair("yk", [P, 4, D])
        zy = ph.sb("zy", [P, 2 * SEQ])
        zy_h = zy[:, :].rearrange("p (h t) -> p h t", h=DH)
        yv = zy[:, :].rearrange("p (h t r) -> p h r t", h=DH, r=2)
        z = zy[:, :].rearrange("p (t d) -> p t d", d=D)
        residual = [t[:, :, :].rearrange("p a (b d) -> p (a b) d", d=D) for t in x0]
        front = TokenNorm(ph, "front", 2 * TT)
        back = TokenNorm(ph, "back", 2 * TT)
        pE = [ph.ps(f"pE{n}", [P, BLK]) for n in range(2)]
        pF = [ph.ps(f"pF{n}", [P, BLK]) for n in range(2)]
        pG = [ph.ps(f"pG{n}", [P, BLK]) for n in range(4)]
        x_loaded = ph.sem("x_loaded")
        res_loaded = [ph.sem(f"res_loaded{b}") for b in range(2)]
        stored = ph.sem("stored")
        turned = ph.sem("turned")
        padded = ph.sem("padded")
        hhi, hlo = ph.sem("hhi"), ph.sem("hlo")
        in_mm, up_done, t0_done = ph.sem("in_mm"), ph.sem("up"), ph.sem("t0")
        cv = ph.sem("cv")
        vT_mm, vT_hi, vT_lo = ph.sem("vT_mm"), ph.sem("vT_hi"), ph.sem("vT_lo")
        f_mm, i_mm = ph.sem("f_mm"), ph.sem("i_mm")
        mul = ph.sem("mul")
        comb = ph.sem("comb")
        half = ph.sem("half")
        y_hi, y_lo = ph.sem("y_hi"), ph.sem("y_lo")
        yv_done, yv_hi, yv_lo = ph.sem("yv"), ph.sem("yv_hi"), ph.sem("yv_lo")
        out_mm, z_done = ph.sem("out_mm"), ph.sem("z")
        added = ph.sem("added")
        block = ctx.enter_context(nc.Block())

        ORDER = [(DH, "x1", 0), (2 * DH, "v", 0), (DH + 1, "x1", 1), (2 * DH + 1, "v", 1), (0, "x0", 0), (1, "x0", 1)]
        STEPS = [2, 3, 2, 3, 2, 2]
        CV = sum(STEPS)
        AHEAD, BEHIND = 2, 1

        def cv_at(i, n):
            return CV * i + sum(STEPS[:n + 1])

        def upto(count, most):
            return min(count, most) if isinstance(count, int) else count

        @block.sync
        def _(sp):
            def load_residual(p, par):
                i = 2 * p + par
                sp.wait_ge(yv_done, 4 * (i + 1))
                src = x_dram[bass.ds(i * SEQ, SEQ), :].rearrange("(t p) d -> p t d", p=P)
                sp.dma_start(residual[par], src).then_inc(res_loaded[par], 16)

            def load(p, par):
                i = 2 * p + par
                for b in range(2):
                    wait(sp, turned, 2 * (i - 1) + b + 1)
                    src = x_dram[bass.ds(i * SEQ + b * BLK, BLK), :].rearrange("(t p) d -> p t d", p=P)
                    sp.dma_start(x[:, b * TT:(b + 1) * TT, :], src).then_inc(x_loaded, 16)

            def store(p, par):
                i = 2 * p + par
                sp.wait_ge(added, i + 1)
                dst = y_dram[bass.ds(i * SEQ, SEQ), :].rearrange("(t p) d -> p t d", p=P)
                sp.dma_start(dst, z).then_inc(stored, 16)

            def body(do):
                do(-1, load_residual)
                do(2, load)
                do(-1, store)

            skewed(sp, BATCH, AHEAD, BEHIND, body)
            sp.wait_ge(stored, 16 * BATCH)

        @block.gpsimd
        def _(pool):
            def sums(k):
                def stage(p, par):
                    i = 2 * p + par
                    for o in range(4):
                        n = 16 * i + 4 * k + o
                        m = pm[o]
                        pool.wait_ge(mul, n + 1)
                        pool.tensor_tensor(m[:, 0, :, :], m[:, 0, :, :], m[:, 1, :, :],
                                           ALU.subtract if o % 2 == 0 else ALU.add).then_inc(comb, 1)
                        pool.wait_ge(comb, n + 1)
                        if o == 0:
                            wait(pool, y_lo, 4 * i + k)
                        pool.tensor_tensor(yf[:, o, :], m[:, 0, 0, :], m[:, 0, 1, :], ALU.add).then_inc(half, 1)
                return stage

            def add(p, par):
                pool.wait_ge(back.done, 2 * p + par + 1)
                pool.wait_ge(res_loaded[par], 16 * (p + 1))
                pool.tensor_tensor(z, z, residual[par], ALU.add).then_inc(added, 1)

            def body(do):
                do(0, sums(0))
                do(-1, lambda p, par: back.factors(pool, consts, p, par))
                do(0, sums(1))
                do(-1, add)
                do(0, sums(2))
                do(2, lambda p, par: front.factors(pool, consts, p, par))
                do(0, sums(3))

            skewed(pool, BATCH, AHEAD, BEHIND, body)

        @block.scalar
        def _(act):
            def high(b):
                def stage(p, par):
                    i = 2 * p + par
                    act.wait_ge(turned, 2 * i + b + 1)
                    wait(act, in_mm, 12 * i)
                    for h in range(DH):
                        last = act.activation(hp[b][0][:, h, :], pE[h][:, :], ACT.Identity)
                    last.then_inc(hhi, 1)
                return stage

            def tile(n):
                def stage(p, par):
                    i = 2 * p + par
                    m, u = ORDER[n][0], up[n % 2]
                    wait(act, cv, cv_at(i, n - 2) if n >= 2 else cv_at(i - 1, n + len(ORDER) - 2))
                    for b in range(2):
                        act.wait_ge(in_mm, 12 * i + 2 * n + b + 1)
                        act.activation(u[:, 2 + b * BLK:2 + (b + 1) * BLK], pE[b][:, :], ACT.Identity,
                                       bias=inb[:, m:m + 1]).then_inc(up_done, 1)
                    act.wait_ge(up_done, 12 * i + 2 * n + 2)
                    wait(act, cv, cv_at(i, n - 1) if n else CV * i)
                    act.activation(acc[:, :], u[:, 2:SEQ + 2], ACT.Identity, bias=sbias[:, m:m + 1],
                                   scale=sw[:, 2, m:m + 1]).then_inc(t0_done, 1)
                return stage

            def vt_high(qs):
                def stage(p, par):
                    i = 2 * p + par
                    wait(act, f_mm, 4 * i)
                    for q in qs:
                        act.wait_ge(vT_mm, 4 * i + q + 1)
                        act.activation(vT[0][:, q, :, :], pE[q % 2][:, :].rearrange("p (r c) -> p r c", r=2),
                                       ACT.Identity).then_inc(vT_hi, 1)
                return stage

            def y_high(k):
                def stage(p, par):
                    i = 2 * p + par
                    act.wait_ge(half, 16 * i + 4 * (k + 1))
                    wait(act, i_mm, 4 * i + k)
                    act.activation(yk[0][:, :, :], yf[:, :, :], ACT.Identity).then_inc(y_hi, 1)
                return stage

            def yv_high(p, par):
                i = 2 * p + par
                act.wait_ge(yv_done, 4 * (i + 1))
                wait(act, out_mm, 4 * i)
                act.activation(yp[0][:, :, :], zy_h, ACT.Identity).then_inc(yv_hi, 1)

            def body(do):
                do(1, high(0))
                do(-1, yv_high)
                do(1, high(1))
                do(1, tile(0))
                do(0, y_high(0))
                do(1, tile(1))
                do(1, tile(2))
                do(0, y_high(1))
                do(-1, lambda p, par: back.apply(act, z, z, p, par))
                do(1, tile(3))
                do(0, y_high(2))
                do(1, tile(4))
                do(1, tile(5))
                do(1, vt_high((0, 1)))
                do(0, y_high(3))
                do(2, lambda p, par: front.apply(act, x, x, p, par))
                do(1, vt_high((2, 3)))

            act.wait_ge(padded, 1)
            skewed(act, BATCH, AHEAD, BEHIND, body)

        @block.vector
        def _(dve):
            def front_stats(p, par):
                dve.wait_ge(x_loaded, 32 * (2 * p + par + 1))
                front.stats(dve, x, p, par)

            def low(b):
                def stage(p, par):
                    i = 2 * p + par
                    dve.wait_ge(hhi, 2 * i + b + 1)
                    for h in range(DH):
                        last = dve.tensor_tensor(hp[b][1][:, h, :], pE[h][:, :], hp[b][0][:, h, :].bitcast(F32),
                                                 ALU.subtract)
                    last.then_inc(hlo, 1)
                return stage

            def conv(n):
                def stage(p, par):
                    i = 2 * p + par
                    m, kind, h = ORDER[n]
                    u = up[n % 2]
                    base = CV * i + sum(STEPS[:n])
                    if n == 0:
                        wait(dve, vT_mm, 4 * i)
                    if kind == "x0":
                        wait(dve, added, i - 1)
                    dve.wait_ge(t0_done, 6 * i + n + 1)
                    dve.scalar_tensor_tensor(acc[:, :], u[:, 1:SEQ + 1], sw[:, 1, m:m + 1], acc[:, :],
                                             ALU.mult, ALU.add).then_inc(cv, 1)
                    dve.wait_ge(cv, base + 1)
                    dst = {"x1": vx[:, h, :], "v": acc[:, :], "x0": x0[par][:, h, :]}[kind]
                    dve.scalar_tensor_tensor(dst, u[:, 0:SEQ], sw[:, 0, m:m + 1], acc[:, :],
                                             ALU.mult, ALU.add).then_inc(cv, 1)
                    if kind == "v":
                        dve.wait_ge(cv, base + 2)
                        dve.tensor_tensor(vx[:, h, :], acc[:, :], vx[:, h, :], ALU.mult).then_inc(cv, 1)
                return stage

            def vt_low(qs):
                def stage(p, par):
                    for q in qs:
                        dve.wait_ge(vT_hi, 4 * (2 * p + par) + q + 1)
                        dve.tensor_tensor(vT[1][:, q, :, :], pE[q % 2][:, :].rearrange("p (r c) -> p r c", r=2),
                                          vT[0][:, q, :, :].bitcast(F32), ALU.subtract).then_inc(vT_lo, 1)
                return stage

            def products(k, parts=range(4)):
                def stage(p, par):
                    i = 2 * p + par
                    re, im = (pF[n][:, :].rearrange("p (r c) -> p r c", r=2) for n in range(2))
                    dve.wait_ge(f_mm, 4 * i + k + 1)
                    for o in parts:
                        m = pm[o]
                        slot = slice(1, 3) if o < 2 else slice(0, 2)
                        a, b = (re, im) if o % 2 == 0 else (im, re)
                        wait(dve, half, 16 * i + 4 * k + o - NPM + 1)
                        dve.tensor_tensor(m[:, 0, :, :], a, ks[:, k, 0, slot, :], ALU.mult)
                        dve.tensor_tensor(m[:, 1, :, :], b, ks[:, k, 1, slot, :], ALU.mult).then_inc(mul, 1)
                return stage

            def y_low(k):
                def stage(p, par):
                    dve.wait_ge(y_hi, 4 * (2 * p + par) + k + 1)
                    dve.tensor_tensor(yk[1][:, :, :], yf[:, :, :], yk[0][:, :, :].bitcast(F32),
                                      ALU.subtract).then_inc(y_lo, 1)
                return stage

            def times_x0(p, par):
                i = 2 * p + par
                dve.wait_ge(i_mm, 4 * (i + 1))
                wait(dve, stored, 16 * i)
                for h in range(DH):
                    for r in range(2):
                        dve.tensor_tensor(yv[:, h, r, :], pG[2 * h + r][:, :],
                                          x0[par][:, h, :].rearrange("p (t r) -> p r t", r=2)[:, r, :],
                                          ALU.mult).then_inc(yv_done, 1)

            def yv_low(p, par):
                i = 2 * p + par
                dve.wait_ge(yv_hi, i + 1)
                dve.tensor_tensor(yp[1][:, :, :], zy_h, yp[0][:, :, :].bitcast(F32), ALU.subtract).then_inc(yv_lo, 1)

            def leave(ns):
                def stage(p, par):
                    i = 2 * p + par
                    dve.wait_ge(yv_lo, i + 1)
                    for n in ns:
                        dve.wait_ge(out_mm, 4 * i + n + 1)
                        dve.tensor_tensor(z[:, 2 * n:2 * n + 2, :], pE[n % 2][:, :].rearrange("p (t d) -> p t d", t=2),
                                          outb[:, :].unsqueeze(1).broadcast_to([P, 2, D]), ALU.add).then_inc(z_done, 1)
                return stage

            def back_stats(p, par):
                dve.wait_ge(z_done, 4 * (2 * p + par + 1))
                back.stats(dve, z, p, par)

            def body(do):
                do(1, low(0))
                do(-1, yv_low)
                do(1, low(1))
                do(0, products(0, (0, 1)))
                do(-1, leave((0, 1)))
                do(0, products(0, (2, 3)))
                do(-1, leave((2, 3)))
                do(-1, back_stats)
                do(1, conv(0))
                do(0, y_low(0))
                do(0, products(1))
                do(1, conv(1))
                do(1, conv(2))
                do(0, y_low(1))
                do(0, products(2))
                do(2, front_stats)
                do(1, conv(3))
                do(0, products(3, (0, 1)))
                do(0, y_low(2))
                do(0, products(3, (2, 3)))
                do(1, conv(4))
                do(1, conv(5))
                do(1, vt_low((0, 1)))
                do(0, y_low(3))
                do(1, vt_low((2, 3)))
                do(0, times_x0)

            dve.memset(up[0][:, 0:2], 0.0)
            dve.memset(up[1][:, 0:2], 0.0).then_inc(padded, 1)
            skewed(dve, BATCH, AHEAD, BEHIND, body)

        @block.tensor
        def _(pe):
            def turn(b):
                def stage(p, par):
                    i = 2 * p + par
                    pe.wait_ge(front.done, i + 1)
                    if b == 0:
                        wait(pe, vT_lo, 4 * i)
                    else:
                        pe.wait_ge(hlo, 2 * i + 1)
                    for h in range(DH):
                        for t in range(TT):
                            last = pe.transpose(pE[h][:, t * P:(t + 1) * P], x[:, b * TT + t, h * P:(h + 1) * P],
                                                consts["ident"][:, :])
                    last.then_inc(turned, 1)
                return stage

            def project(n):
                def stage(p, par):
                    i = 2 * p + par
                    m = ORDER[n][0]
                    pe.wait_ge(hlo, 2 * i + 2)
                    for b in range(2):
                        if n == 0:
                            wait(pe, z_done, 4 * (i - 2) + 3 + b)
                        else:
                            pe.wait_ge(up_done, 12 * i + 2 * n + b - 1)
                        for k in range(DH):
                            mm = three_pass(pe, pE[b][:, :], tuple(w[:, k, m * P:(m + 1) * P] for w in wi),
                                            tuple(t[:, k, :] for t in hp[b]), k == 0, k == DH - 1)
                        mm.then_inc(in_mm, 1)
                return stage

            def turn_vx(qs):
                def stage(p, par):
                    i = 2 * p + par
                    pe.wait_ge(cv, cv_at(i, 3))
                    for q in qs:
                        pe.wait_ge(*((up_done, 12 * i + 11 + q) if q < 2 else (vT_lo, 4 * i + q - 1)))
                        for r in range(2):
                            for h in range(DH):
                                src = vx[:, h, :].rearrange("p (q s r) -> p q r s", q=KT, r=2)[:, q, r, :]
                                mm = pe.transpose(pE[q % 2][:, r * D + h * P:r * D + (h + 1) * P], src,
                                                  consts["ident"][:, :])
                        mm.then_inc(vT_mm, 1)
                return stage

            def forward(k, parts=(0, 1)):
                def stage(p, par):
                    i = 2 * p + par
                    if k == 0:
                        pe.wait_ge(vT_lo, 4 * (i + 1))
                    wait(pe, mul, 16 * i + 4 * k)
                    for n in parts:
                        m = (cos_m, sin_m)[n]
                        for q in range(KT):
                            mm = three_pass(pe, pF[n][:, :], tuple(w[:, q, k * P:(k + 1) * P] for w in m),
                                            tuple(v[:, q, :, :].rearrange("p r c -> p (r c)") for v in vT),
                                            q == 0, q == KT - 1)
                    if parts[-1] == 1:
                        mm.then_inc(f_mm, 1)
                return stage

            def inverse(k, halves=range(DH)):
                def stage(p, par):
                    i = 2 * p + par
                    pe.wait_ge(y_lo, 4 * i + k + 1)
                    if k == 0:
                        wait(pe, yv_done, 4 * i)
                    for h in halves:
                        for r in range(2):
                            for n, m in enumerate((cos_m, sin_m)):
                                mm = three_pass(pe, pG[2 * h + r][:, :],
                                                tuple(y[:, 2 * r + n, h * P:(h + 1) * P] for y in yk),
                                                tuple(w[:, k, :] for w in m), k == 0 and n == 0,
                                                k == KT - 1 and n == 1)
                    if halves[-1] == DH - 1:
                        mm.then_inc(i_mm, 1)
                return stage

            def project_out(p, par):
                i = 2 * p + par
                pe.wait_ge(yv_lo, i + 1)
                pe.wait_ge(hlo, upto(2 * (i + 3), 2 * BATCH))
                pe.wait_ge(vT_lo, upto(4 * (i + 2), 4 * BATCH))
                for n in range(4):
                    wait(pe, z_done, 4 * i + n - 1)
                    for t in (2 * n, 2 * n + 1):
                        for h in range(DH):
                            mm = three_pass(pe, pE[n % 2][:, (t % 2) * D:(t % 2 + 1) * D],
                                            tuple(y[:, h, t * P:(t + 1) * P] for y in yp),
                                            tuple(w[:, h, :] for w in wo), h == 0, h == DH - 1)
                    mm.then_inc(out_mm, 1)

            def body(do):
                do(1, turn(0))
                do(0, forward(0, (0,)))
                do(1, turn(1))
                do(0, forward(0, (1,)))
                do(-1, project_out)
                do(1, project(0))
                do(0, forward(1))
                do(1, project(1))
                do(0, inverse(0))
                do(1, project(2))
                do(0, forward(2))
                do(1, project(3))
                do(0, inverse(1))
                do(0, forward(3))
                do(1, project(4))
                do(1, project(5))
                do(0, inverse(2))
                do(1, turn_vx((0, 1)))
                do(0, inverse(3, (0,)))
                do(1, turn_vx((2, 3)))
                do(0, inverse(3, (1,)))

            skewed(pe, BATCH, AHEAD, BEHIND, body)


def program(nc, t, out):
    def scratch(name, shape):
        return nc.dram_tensor(name, shape, F32, kind="Internal").ap()

    xs = [scratch(f"x_after_{n}", (TOKENS, D)) for n in range(3)]
    mid = scratch("x_mid", (TOKENS, D))
    mw = scratch("batch_weights", (CHUNKS, BATCH, P, D))
    with ExitStack() as ctx:
        consts = make_consts(nc, ctx, t["identity"])
        hyena(nc, t["u"], xs[0], consts, t["cos"], t["sin"],
              tuple(t[n] for n in ("pos", "times", "decay", "mlp_w1", "mlp_w2", "mlp_w3", "mlp_wo", "mlp_b", "freq",
                                   "filt_bias", "half_angle")),
              t["in_w"], t["in_b"], t["short_w"], t["short_b"], t["out_w"], t["out_b"])
        channel_mix(nc, xs[0], xs[1], consts, t["W_r"], t["W_k"], t["W_v"], t["mu_r"], t["mu_k"])
        linear_attention(nc, xs[1], mid, consts, t["wq"], t["wk"], t["wv"], t["wo"], t["ln1_g"], t["ln1_b"],
                         t["head_of_half"], t["causal"], t["same_head"])
        gelu_levels(nc, xs[1], mid, xs[2], consts, t["ln2_g"], t["ln2_b"], t["cms_w1"], t["cms_b1"], t["cms_w2"],
                    t["cms_b2"], t["cms_b2_last"])
        ph = Phase(nc, ctx, "shared")
        shared = ph.sb("mb1", [P, BATCH, FT]), ph.sb("mb2", [P, BATCH, D])
        expert_weights(nc, xs[2], consts, shared, mw, t["expert_rows"], t["base_rows"], t["gate_w1"], t["gate_b1"],
                       t["gate_w2"], t["gate_b2"], t["expert_select"], t["row_select"], t["row_spread"],
                       t["Tb1"], t["b1"], t["Tb2"], t["b2"])
        batch_mlp(nc, xs[2], out, consts, shared, mw)


def tables():
    f = np.float32

    def columns(v):
        return v.reshape(-1, P).T

    def rows(w):
        return w.reshape(w.shape[0] // P, P, -1).transpose(1, 0, 2).reshape(P, -1)

    time = np.linspace(0.0, 1.0, SEQ).astype(f)
    angle = (f(1e-4) * (f(TWO_PI) * np.linspace(0.0, SEQ - 1.0, SEQ).astype(f) / f(SEQ))).astype(f)
    deltas = np.linspace(np.log(0.01) / 1.5, np.log(0.01) / 0.3, D).astype(f)
    k = np.arange(HALF) + 0.5
    grid = TWO_PI / SEQ * np.outer(k, k)
    half = np.pi * k / SEQ
    head = np.arange(P) // HD
    got = {
        "identity": np.eye(P), "cos": rows(np.cos(grid)), "sin": rows(np.sin(grid)),
        "pos": np.stack([time, np.cos(angle), -np.sin(angle)]),
        "times": time.reshape(KT, P, 2).transpose(1, 0, 2).reshape(P, 2 * KT), "decay": -np.abs(deltas),
        "half_angle": np.concatenate([columns(g / HALF) for g in (np.cos(half), np.sin(half), -np.sin(half))], 1),
        "head_of_half": np.stack([head == o for o in range(HH)], 1), "causal": np.triu(np.ones((P, P))),
        "same_head": head[:, None] == head[None, :], "expert_select": np.repeat(np.eye(EXPERTS), GROUP, 1),
        "row_select": np.tile(np.eye(GROUP), (EXPERTS, 1)), "row_spread": np.concatenate([np.tile(np.eye(P)[:, g::SHARE], (1, BATCH)) for g in range(SHARE)], 1),
    }
    return {n: np.ascontiguousarray(a, dtype=f) for n, a in got.items()}


def kernel(**inputs):
    import concourse.bacc as bacc
    from concourse.bass_utils import run_bass_kernel_spmd

    def columns(v):
        return v.reshape(-1, P).T

    def rows(w):
        return w.reshape(w.shape[0] // P, P, -1).transpose(1, 0, 2).reshape(P, -1)

    def part(prefix):
        return lambda name: np.asarray(inputs[f"{prefix}_{name}"])

    a, c, l, g = part("L0_attn"), part("L0_ffn"), part("L1_attn"), part("L1_ffn")
    sw = a("short_w")

    def chunks(w1, w2):
        lead = w1.shape[:-2]
        w1 = np.swapaxes(w1, -1, -2).reshape(lead + (DH, P, HID // D, D))
        w1 = np.swapaxes(w1, -2, -3).reshape(lead + (CHUNKS // 2, P, D))
        return np.concatenate([w1, np.swapaxes(w2, -1, -2).reshape(lead + (FT, P, D))], -3)

    experts = chunks(g("TW1"), g("TW2")).reshape(EXPERTS, CHUNKS, GROUP, SHARE * D)
    given = {
        "u": a("u").reshape(TOKENS, D), "in_w": rows(a("in_w")), "in_b": columns(a("in_b")),
        "short_w": np.concatenate([columns(sw[:, j]) for j in range(3)], 1), "short_b": columns(a("short_b")),
        "mlp_w1": a("mlp_w1"), "mlp_w2": a("mlp_w2"), "mlp_w3": a("mlp_w3"), "mlp_wo": a("mlp_wo"),
        "mlp_b": np.stack([a("mlp_b1"), a("mlp_b2"), a("mlp_b3")], 1), "freq": a("freq").T,
        "filt_bias": a("filt_bias").reshape(1, D), "out_w": rows(a("out_w")), "out_b": a("out_b"),
        "W_r": rows(c("W_r").T), "W_k": rows(c("W_k").T), "W_v": rows(c("W_v").T),
        "mu_r": columns(c("mu_r")), "mu_k": columns(c("mu_k")),
        "wq": rows(l("wq")), "wk": rows(l("wk")), "wv": rows(l("wv")), "wo": rows(l("wo")),
        "ln1_g": columns(l("ln1_g")), "ln1_b": columns(l("ln1_b")),
        "ln2_g": columns(l("ln2_g")), "ln2_b": columns(l("ln2_b")),
        "cms_w1": np.stack([rows(w) for w in l("cms_w1")]), "cms_w2": np.stack([rows(w) for w in l("cms_w2")]),
        "cms_b1": columns(l("cms_b1")), "cms_b2": columns(l("cms_b2")), "cms_b2_last": l("cms_b2")[-1],
        "gate_w1": rows(g("gate_w1").T), "gate_b1": columns(g("gate_b1")), "gate_w2": rows(g("gate_w2").T),
        "gate_b2": g("gate_b2").reshape(EXPERTS, 1),
        "expert_rows": experts.transpose(1, 0, 2, 3).reshape(CHUNKS * P, SHARE * D),
        "base_rows": chunks(g("W1"), g("W2")).reshape(CHUNKS * P, D),
        "b1": columns(g("b1")), "b2": g("b2").reshape(1, D), "Tb1": g("Tb1"), "Tb2": g("Tb2"),
    }
    nc = bacc.Bacc("TRN2", target_bir_lowering=False, num_devices=1)
    arrays, views = {}, {}
    for name, value in {**given, **tables()}.items():
        arrays[f"{name}_dram"] = np.ascontiguousarray(value)
        views[name] = nc.dram_tensor(f"{name}_dram", value.shape, F32, kind="ExternalInput").ap()
    out = nc.dram_tensor("out_dram", (TOKENS, D), F32, kind="ExternalOutput").ap()
    program(nc, views, out)
    result = run_bass_kernel_spmd(nc, [arrays], core_ids=[0])
    return result.results[0]["out_dram"].reshape(BATCH, SEQ, D)
```
